# Optimizing a Trainium2 kernel written in Bass

```python
import numpy as np
import jax
import jax.numpy as jnp

def _softmax(x, axis=-1):
    return jax.nn.softmax(x, axis=axis)

def _gelu(x):
    return jax.nn.gelu(x, approximate=True)

def _silu(x):
    return jax.nn.silu(x)

def _sigmoid(x):
    return jax.nn.sigmoid(x)

def _layernorm(x, axis=-1, eps=1e-05):
    m = jnp.mean(x, axis=axis, keepdims=True)
    v = jnp.var(x, axis=axis, keepdims=True)
    return (x - m) / jnp.sqrt(v + eps)

def _scatter_add(tgt, idx, src, axis=0):
    return tgt.at[idx].add(src)

def _segment_sum(src, seg, n):
    return jax.ops.segment_sum(src, seg, n)
kernel_name = 'mk_decoder_preln_d2_seqx_r4_d0ef1d'

def setup_inputs(seed: int=0):
    np.random.seed(seed)
    _w = jnp.asarray

    def _rec_inputs():
        import jax
        import jax.numpy as jnp
        _rk = jax.random.key(seed)
        x = 7.22e-05 + 1 * jax.random.normal(jax.random.fold_in(_rk, 1), (16, 128, 256), jnp.float32)
        _lenS = 128 - jax.random.randint(jax.random.fold_in(_rk, 7), (16,), 0, max(1, 128 // 4) + 1, jnp.int32)
        _lenS2 = 128 - jax.random.randint(jax.random.fold_in(_rk, 8), (16,), 0, max(1, 128 // 4) + 1, jnp.int32)
        _ctx_1024P = jax.random.normal(jax.random.fold_in(_rk, 11), (16, 16, 256), jnp.float32)
        _ctx_1024c = jax.random.dirichlet(jax.random.fold_in(_rk, 511), 0.3 * jnp.ones((16,), jnp.float32), (16, 128))
        _ctx_1024t = jnp.einsum('bsk,bkd->bsd', _ctx_1024c, _ctx_1024P)
        _ctx_1024t = _ctx_1024t * jax.lax.rsqrt(jnp.mean(jnp.square(_ctx_1024t)) + 1e-12) * 0.953939
        ctx_1024 = 4.13588e-05 + 0.999923 * (_ctx_1024t + 0.3 * jax.random.normal(jax.random.fold_in(_rk, 611), (16, 128, 256), jnp.float32))
        return (x, ctx_1024)
    x, ctx_1024 = _rec_inputs()

    def _L0_attn_setup():
        import jax, jax.numpy as jnp
        import numpy as np
        NUM_HEADS = 32
        EPS = 1e-15
        key = jax.random.key(seed)
        k1, k2, k3, k4 = jax.random.split(key, 4)
        B, N, C = (8, 1024, 256)
        x = jax.random.normal(k1, (B, N, C), dtype=jnp.float32)
        qkv_weight = jax.random.normal(k2, (3 * C, C), dtype=jnp.float32) * C ** (-0.5)
        proj_weight = jax.random.normal(k3, (C, C), dtype=jnp.float32) * C ** (-0.5)
        proj_bias = jax.random.normal(k4, (C,), dtype=jnp.float32) * 0.01
        return {'x': x, 'qkv_weight': qkv_weight, 'proj_weight': proj_weight, 'proj_bias': proj_bias}
    _L0_attn_all = _L0_attn_setup()
    _L0_attn_in = {k: v for k, v in _L0_attn_all.items() if k in ('qkv_weight', 'proj_weight', 'proj_bias')}
    del _L0_attn_all

    def _L0_xattn_setup():
        import jax, jax.numpy as jnp
        import numpy as np
        D_MODEL = 256
        NHEAD = 16
        HEAD_DIM = D_MODEL // NHEAD
        key = jax.random.key(seed)
        ks = jax.random.split(key, 11)
        B, S, D = (4, 512, D_MODEL)
        scale = 1.0 / np.sqrt(D)
        inp = {'q': jax.random.normal(ks[0], (B, S, D), jnp.float32), 'k': jax.random.normal(ks[1], (B, S, D), jnp.float32), 'v': jax.random.normal(ks[2], (B, S, D), jnp.float32), 'Wq': jax.random.normal(ks[3], (D, D), jnp.float32) * scale, 'bq': jnp.zeros((D,), jnp.float32), 'Wk': jax.random.normal(ks[4], (D, D), jnp.float32) * scale, 'bk': jnp.zeros((D,), jnp.float32), 'Wv': jax.random.normal(ks[5], (D, D), jnp.float32) * scale, 'bv': jnp.zeros((D,), jnp.float32), 'Wo': jax.random.normal(ks[6], (D, D), jnp.float32) * scale, 'bo': jnp.zeros((D,), jnp.float32)}
        return inp
    _L0_xattn_all = _L0_xattn_setup()
    _L0_xattn_in = {k: v for k, v in _L0_xattn_all.items() if k in ('Wq', 'bq', 'Wk', 'bk', 'Wv', 'bv', 'Wo', 'bo')}
    del _L0_xattn_all

    def _L0_ffn_setup():
        import jax, jax.numpy as jnp
        import numpy as np
        N_EMBD = 256
        NUM_EXPERTS = 8
        TOP_K = 2

        def new_gelu(x):
            c = jnp.sqrt(2.0 / jnp.pi).astype(x.dtype)
            return 0.5 * x * (1.0 + jnp.tanh(c * (x + 0.044715 * x ** 3)))
        key = jax.random.key(seed)
        ks = jax.random.split(key, 6)
        C, E, H = (N_EMBD, NUM_EXPERTS, 4 * N_EMBD)
        x = jax.random.normal(ks[0], (4, 512, C), dtype=jnp.float32)
        router_w = 0.02 * jax.random.normal(ks[1], (E, C), dtype=jnp.float32)
        w1 = 0.02 * jax.random.normal(ks[2], (E, H, C), dtype=jnp.float32)
        b1 = jnp.zeros((E, H), dtype=jnp.float32)
        w2 = 0.02 * jax.random.normal(ks[3], (E, C, H), dtype=jnp.float32)
        b2 = jnp.zeros((E, C), dtype=jnp.float32)
        return {'x': x, 'router_w': router_w, 'w1': w1, 'b1': b1, 'w2': w2, 'b2': b2}
    _L0_ffn_all = _L0_ffn_setup()
    _L0_ffn_in = {k: v for k, v in _L0_ffn_all.items() if k in ('router_w', 'w1', 'b1', 'w2', 'b2')}
    del _L0_ffn_all

    def _L1_attn_setup():
        import jax, jax.numpy as jnp
        import numpy as np
        B, T, C = (4, 512, 256)
        H = 16
        D = C // H
        key = jax.random.key(seed)
        k1, k2, k3 = jax.random.split(key, 3)
        x = jax.random.normal(k1, (B, T, C), dtype=jnp.float32)
        w_attn = jax.random.normal(k2, (C, 3 * C), dtype=jnp.float32) * (1.0 / np.sqrt(C))
        b_attn = jnp.zeros((3 * C,), dtype=jnp.float32)
        w_proj = jax.random.normal(k3, (C, C), dtype=jnp.float32) * (1.0 / np.sqrt(C))
        b_proj = jnp.zeros((C,), dtype=jnp.float32)
        return {'x': x, 'w_attn': w_attn, 'b_attn': b_attn, 'w_proj': w_proj, 'b_proj': b_proj}
    _L1_attn_all = _L1_attn_setup()
    _L1_attn_in = {k: v for k, v in _L1_attn_all.items() if k in ('w_attn', 'b_attn', 'w_proj', 'b_proj')}
    del _L1_attn_all

    def _L1_xattn_setup():
        import jax, jax.numpy as jnp
        import numpy as np
        D_MODEL = 256
        NUM_HEADS = 16
        HEAD_DIM = D_MODEL // NUM_HEADS
        key = jax.random.key(seed)
        ks = jax.random.split(key, 11)
        B, S = (4, 1024)
        scale = 1.0 / np.sqrt(D_MODEL)
        inp = {'q': jax.random.normal(ks[0], (B, S, D_MODEL), jnp.float32), 'k': jax.random.normal(ks[1], (B, S, D_MODEL), jnp.float32), 'v': jax.random.normal(ks[2], (B, S, D_MODEL), jnp.float32), 'Wq': jax.random.normal(ks[3], (D_MODEL, D_MODEL), jnp.float32) * scale, 'bq': jax.random.normal(ks[4], (D_MODEL,), jnp.float32) * scale, 'Wk': jax.random.normal(ks[5], (D_MODEL, D_MODEL), jnp.float32) * scale, 'bk': jax.random.normal(ks[6], (D_MODEL,), jnp.float32) * scale, 'Wv': jax.random.normal(ks[7], (D_MODEL, D_MODEL), jnp.float32) * scale, 'bv': jax.random.normal(ks[8], (D_MODEL,), jnp.float32) * scale, 'Wo': jax.random.normal(ks[9], (D_MODEL, D_MODEL), jnp.float32) * scale, 'bo': jax.random.normal(ks[10], (D_MODEL,), jnp.float32) * scale}
        return inp
    _L1_xattn_all = _L1_xattn_setup()
    _L1_xattn_in = {k: v for k, v in _L1_xattn_all.items() if k in ('Wq', 'bq', 'Wk', 'bk', 'Wv', 'bv', 'Wo', 'bo')}
    del _L1_xattn_all

    def _L1_ffn_setup():
        import jax, jax.numpy as jnp
        import numpy as np
        B, S, H = (2, 512, 256)
        I = 128
        E_R, E_Z = (32, 8)
        E_T = E_R + E_Z
        K = 6
        SCALE = 2.5
        W_INIT = 0.02
        key = jax.random.key(seed)
        k0, k1, k2, k3 = jax.random.split(key, 4)
        return {'hidden_states': jax.random.normal(k0, (B, S, H), jnp.float32), 'classifier_weight': jax.random.normal(k1, (E_T, H), jnp.float32) * W_INIT, 'e_score_correction_bias': jnp.zeros((E_T,), jnp.float32), 'gate_up_proj': jax.random.normal(k2, (E_T, 2 * I, H), jnp.float32) * W_INIT, 'down_proj': jax.random.normal(k3, (E_R, H, I), jnp.float32) * W_INIT}
    _L1_ffn_all = _L1_ffn_setup()
    _L1_ffn_in = {k: v for k, v in _L1_ffn_all.items() if k in ('classifier_weight', 'e_score_correction_bias', 'gate_up_proj', 'down_proj')}
    del _L1_ffn_all
    return {'x': x, 'ctx_1024': ctx_1024, 'L0_attn_qkv_weight': _L0_attn_in['qkv_weight'], 'L0_attn_proj_weight': _L0_attn_in['proj_weight'], 'L0_attn_proj_bias': _L0_attn_in['proj_bias'], 'L0_xattn_Wq': _L0_xattn_in['Wq'], 'L0_xattn_bq': _L0_xattn_in['bq'], 'L0_xattn_Wk': _L0_xattn_in['Wk'], 'L0_xattn_bk': _L0_xattn_in['bk'], 'L0_xattn_Wv': _L0_xattn_in['Wv'], 'L0_xattn_bv': _L0_xattn_in['bv'], 'L0_xattn_Wo': _L0_xattn_in['Wo'], 'L0_xattn_bo': _L0_xattn_in['bo'], 'L0_ffn_router_w': _L0_ffn_in['router_w'], 'L0_ffn_w1': _L0_ffn_in['w1'], 'L0_ffn_b1': _L0_ffn_in['b1'], 'L0_ffn_w2': _L0_ffn_in['w2'], 'L0_ffn_b2': _L0_ffn_in['b2'], 'L1_attn_w_attn': _L1_attn_in['w_attn'], 'L1_attn_b_attn': _L1_attn_in['b_attn'], 'L1_attn_w_proj': _L1_attn_in['w_proj'], 'L1_attn_b_proj': _L1_attn_in['b_proj'], 'L1_xattn_Wq': _L1_xattn_in['Wq'], 'L1_xattn_bq': _L1_xattn_in['bq'], 'L1_xattn_Wk': _L1_xattn_in['Wk'], 'L1_xattn_bk': _L1_xattn_in['bk'], 'L1_xattn_Wv': _L1_xattn_in['Wv'], 'L1_xattn_bv': _L1_xattn_in['bv'], 'L1_xattn_Wo': _L1_xattn_in['Wo'], 'L1_xattn_bo': _L1_xattn_in['bo'], 'L1_ffn_classifier_weight': _L1_ffn_in['classifier_weight'], 'L1_ffn_e_score_correction_bias': _L1_ffn_in['e_score_correction_bias'], 'L1_ffn_gate_up_proj': _L1_ffn_in['gate_up_proj'], 'L1_ffn_down_proj': _L1_ffn_in['down_proj']}

def reference(x, ctx_1024, L0_attn_qkv_weight, L0_attn_proj_weight, L0_attn_proj_bias, L0_xattn_Wq, L0_xattn_bq, L0_xattn_Wk, L0_xattn_bk, L0_xattn_Wv, L0_xattn_bv, L0_xattn_Wo, L0_xattn_bo, L0_ffn_router_w, L0_ffn_w1, L0_ffn_b1, L0_ffn_w2, L0_ffn_b2, L1_attn_w_attn, L1_attn_b_attn, L1_attn_w_proj, L1_attn_b_proj, L1_xattn_Wq, L1_xattn_bq, L1_xattn_Wk, L1_xattn_bk, L1_xattn_Wv, L1_xattn_bv, L1_xattn_Wo, L1_xattn_bo, L1_ffn_classifier_weight, L1_ffn_e_score_correction_bias, L1_ffn_gate_up_proj, L1_ffn_down_proj):
    import jax
    import jax.numpy as jnp

    def _L0_attn_ref(x, qkv_weight, proj_weight, proj_bias):
        import jax, jax.numpy as jnp
        import numpy as np
        NUM_HEADS = 32
        EPS = 1e-15
        B, N, C = x.shape
        H = NUM_HEADS
        D = C // H
        qkv = jax.nn.relu(jnp.einsum('bnc,oc->bno', x, qkv_weight))
        qkv = qkv.reshape(B, N, 3, H, D)
        q, k, v = (qkv[:, :, 0], qkv[:, :, 1], qkv[:, :, 2])
        v_pad = jnp.concatenate([v, jnp.ones((B, N, H, 1), dtype=v.dtype)], axis=-1)
        vk = jnp.einsum('bnhe,bnhd->bhed', v_pad.astype(jnp.float32), k.astype(jnp.float32))
        vk_q = jnp.einsum('bhed,bnhd->bnhe', vk, q.astype(jnp.float32))
        proj_input = (vk_q[..., :D] / (vk_q[..., D:] + EPS)).astype(qkv.dtype)
        proj_input = proj_input.reshape(B, N, C)
        y = jnp.einsum('bnc,oc->bno', proj_input, proj_weight) + proj_bias
        return y

    def _L0_xattn_ref(q, k, v, Wq, bq, Wk, bk, Wv, bv, Wo, bo):
        import jax, jax.numpy as jnp
        import numpy as np
        D_MODEL = 256
        NHEAD = 16
        HEAD_DIM = D_MODEL // NHEAD
        B, S, D = q.shape
        H, Hd = (NHEAD, HEAD_DIM)
        qh = (q @ Wq.T + bq).reshape(B, S, H, Hd).transpose(0, 2, 1, 3)
        kh = (k @ Wk.T + bk).reshape(B, S, H, Hd).transpose(0, 2, 1, 3)
        vh = (v @ Wv.T + bv).reshape(B, S, H, Hd).transpose(0, 2, 1, 3)
        scores = jnp.einsum('bhqd,bhkd->bhqk', qh, kh) / jnp.sqrt(jnp.float32(Hd))
        attn = jax.nn.softmax(scores, axis=-1)
        out = jnp.einsum('bhqk,bhkd->bhqd', attn, vh)
        out = out.transpose(0, 2, 1, 3).reshape(B, S, D)
        return out @ Wo.T + bo

    def _L0_ffn_ref(x, router_w, w1, b1, w2, b2):
        import jax, jax.numpy as jnp
        import numpy as np
        N_EMBD = 256
        NUM_EXPERTS = 8
        TOP_K = 2

        def new_gelu(x):
            c = jnp.sqrt(2.0 / jnp.pi).astype(x.dtype)
            return 0.5 * x * (1.0 + jnp.tanh(c * (x + 0.044715 * x ** 3)))
        B, T, C = x.shape
        E = router_w.shape[0]
        x_flat = x.reshape(B * T, C)
        router_logits = x_flat @ router_w.T
        router_probs = jax.nn.softmax(router_logits, axis=-1)
        top_k_probs, top_k_idx = jax.lax.top_k(router_probs, TOP_K)
        top_k_probs = top_k_probs / (top_k_probs.sum(axis=-1, keepdims=True) + 1e-08)
        cw = (jax.nn.one_hot(top_k_idx, E, dtype=x.dtype) * top_k_probs[..., None]).sum(axis=1)
        output = jnp.zeros_like(x_flat)
        for e in range(E):
            h = new_gelu(x_flat @ w1[e].T + b1[e])
            out_e = h @ w2[e].T + b2[e]
            output = output + cw[:, e:e + 1] * out_e
        return output.reshape(B, T, C)

    def _L1_attn_ref(x, w_attn, b_attn, w_proj, b_proj):
        import jax, jax.numpy as jnp
        import numpy as np
        B, T, C = (4, 512, 256)
        H = 16
        D = C // H
        Bx, Tx, Cx = x.shape
        qkv = x @ w_attn + b_attn
        q, k, v = jnp.split(qkv, 3, axis=-1)
        q = q.reshape(Bx, Tx, H, D).transpose(0, 2, 1, 3)
        k = k.reshape(Bx, Tx, H, D).transpose(0, 2, 1, 3)
        v = v.reshape(Bx, Tx, H, D).transpose(0, 2, 1, 3)
        scores = jnp.einsum('bhqd,bhkd->bhqk', q, k) / jnp.sqrt(jnp.float32(D))
        causal = jnp.tril(jnp.ones((Tx, Tx), dtype=bool))
        scores = jnp.where(causal[None, None, :, :], scores, -jnp.inf)
        attn = jax.nn.softmax(scores, axis=-1)
        y = jnp.einsum('bhqk,bhkd->bhqd', attn, v)
        y = y.transpose(0, 2, 1, 3).reshape(Bx, Tx, Cx)
        return y @ w_proj + b_proj

    def _L1_xattn_ref(q, k, v, Wq, bq, Wk, bk, Wv, bv, Wo, bo):
        import jax, jax.numpy as jnp
        import numpy as np
        D_MODEL = 256
        NUM_HEADS = 16
        HEAD_DIM = D_MODEL // NUM_HEADS
        b, s, _ = q.shape
        Q = (q @ Wq + bq).reshape(b, s, NUM_HEADS, HEAD_DIM)
        K = (k @ Wk + bk).reshape(b, s, NUM_HEADS, HEAD_DIM)
        V = (v @ Wv + bv).reshape(b, s, NUM_HEADS, HEAD_DIM)
        score = jnp.einsum('bsid,bsjd->bsij', Q, K) / np.sqrt(HEAD_DIM)
        w = jax.nn.softmax(score, axis=-1)
        attn = jnp.einsum('bsij,bsjd->bsid', w, V).reshape(b, s, D_MODEL)
        return attn @ Wo + bo

    def _L1_ffn_ref(hidden_states, classifier_weight, e_score_correction_bias, gate_up_proj, down_proj):
        import jax, jax.numpy as jnp
        import numpy as np
        B, S, H = (2, 512, 256)
        I = 128
        E_R, E_Z = (32, 8)
        E_T = E_R + E_Z
        K = 6
        SCALE = 2.5
        W_INIT = 0.02
        orig_shape = hidden_states.shape
        x = hidden_states.reshape(-1, H).astype(jnp.float32)
        T = x.shape[0]
        logits = x @ classifier_weight.T
        scores = jax.nn.softmax(logits, axis=-1)
        _, topk_idx = jax.lax.top_k(scores + e_score_correction_bias[None, :], K)
        topk_w = jnp.take_along_axis(scores, topk_idx, axis=1) * SCALE
        w_full = jnp.zeros((T, E_T), jnp.float32).at[jnp.arange(T)[:, None], topk_idx].add(topk_w)
        zero_w = w_full[:, E_R:].sum(axis=-1, keepdims=True)
        out0 = x * zero_w
        routed_w = w_full[:, :E_R].T

        def body(out, xs):
            Wgu, Wd, we = xs
            gate, up = jnp.split(x @ Wgu.T, 2, axis=-1)
            y = jax.nn.silu(gate) * up @ Wd.T
            return (out + we[:, None] * y, None)
        out, _ = jax.lax.scan(body, out0, (gate_up_proj[:E_R], down_proj, routed_w))
        return out.reshape(orig_shape).astype(hidden_states.dtype)
    x = x + _L0_attn_ref(_layernorm(x, axis=-1), L0_attn_qkv_weight, L0_attn_proj_weight, L0_attn_proj_bias)
    x = x + _L0_xattn_ref(_layernorm(x, axis=-1), ctx_1024, ctx_1024, L0_xattn_Wq, L0_xattn_bq, L0_xattn_Wk, L0_xattn_bk, L0_xattn_Wv, L0_xattn_bv, L0_xattn_Wo, L0_xattn_bo)
    x = x + _L0_ffn_ref(_layernorm(x, axis=-1), L0_ffn_router_w, L0_ffn_w1, L0_ffn_b1, L0_ffn_w2, L0_ffn_b2)
    x = x + _L1_attn_ref(_layernorm(x, axis=-1), L1_attn_w_attn, L1_attn_b_attn, L1_attn_w_proj, L1_attn_b_proj)
    x = x + _L1_xattn_ref(_layernorm(x, axis=-1), ctx_1024, ctx_1024, L1_xattn_Wq, L1_xattn_bq, L1_xattn_Wk, L1_xattn_bk, L1_xattn_Wv, L1_xattn_bv, L1_xattn_Wo, L1_xattn_bo)
    x = x + _L1_ffn_ref(_layernorm(x, axis=-1), L1_ffn_classifier_weight, L1_ffn_e_score_correction_bias, L1_ffn_gate_up_proj, L1_ffn_down_proj)
    return x

_drawn_inputs = setup_inputs


def setup_inputs(seed=0):
    import zlib

    import numpy as np

    out = dict(_drawn_inputs(seed))
    spreads = {'L0_xattn_bq': (0.0, 0.329),
     'L0_xattn_bk': (0.0, 0.8),
     'L0_xattn_bv': (0.0, 0.1),
     'L0_xattn_bo': (0.0, 0.1),
     'L0_ffn_b1': (0.0, 0.368),
     'L0_ffn_b2': (0.0, 0.1),
     'L1_attn_b_attn': (0.0, 0.1),
     'L1_attn_b_proj': (0.0, 0.1),
     'L1_ffn_e_score_correction_bias': (0.0, 0.1)}
    factors = {'L0_attn_proj_bias': 5.105,
     'L1_xattn_bq': 3.947,
     'L1_xattn_bk': 3.93,
     'L1_xattn_bv': 3.343,
     'L1_ffn_gate_up_proj': 8.0,
     'L1_ffn_down_proj': 8.0}
    for name, (base, spread) in spreads.items():
        noise = np.random.default_rng([zlib.crc32(name.encode()), seed]).standard_normal(out[name].shape)
        drawn = base * np.exp(spread * noise) if base else spread * noise
        out[name] = jnp.asarray(drawn.astype(out[name].dtype))
    for name, factor in factors.items():
        out[name] = (out[name] * factor).astype(out[name].dtype)
    return out
```

```python
from contextlib import ExitStack

import concourse.bass as bass
from concourse import mybir

P = 128
NT = 16
TG = 4
NG = NT // TG
GT = TG * P
C = 256
KC = C // P
LN_EPS = 1e-5
LIN_EPS = 1e-15
FAR = 3.0e38

F32 = mybir.dt.float32
BF16 = mybir.dt.bfloat16
ALU = mybir.AluOpType
ACT = mybir.ActivationFunctionType
AX = mybir.AxisListType


def named_semaphores(ctx, nc, prefix, names):
    sems = {n: nc.alloc_semaphore(f"{prefix}_{n}") for n in names.split()}

    def give_back():
        nc.clear_and_free_semaphores(list(sems.values()))
        nc.all_engine_barrier()

    ctx.callback(give_back)
    return sems


def drained(uses, n):
    return sum(u == uses[n] for u in uses[:n + 1])


def total(uses, who):
    return sum(u == who for u in uses)


def tile_of(buf, i, t):
    return buf[:, bass.ds(i * TG + t, 1), :].rearrange("p a c -> p (a c)")



NORM_SEMS = "stats moments eps rstd normed biased"


def norm_buffers(sb, pre):
    return dict(st=sb(f"{pre}_st", [P, TG, 6]), mv=sb(f"{pre}_mv", [P, TG, 2]), ve=sb(f"{pre}_ve", [P, TG]),
                rs=sb(f"{pre}_rs", [P, TG]), xn=sb(f"{pre}_xn", [P, TG, C]), junk=sb(f"{pre}_junk", [P, 1]))


def norm_vector(dve, S, B, xs, i):
    for t in range(TG):
        dve.bn_stats(B["st"][:, t, :], tile_of(xs, i, t)).then_inc(S["stats"], 1)
    dve.wait_ge(S["stats"], i * TG + TG)
    dve.memset(B["junk"][:], 0.0)
    for t in range(TG):
        dve.bn_aggr(B["mv"][:, t, :], B["st"][:, t, :]).then_inc(S["moments"], 1)
    dve.wait_ge(S["rstd"], i + 1)
    for t in range(TG):
        dve.tensor_scalar(B["xn"][:, t, :], tile_of(xs, i, t), B["mv"][:, t, 0:1], B["rs"][:, t:t + 1],
                          ALU.subtract, ALU.mult).then_inc(S["normed"], 1)


def norm_pool(pool, S, B, K, i):
    pool.wait_ge(S["moments"], i * TG + TG)
    pool.tensor_tensor(B["ve"][:], B["mv"][:, :, 1], K["eps4"][:], ALU.add).then_inc(S["eps"], 1)
    pool.wait_ge(S["eps"], i + 1)
    pool.tensor_tensor(B["rs"][:], B["ve"][:], K["half4"][:], ALU.pow).then_inc(S["rstd"], 1)


def bias_pool(pool, S, xs, bias, i):
    for t in range(TG):
        pool.wait_ge(S["normed"], i * TG + t + 1)
        pool.tensor_tensor(tile_of(xs, i, t), tile_of(xs, i, t), bias[:], ALU.add).then_inc(S["biased"], 1)



def linear_attention(nc, K, xs, W):
    with ExitStack() as ctx:
        def sb(n, s, d=F32):
            return ctx.enter_context(nc.sbuf_tensor("la_" + n, s, d))

        def pb(n, s, d=F32):
            return ctx.enter_context(nc.psum_tensor("la_" + n, s, d))

        B = norm_buffers(sb, "n")
        xnT = sb("xnT", [P, KC, GT])
        qT = sb("qT", [P, KC, GT])
        k = sb("k", [P, TG, C])
        v1 = sb("v1", [P, TG, KC, P + 1])
        nd = sb("nd", [P, 2, KC, 2, P])
        den = sb("den", [P, 2, KC, P])
        rden = sb("rden", [P, 2, KC, P])
        y = sb("y", [P, 2, C])
        yT = sb("yT", [P, 2, KC, P])
        mx = [pb(f"mx{b}", [P, 512]) for b in range(2)]
        vk = [pb(f"vk{b}", [P, KC, 256]) for b in range(2)]
        pn = [pb(f"pn{b}", [P, KC, 2, P]) for b in range(2)]
        py = pb("py", [P, 512])
        po = pb("po", [P, 512])
        S = named_semaphores(ctx, nc, "la", NORM_SEMS + " ones full emptied vk masked nd den_eps den_inv y_ready turned yT out added")
        USES = 4 + 2 + 4
        block = ctx.enter_context(nc.Block())

        @block.gpsimd
        def _(pool):
            pool.memset(v1[:, :, :, P:P + 1], 1.0).then_inc(S["ones"], 1)
            pool.wait_ge(K["s"]["x"], 16 * NG)
            pool.wait_ge(K["s"]["weights"], 16 * K["n_weights"])
            with pool.Fori(0, NG) as i:
                norm_pool(pool, S, B, K, i)
                bias_pool(pool, S, xs, W["bp"], i)

        @block.vector
        def _(dve):
            dve.wait_ge(K["s"]["x"], 16 * NG)
            with dve.Fori(0, NG) as i:
                norm_vector(dve, S, B, xs, i)
                for s in range(TG + 3):
                    if s < TG:
                        t = s
                        dve.wait_ge(S["vk"], i * TG + t + 1)
                        dve.tensor_tensor(nd[:, t % 2, :, 0, :], vk[t % 2][:, :, 0:P],
                                          K["heads8"][:].unsqueeze(1).to_broadcast([P, KC, P]), ALU.mult)
                        for c in range(KC):
                            op = dve.tensor_scalar(nd[:, t % 2, c, 1, :], K["heads8"][:], vk[t % 2][:, c, P:P + 1],
                                                   None, ALU.mult)
                        op.then_inc(S["masked"], 1)
                    if 0 <= s - 1 < TG:
                        t = s - 1
                        dve.wait_ge(S["nd"], i * TG + t + 1)
                        dve.tensor_scalar(den[:, t % 2], pn[t % 2][:, :, 1, :], LIN_EPS, None,
                                          ALU.add).then_inc(S["den_eps"], 1)
                        dve.wait_ge(S["den_eps"], i * TG + t + 1)
                        dve.reciprocal(rden[:, t % 2], den[:, t % 2]).then_inc(S["den_inv"], 1)
                        dve.wait_ge(S["den_inv"], i * TG + t + 1)
                        dve.tensor_tensor(y[:, t % 2, :].rearrange("p (a b) -> p a b", a=KC), pn[t % 2][:, :, 0, :],
                                          rden[:, t % 2], ALU.mult).then_inc(S["y_ready"], 1)
                    if 0 <= s - 3 < TG:
                        t = s - 3
                        dve.wait_ge(S["out"], i * TG + t + 1)
                        dve.wait_ge(S["biased"], i * TG + t + 1)
                        dve.tensor_tensor(tile_of(xs, i, t), tile_of(xs, i, t), po[:, 0:C], ALU.add).then_inc(S["added"], 1)

        @block.scalar
        def _(act):
            act.wait_ge(S["ones"], 1)
            with act.Fori(0, NG) as i:
                for t in range(TG):
                    act.wait_ge(S["full"], i * USES + t + 1)
                    act.activation(xnT[:, :, t * P:(t + 1) * P], mx[t % 2][:, 0:C].rearrange("p (a b) -> p a b", a=KC),
                                   ACT.Copy).then_inc(S["emptied"], 1)
                for c in range(KC):
                    act.wait_ge(S["full"], i * USES + 4 + c + 1)
                    act.activation(qT[:, c, :], mx[c % 2][:], ACT.Relu).then_inc(S["emptied"], 1)
                for t in range(TG):
                    act.wait_ge(S["full"], i * USES + 6 + t + 1)
                    act.activation(k[:, t, :], mx[t % 2][:, 0:C], ACT.Relu)
                    act.activation(v1[:, t, :, 0:P], mx[t % 2][:, C:2 * C].rearrange("p (a b) -> p a b", a=KC),
                                   ACT.Relu).then_inc(S["emptied"], 1)
                for t in range(TG):
                    act.wait_ge(S["turned"], i * TG + t + 1)
                    act.activation(yT[:, t % 2], py[:, 0:C].rearrange("p (a b) -> p a b", a=KC),
                                   ACT.Copy).then_inc(S["yT"], 1)

        @block.tensor
        def _(pe):
            pe.wait_ge(K["s"]["weights"], 16 * K["n_weights"])
            pe.wait_ge(K["s"]["consts"], K["n_consts"])
            pe.wait_ge(S["ones"], 1)
            with pe.Fori(0, NG) as i:
                for t in range(TG):
                    pe.wait_ge(S["normed"], i * TG + t + 1)
                    if t >= 2:
                        pe.wait_ge(S["emptied"], i * USES + t - 1)
                    for c in range(KC):
                        op = pe.transpose(mx[t % 2][:, c * P:(c + 1) * P], B["xn"][:, t, c * P:(c + 1) * P], K["ident"][:])
                    op.then_inc(S["full"], 1)
                for c in range(KC):
                    pe.wait_ge(S["emptied"], i * USES + 4)
                    if c:
                        pe.wait_ge(S["emptied"], i * USES + 4)
                    for kc in range(KC):
                        op = pe.matmul(mx[c % 2][:], W["qkv"][:, kc, c * P:(c + 1) * P], xnT[:, kc, :],
                                       start=(kc == 0), stop=(kc == KC - 1))
                    op.then_inc(S["full"], 1)
                for t in range(TG):
                    pe.wait_ge(S["emptied"], i * USES + 5 + t)
                    for kc in range(KC):
                        op = pe.matmul(mx[t % 2][:], xnT[:, kc, t * P:(t + 1) * P], W["qkv"][:, kc, C:3 * C],
                                       start=(kc == 0), stop=(kc == KC - 1))
                    op.then_inc(S["full"], 1)
                for s in range(TG + 3):
                    if s < TG:
                        t = s
                        pe.wait_ge(S["emptied"], i * USES + 7 + t)
                        if t >= 2:
                            pe.wait_ge(S["masked"], i * TG + t - 1)
                        for c in range(KC):
                            op = pe.matmul(vk[t % 2][:, c, 0:P + 1], k[:, t, c * P:(c + 1) * P], v1[:, t, c, :],
                                           start=True, stop=True)
                        op.then_inc(S["vk"], 1)
                    if 0 <= s - 1 < TG:
                        t = s - 1
                        pe.wait_ge(S["masked"], i * TG + t + 1)
                        if t >= 2:
                            pe.wait_ge(S["y_ready"], i * TG + t - 1)
                        for c in range(KC):
                            op = pe.matmul(pn[t % 2][:, c], qT[:, c, t * P:(t + 1) * P],
                                           nd[:, t % 2, c].rearrange("p a b -> p (a b)"), start=True, stop=True)
                        op.then_inc(S["nd"], 1)
                    if 0 <= s - 2 < TG:
                        t = s - 2
                        pe.wait_ge(S["y_ready"], i * TG + t + 1)
                        if t >= 1:
                            pe.wait_ge(S["yT"], i * TG + t)
                        for c in range(KC):
                            op = pe.transpose(py[:, c * P:(c + 1) * P], y[:, t % 2, c * P:(c + 1) * P], K["ident"][:])
                        op.then_inc(S["turned"], 1)
                    if 0 <= s - 3 < TG:
                        t = s - 3
                        pe.wait_ge(S["yT"], i * TG + t + 1)
                        if t >= 1:
                            pe.wait_ge(S["added"], i * TG + t)
                        for kc in range(KC):
                            op = pe.matmul(po[:, 0:C], yT[:, t % 2, kc, :], W["wp"][:, kc, :],
                                           start=(kc == 0), stop=(kc == KC - 1))
                        op.then_inc(S["out"], 1)



def softmax_attention(nc, K, xs, W, pre, ctx_dram=None, causal=False):
    NH, HD = 16, 16
    NB = 4
    UN = TG * NB
    with ExitStack() as ctx:
        def sb(n, s, d=F32):
            return ctx.enter_context(nc.sbuf_tensor(f"{pre}_{n}", s, d))

        def pb(n, s, d=F32):
            return ctx.enter_context(nc.psum_tensor(f"{pre}_{n}", s, d))

        B = norm_buffers(sb, "n")
        xnT = sb("xnT", [P, KC, GT])
        cT = sb("cT", [P, KC, GT]) if ctx_dram is not None else xnT
        qT = sb("qT", [P, KC, GT])
        kk = sb("kk", [P, KC, TG, 2, P])
        v1 = sb("v1", [P, TG, NH, HD + 1])
        p = sb("p", [P, 2, 4, P])
        pT = sb("pT", [P, 2, 4, P])
        nm = sb("nm", [P, 2, 4])
        rz = sb("rz", [P, 2, NH])
        y = sb("y", [P, 2, C])
        yT = sb("yT", [P, 2, KC, P])
        mx = [pb(f"mx{b}", [P, 512]) for b in range(2)]
        sc = [pb(f"sc{b}", [P, 4, P]) for b in range(2)]
        tp = [pb(f"tp{b}", [P, 4, P]) for b in range(2)]
        po = [pb(f"po{b}", [P, NH, HD + 1]) for b in range(2)]
        S = named_semaphores(ctx, nc, pre, NORM_SEMS + " ones ctx_in full by_act by_dve scored maxed shifted exped pt_full pt"
                  " pv zinv y_ready")
        USES = ["act"] * 4 + ["act"] * 2 + ["dve"] * 2 + ["dve"] * 4 + ["act", "dve"] * 4
        NU, NA, ND = len(USES), total(USES, "act"), total(USES, "dve")
        Q0, K0, V0, Y0 = 4, 6, 8, 12
        block = ctx.enter_context(nc.Block())

        def wait_emptied(eng, i, n):
            if USES[n] == "act":
                eng.wait_ge(S["by_act"], i * NA + drained(USES, n))
            else:
                eng.wait_ge(S["by_dve"], i * ND + drained(USES, n))

        def heads(u):
            b = u % NB
            return [2 * b, 2 * b + 1, 8 + 2 * b, 9 + 2 * b]

        if ctx_dram is not None:
            @block.sync
            def _(sp):
                sp.dma_start(cT[:], ctx_dram[:, :, 0:GT].rearrange("k p t -> p k t")).then_inc(S["ctx_in"], 16)
                with sp.Fori(1, NG) as i:
                    sp.wait_ge(S["full"], (i - 1) * NU + Y0)
                    sp.dma_start(cT[:], ctx_dram[:, :, bass.ds(i * GT, GT)].rearrange("k p t -> p k t")).then_inc(S["ctx_in"], 16)

        @block.gpsimd
        def _(pool):
            pool.memset(v1[:, :, :, HD:HD + 1], 1.0).then_inc(S["ones"], 1)
            with pool.Fori(0, NG) as i:
                norm_pool(pool, S, B, K, i)
                bias_pool(pool, S, xs, W["bo"], i)

        def resid(dve, i, t):
            n = Y0 + 2 * t + 1
            dve.wait_ge(S["full"], i * NU + n + 1)
            dve.wait_ge(S["biased"], i * TG + t + 1)
            dve.tensor_tensor(tile_of(xs, i, t), tile_of(xs, i, t), mx[n % 2][:, 0:C], ALU.add).then_inc(S["by_dve"], 1)

        @block.vector
        def _(dve):
            dve.wait_ge(S["ones"], 1)
            dve.wait_ge(K["s"]["weights"], 16 * K["n_weights"])
            with dve.Fori(0, NG) as i:
                norm_vector(dve, S, B, xs, i)
                for c in range(KC):
                    dve.wait_ge(S["full"], i * NU + K0 + c + 1)
                    for par in range(2):
                        op = dve.tensor_scalar(kk[:, c, :, par, :], mx[(K0 + c) % 2][:].rearrange("p (t n) -> p t n", t=TG),
                                               W["bk"][:, c:c + 1], K["evenodd"][:, par:par + 1], ALU.add, ALU.mult)
                    op.then_inc(S["by_dve"], 1)
                for t in range(TG):
                    dve.wait_ge(S["full"], i * NU + V0 + t + 1)
                    dve.tensor_tensor(v1[:, t, :, 0:HD], mx[(V0 + t) % 2][:, 0:C].rearrange("p (h d) -> p h d", h=NH),
                                      W["bv"][:].rearrange("p (h d) -> p h d", h=NH), ALU.add).then_inc(S["by_dve"], 1)
                for s in range(UN + 7):
                    if s < UN:
                        u = s
                        dve.wait_ge(S["scored"], i * UN + u + 1)
                        dve.tensor_reduce(nm[:, u % 2, :], sc[u % 2][:], AX.X, ALU.max, negate=True).then_inc(S["maxed"], 1)
                        dve.wait_ge(S["maxed"], i * UN + u + 1)
                        if u >= 2:
                            dve.wait_ge(S["pt_full"], i * UN + u - 1)
                        dve.tensor_tensor(p[:, u % 2], sc[u % 2][:], nm[:, u % 2, :].unsqueeze(2).to_broadcast([P, 4, P]),
                                          ALU.add).then_inc(S["shifted"], 1)
                    if s >= 7 and (s - 7) % 4 == 0:
                        t = (s - 7) // 4
                        dve.wait_ge(S["pv"], i * UN + 4 * t + 4)
                        dve.reciprocal(rz[:, t % 2, :], po[t % 2][:, :, HD]).then_inc(S["zinv"], 1)
                        dve.wait_ge(S["zinv"], i * TG + t + 1)
                        dve.tensor_tensor(y[:, t % 2, :].rearrange("p (h d) -> p h d", h=NH), po[t % 2][:, :, 0:HD],
                                          rz[:, t % 2, :].unsqueeze(2).to_broadcast([P, NH, HD]), ALU.mult).then_inc(S["y_ready"], 1)
                    if s >= 9 and (s - 9) % 4 == 0:
                        t = (s - 9) // 4
                        resid(dve, i, t)

        @block.scalar
        def _(act):
            act.wait_ge(K["s"]["weights"], 16 * K["n_weights"])
            with act.Fori(0, NG) as i:
                for t in range(TG):
                    act.wait_ge(S["full"], i * NU + t + 1)
                    act.activation(xnT[:, :, t * P:(t + 1) * P], mx[t % 2][:, 0:C].rearrange("p (a b) -> p a b", a=KC),
                                   ACT.Copy).then_inc(S["by_act"], 1)
                for c in range(KC):
                    act.wait_ge(S["full"], i * NU + Q0 + c + 1)
                    act.activation(qT[:, c, :], mx[(Q0 + c) % 2][:], ACT.Identity, bias=W["bq"][:, c:c + 1]).then_inc(S["by_act"], 1)

                def y_turn(t):
                    n = Y0 + 2 * t
                    act.wait_ge(S["full"], i * NU + n + 1)
                    act.activation(yT[:, t % 2], mx[n % 2][:, 0:C].rearrange("p (a b) -> p a b", a=KC),
                                   ACT.Copy).then_inc(S["by_act"], 1)

                for s in range(UN + 7):
                    if s < UN:
                        u = s
                        act.wait_ge(S["shifted"], i * UN + u + 1)
                        act.activation(p[:, u % 2], p[:, u % 2], ACT.Exp, scale=HD ** -0.5).then_inc(S["exped"], 1)
                    if 0 <= s - 2 < UN:
                        u = s - 2
                        act.wait_ge(S["pt_full"], i * UN + u + 1)
                        if u >= 2:
                            act.wait_ge(S["pv"], i * UN + u - 1)
                        act.activation(pT[:, u % 2], tp[u % 2][:], ACT.Copy).then_inc(S["pt"], 1)
                    if s >= 8 and (s - 8) % 4 == 0:
                        y_turn((s - 8) // 4)

        @block.tensor
        def _(pe):
            pe.wait_ge(K["s"]["weights"], 16 * K["n_weights"])
            pe.wait_ge(K["s"]["consts"], K["n_consts"])
            pe.wait_ge(S["ones"], 1)
            with pe.Fori(0, NG) as i:
                for t in range(TG):
                    pe.wait_ge(S["normed"], i * TG + t + 1)
                    if t >= 2:
                        wait_emptied(pe, i, t - 2)
                    for c in range(KC):
                        op = pe.transpose(mx[t % 2][:, c * P:(c + 1) * P], B["xn"][:, t, c * P:(c + 1) * P], K["ident"][:])
                    op.then_inc(S["full"], 1)
                wait_emptied(pe, i, 3)
                if ctx_dram is not None:
                    pe.wait_ge(S["ctx_in"], i * 16 + 16)
                for what, src, n0 in (("wq", xnT, Q0), ("wk", cT, K0)):
                    for c in range(KC):
                        n = n0 + c
                        wait_emptied(pe, i, n - 2)
                        for kc in range(KC):
                            op = pe.matmul(mx[n % 2][:], W[what][:, kc, c * P:(c + 1) * P], src[:, kc, :],
                                           start=(kc == 0), stop=(kc == KC - 1))
                        op.then_inc(S["full"], 1)
                for t in range(TG):
                    n = V0 + t
                    wait_emptied(pe, i, n - 2)
                    for kc in range(KC):
                        op = pe.matmul(mx[n % 2][:, 0:C], cT[:, kc, t * P:(t + 1) * P], W["wv"][:, kc, :],
                                       start=(kc == 0), stop=(kc == KC - 1))
                    op.then_inc(S["full"], 1)

                def turn_y(t):
                    n = Y0 + 2 * t
                    pe.wait_ge(S["y_ready"], i * TG + t + 1)
                    wait_emptied(pe, i, n - 2)
                    for c in range(KC):
                        op = pe.transpose(mx[n % 2][:, c * P:(c + 1) * P], y[:, t % 2, c * P:(c + 1) * P], K["ident"][:])
                    op.then_inc(S["full"], 1)

                def project(t):
                    n = Y0 + 2 * t + 1
                    wait_emptied(pe, i, n - 1)
                    wait_emptied(pe, i, n - 2)
                    for kc in range(KC):
                        op = pe.matmul(mx[n % 2][:, 0:C], yT[:, t % 2, kc, :], W["wo"][:, kc, :],
                                       start=(kc == 0), stop=(kc == KC - 1))
                    op.then_inc(S["full"], 1)

                for s in range(UN + 7):
                    if s < UN:
                        u, t, b = s, s // NB, s % NB
                        if u == 0:
                            wait_emptied(pe, i, V0 + 3)
                        if u >= 2:
                            pe.wait_ge(S["shifted"], i * UN + u - 1)
                        if causal:
                            pe.matmul(sc[u % 2][:], K["identb"][:], K["causal"][:], start=True, stop=True)
                        for c in range(KC):
                            r = slice(32 * b, 32 * b + 32)
                            op = pe.matmul(sc[u % 2][:, 2 * c:2 * c + 2, :], qT[r, c, t * P:(t + 1) * P],
                                           kk[r, c, t, :, :], start=not causal, stop=True,
                                           tile_position=(32 * b, 0), skip_group_check=causal)
                        op.then_inc(S["scored"], 1)
                    if 0 <= s - 2 < UN:
                        u = s - 2
                        pe.wait_ge(S["exped"], i * UN + u + 1)
                        if u >= 2:
                            pe.wait_ge(S["pt"], i * UN + u - 1)
                        for j in range(4):
                            op = pe.transpose(tp[u % 2][:, j, :], p[:, u % 2, j, :], K["ident"][:])
                        op.then_inc(S["pt_full"], 1)
                    if 0 <= s - 3 < UN:
                        u = s - 3
                        t = u // NB
                        pe.wait_ge(S["pt"], i * UN + u + 1)
                        if u % NB == 0 and t >= 2:
                            pe.wait_ge(S["y_ready"], i * TG + t - 1)
                        for j, h in enumerate(heads(u)):
                            op = pe.matmul(po[t % 2][:, h, :], pT[:, u % 2, j, :], v1[:, t, h, :], start=True, stop=True)
                        op.then_inc(S["pv"], 1)
                    if s >= 8 and (s - 8) % 4 == 0:
                        turn_y((s - 8) // 4)
                    if s >= 9 and (s - 9) % 4 == 0:
                        project((s - 9) // 4)



def head_attention(nc, K, xs, W, ctx_dram):
    NH, HD = 16, 16
    NV = 9
    with ExitStack() as ctx:
        def sb(n, s, d=F32):
            return ctx.enter_context(nc.sbuf_tensor("ha_" + n, s, d))

        def pb(n, s, d=F32):
            return ctx.enter_context(nc.psum_tensor("ha_" + n, s, d))

        B = norm_buffers(sb, "n")
        xnT = sb("xnT", [P, KC, GT])
        cT = sb("cT", [P, KC, GT])
        q = sb("q", [P, 2, NH, HD])
        k = sb("k", [P, 2, NH, HD])
        vT = sb("vT", [P, 2, HD, NH])
        qk = sb("qk", [P, NH, NH, HD])
        wv = sb("wv", [P, NH, HD, NH])
        sc = sb("sc", [P, 2, NH, NH])
        sh = sb("sh", [P, 2, NH, NH])
        w = sb("w", [P, 2, NH, NH])
        nm = sb("nm", [P, 2, NH])
        z = sb("z", [P, 2, NH])
        rz = sb("rz", [P, 2, NH])
        o = sb("o", [P, 2, NH, HD])
        y = sb("y", [P, 2, C])
        yT = sb("yT", [P, 2, KC, P])
        mx = [pb(f"mx{b}", [P, 512]) for b in range(2)]
        pq = [pb(f"pq{b}", [P, 512]) for b in range(2)]
        pk = [pb(f"pk{b}", [P, 512]) for b in range(2)]
        py = pb("py", [P, 512])
        po = pb("po", [P, 512])
        S = named_semaphores(ctx, nc, "ha", NORM_SEMS + " ctx_in full emptied q_full k_full q_taken k_taken qk_dve qk_pool scored maxed"
                  " shifted weighed wv_dve wv_pool summed zed zinv y_ready turned yT out added")
        block = ctx.enter_context(nc.Block())

        def qk_product(eng, b, lo, hi):
            n = hi - lo
            return eng.tensor_tensor(qk[:, lo:hi], q[:, b, lo:hi].unsqueeze(2).to_broadcast([P, n, NH, HD]),
                                     k[:, b].unsqueeze(1).to_broadcast([P, n, NH, HD]), ALU.mult)

        def wv_product(eng, b, lo, hi):
            n = hi - lo
            return eng.tensor_tensor(wv[:, lo:hi], w[:, b, lo:hi].unsqueeze(2).to_broadcast([P, n, HD, NH]),
                                     vT[:, b].unsqueeze(1).to_broadcast([P, n, HD, NH]), ALU.mult)

        @block.sync
        def _(sp):
            sp.dma_start(cT[:], ctx_dram[:, :, 0:GT].rearrange("k p t -> p k t")).then_inc(S["ctx_in"], 16)
            with sp.Fori(1, NG) as i:
                sp.wait_ge(S["k_full"], i * TG)
                sp.dma_start(cT[:], ctx_dram[:, :, bass.ds(i * GT, GT)].rearrange("k p t -> p k t")).then_inc(S["ctx_in"], 16)

        @block.gpsimd
        def _(pool):
            pool.wait_ge(K["s"]["x"], 16 * NG)
            pool.wait_ge(K["s"]["weights"], 16 * K["n_weights"])
            pool.wait_ge(K["s"]["consts"], K["n_consts"])
            with pool.Fori(0, NG) as i:
                norm_pool(pool, S, B, K, i)
                bias_pool(pool, S, xs, W["bo"], i)
                for s in range(TG + 1):
                    if s < TG:
                        t = s
                        pool.wait_ge(S["q_taken"], i * TG + t + 1)
                        pool.wait_ge(S["k_taken"], i * TG + t + 1)
                        if t >= 1:
                            pool.wait_ge(S["scored"], i * TG + t)
                        qk_product(pool, t % 2, NV, NH).then_inc(S["qk_pool"], 1)
                    if s >= 1:
                        t = s - 1
                        pool.wait_ge(S["weighed"], i * TG + t + 1)
                        if t >= 1:
                            pool.wait_ge(S["summed"], i * TG + t)
                        wv_product(pool, t % 2, NV, NH).then_inc(S["wv_pool"], 1)

        def added(dve, i, t):
            dve.wait_ge(S["out"], i * TG + t + 1)
            dve.wait_ge(S["biased"], i * TG + t + 1)
            dve.tensor_tensor(tile_of(xs, i, t), tile_of(xs, i, t), po[:, 0:C], ALU.add).then_inc(S["added"], 1)

        @block.vector
        def _(dve):
            dve.wait_ge(K["s"]["x"], 16 * NG)
            dve.wait_ge(K["s"]["weights"], 16 * K["n_weights"])
            dve.wait_ge(K["s"]["consts"], K["n_consts"])
            with dve.Fori(0, NG) as i:
                norm_vector(dve, S, B, xs, i)
                for s in range(TG + 2):
                    if s < TG:
                        t, b = s, s % 2
                        dve.wait_ge(S["q_full"], i * TG + t + 1)
                        dve.tensor_tensor(q[:, b].rearrange("p h d -> p (h d)"), pq[b][:, 0:C], W["bq"][:],
                                          ALU.add).then_inc(S["q_taken"], 1)
                        dve.wait_ge(S["k_full"], i * TG + t + 1)
                        dve.tensor_tensor(k[:, b].rearrange("p h d -> p (h d)"), pk[b][:, 0:C], W["bk"][:], ALU.add)
                        dve.tensor_tensor(vT[:, b], pk[b][:, C:2 * C].rearrange("p (h d) -> p d h", h=NH),
                                          W["bv"][:].rearrange("p (h d) -> p d h", h=NH), ALU.add).then_inc(S["k_taken"], 1)
                        dve.wait_ge(S["k_taken"], i * TG + t + 1)
                        qk_product(dve, b, 0, NV).then_inc(S["qk_dve"], 1)
                    if 0 <= s - 1 < TG:
                        t, b = s - 1, (s - 1) % 2
                        dve.wait_ge(S["weighed"], i * TG + t + 1)
                        wv_product(dve, b, 0, NV).then_inc(S["wv_dve"], 1)
                        dve.tensor_reduce(z[:, b, :], w[:, b], AX.X, ALU.add).then_inc(S["zed"], 1)
                    if s < TG:
                        t, b = s, s % 2
                        dve.wait_ge(S["qk_dve"], i * TG + t + 1)
                        dve.wait_ge(S["qk_pool"], i * TG + t + 1)
                        dve.tensor_reduce(sc[:, b], qk[:], AX.X, ALU.add).then_inc(S["scored"], 1)
                        dve.wait_ge(S["scored"], i * TG + t + 1)
                        dve.tensor_reduce(nm[:, b, :], sc[:, b], AX.X, ALU.max, negate=True).then_inc(S["maxed"], 1)
                        dve.wait_ge(S["maxed"], i * TG + t + 1)
                        dve.tensor_tensor(sh[:, b], sc[:, b], nm[:, b, :].unsqueeze(2).to_broadcast([P, NH, NH]),
                                          ALU.add).then_inc(S["shifted"], 1)
                    if 0 <= s - 1 < TG:
                        t, b = s - 1, (s - 1) % 2
                        dve.wait_ge(S["zed"], i * TG + t + 1)
                        dve.reciprocal(rz[:, b, :], z[:, b, :]).then_inc(S["zinv"], 1)
                        dve.wait_ge(S["wv_dve"], i * TG + t + 1)
                        dve.wait_ge(S["wv_pool"], i * TG + t + 1)
                        dve.tensor_reduce(o[:, b], wv[:], AX.X, ALU.add).then_inc(S["summed"], 1)
                        dve.wait_ge(S["zinv"], i * TG + t + 1)
                        dve.wait_ge(S["summed"], i * TG + t + 1)
                        dve.tensor_tensor(y[:, b, :].rearrange("p (h d) -> p h d", h=NH), o[:, b],
                                          rz[:, b, :].unsqueeze(2).to_broadcast([P, NH, HD]), ALU.mult).then_inc(S["y_ready"], 1)
                    if 0 <= s - 2 < TG:
                        added(dve, i, s - 2)

        @block.scalar
        def _(act):
            with act.Fori(0, NG) as i:
                for t in range(TG):
                    act.wait_ge(S["full"], i * TG + t + 1)
                    act.activation(xnT[:, :, t * P:(t + 1) * P], mx[t % 2][:, 0:C].rearrange("p (a b) -> p a b", a=KC),
                                   ACT.Copy).then_inc(S["emptied"], 1)
                for s in range(TG + 1):
                    if s < TG:
                        t = s
                        act.wait_ge(S["shifted"], i * TG + t + 1)
                        act.activation(w[:, t % 2], sh[:, t % 2], ACT.Exp, scale=HD ** -0.5).then_inc(S["weighed"], 1)
                    if s >= 1:
                        t = s - 1
                        act.wait_ge(S["turned"], i * TG + t + 1)
                        act.activation(yT[:, t % 2], py[:, 0:C].rearrange("p (a b) -> p a b", a=KC),
                                       ACT.Copy).then_inc(S["yT"], 1)

        @block.tensor
        def _(pe):
            pe.wait_ge(K["s"]["x"], 16 * NG)
            pe.wait_ge(K["s"]["weights"], 16 * K["n_weights"])
            pe.wait_ge(K["s"]["consts"], K["n_consts"])
            with pe.Fori(0, NG) as i:
                for t in range(TG):
                    pe.wait_ge(S["normed"], i * TG + t + 1)
                    if t >= 2:
                        pe.wait_ge(S["emptied"], i * TG + t - 1)
                    for c in range(KC):
                        op = pe.transpose(mx[t % 2][:, c * P:(c + 1) * P], B["xn"][:, t, c * P:(c + 1) * P], K["ident"][:])
                    op.then_inc(S["full"], 1)
                pe.wait_ge(S["ctx_in"], i * 16 + 16)
                for s in range(TG + 1):
                    if s < TG:
                        t, b = s, s % 2
                        pe.wait_ge(S["emptied"], i * TG + t + 1)
                        if t >= 2:
                            pe.wait_ge(S["k_taken"], i * TG + t - 1)
                        for kc in range(KC):
                            op = pe.matmul(pq[b][:, 0:C], xnT[:, kc, t * P:(t + 1) * P], W["wq"][:, kc, :],
                                           start=(kc == 0), stop=(kc == KC - 1))
                        op.then_inc(S["q_full"], 1)
                        for kc in range(KC):
                            op = pe.matmul(pk[b][:], cT[:, kc, t * P:(t + 1) * P], W["wkv"][:, kc, :],
                                           start=(kc == 0), stop=(kc == KC - 1))
                        op.then_inc(S["k_full"], 1)
                    if s >= 1:
                        t, b = s - 1, (s - 1) % 2
                        pe.wait_ge(S["y_ready"], i * TG + t + 1)
                        if t >= 1:
                            pe.wait_ge(S["yT"], i * TG + t)
                        for c in range(KC):
                            op = pe.transpose(py[:, c * P:(c + 1) * P], y[:, b, c * P:(c + 1) * P], K["ident"][:])
                        op.then_inc(S["turned"], 1)
                        pe.wait_ge(S["yT"], i * TG + t + 1)
                        if t >= 1:
                            pe.wait_ge(S["added"], i * TG + t)
                        for kc in range(KC):
                            op = pe.matmul(po[:, 0:C], yT[:, b, kc, :], W["wo"][:, kc, :],
                                           start=(kc == 0), stop=(kc == KC - 1))
                        op.then_inc(S["out"], 1)



def route(nc, K, xs, R, pre, NE, TOP, NR, M):
    NS = 8 - TOP
    l0 = NE == NR
    with ExitStack() as ctx:
        def sb(n, s, d=F32):
            return ctx.enter_context(nc.sbuf_tensor(f"{pre}_{n}", s, d))

        def pb(n, s, d=F32):
            return ctx.enter_context(nc.psum_tensor(f"{pre}_{n}", s, d))

        B = norm_buffers(sb, "n")
        xnT = sb("xnT", [P, KC, GT])
        nm = sb("nm", [P, TG])
        sh = sb("sh", [P, TG, NE])
        ex = sb("ex", [P, TG, NE])
        z = sb("z", [P, TG])
        rz = sb("rz", [P, TG])
        pr = sb("pr", [P, TG, NE])
        cand = sb("cand", [P, TG, NE + NS])
        top8 = sb("top8", [P, TG, 8])
        pick = sb("pick", [P, TG, 8])
        mark = sb("mark", [P, TG, NE + NS])
        wt = sb("wt", [P, TG, NE])
        zs = sb("zs", [P, TG])
        ze = sb("ze", [P, TG])
        cw = sb("cw", [P, TG, NE])
        cwT = sb("cwT", [NE, TG, P])
        mx = [pb(f"mx{b}", [P, 512]) for b in range(2)]
        lg = pb("lg", [P, TG, NE])
        pt = pb("pt", [NE, TG, P])
        pbias = [pb(f"pbias{b}", [P, 512]) for b in range(2)]
        CH = 13 if l0 else 11
        S = named_semaphores(ctx, nc, pre, NORM_SEMS + " consts full emptied logits shifted exped chain topped marked weighed cw_turned"
                  " cwT bias added")
        block = ctx.enter_context(nc.Block())

        @block.gpsimd
        def _(pool):
            pool.wait_ge(K["s"]["x"], 16 * NG)
            pool.wait_ge(K["s"]["weights"], 16 * K["n_weights"])
            pool.wait_ge(K["s"]["consts"], K["n_consts"])
            with pool.Fori(0, NG) as i:
                norm_pool(pool, S, B, K, i)

        @block.vector
        def _(dve):
            dve.wait_ge(K["s"]["x"], 16 * NG)
            dve.wait_ge(K["s"]["weights"], 16 * K["n_weights"])
            dve.wait_ge(K["s"]["consts"], K["n_consts"])
            dve.memset(cand[:, :, NE:], FAR)
            dve.memset(pick[:, :, TOP:], FAR).then_inc(S["consts"], 1)
            dve.wait_ge(S["consts"], 1)
            with dve.Fori(0, NG) as i:
                step = [0]

                def link(op):
                    step[0] += 1
                    op.then_inc(S["chain"], 1)
                    dve.wait_ge(S["chain"], i * CH + step[0])

                norm_vector(dve, S, B, xs, i)
                for t in range(TG):
                    dve.wait_ge(S["emptied"], i * TG + t + 1)
                    at = bass.ds(i * GT + t * P, P)
                    dve.tensor_tensor(M["xl"][:, :, at], xnT[:, :, t * P:(t + 1) * P], M["xh"][:, :, at], ALU.subtract)
                dve.wait_ge(S["logits"], i + 1)
                link(dve.tensor_reduce(nm[:], lg[:], AX.X, ALU.max, negate=True))
                dve.tensor_tensor(sh[:], lg[:], nm[:].unsqueeze(2).to_broadcast([P, TG, NE]), ALU.add).then_inc(S["shifted"], 1)
                dve.wait_ge(S["exped"], i + 1)
                link(dve.tensor_reduce(z[:], ex[:], AX.X, ALU.add))
                link(dve.reciprocal(rz[:], z[:]))
                link(dve.tensor_tensor(pr[:], ex[:], rz[:].unsqueeze(2).to_broadcast([P, TG, NE]), ALU.mult))
                if l0:
                    link(dve.tensor_copy(cand[:, :, 0:NE], pr[:]))
                else:
                    link(dve.tensor_tensor(cand[:, :, 0:NE], pr[:], R["corr"][:].unsqueeze(1).to_broadcast([P, TG, NE]), ALU.add))
                dve.memset(B["junk"][:], 0.0)
                for t in range(TG):
                    op = dve.max(top8[:, t, :], cand[:, t, 0:NE])
                link(op)
                link(dve.tensor_copy(pick[:, :, 0:TOP], top8[:, :, 0:TOP]))
                dve.memset(B["junk"][:], 0.0)
                for t in range(TG):
                    op = dve.match_replace(mark[:, t, :], pick[:, t, :], cand[:, t, :], -FAR)
                link(op)
                if l0:
                    link(dve.scalar_tensor_tensor(out=wt[:], in0=mark[:, :, 0:NE], scalar=-FAR, in1=pr[:],
                                                  op0=ALU.is_equal, op1=ALU.mult))
                    link(dve.tensor_reduce(zs[:], wt[:], AX.X, ALU.add))
                    link(dve.tensor_scalar(ze[:], zs[:], 1e-8, None, ALU.add))
                    link(dve.reciprocal(zs[:], ze[:]))
                    link(dve.tensor_tensor(cw[:], wt[:], zs[:].unsqueeze(2).to_broadcast([P, TG, NE]), ALU.mult))
                    dve.tensor_copy(M["rw"][:, bass.ds(i * TG, TG), :], cw[:]).then_inc(S["weighed"], 1)
                    for t in range(TG):
                        dve.wait_ge(S["bias"], i * TG + t + 1)
                        dve.tensor_tensor(tile_of(xs, i, t), tile_of(xs, i, t), pbias[t % 2][:, 0:C], ALU.add).then_inc(S["added"], 1)
                else:
                    link(dve.scalar_tensor_tensor(out=wt[:], in0=mark[:, :, 0:NE], scalar=-FAR, in1=pr[:],
                                                  op0=ALU.is_equal, op1=ALU.mult))
                    link(dve.tensor_scalar(M["rw"][:, bass.ds(i * TG, TG), :], wt[:], R["scale"], None, ALU.mult))
                    link(dve.tensor_reduce(zs[:], M["rw"][:, bass.ds(i * TG, TG), NR:NE], AX.X, ALU.add))
                    for t in range(TG):
                        dve.scalar_tensor_tensor(out=tile_of(xs, i, t), in0=B["xn"][:, t, :], scalar=zs[:, t:t + 1],
                                                 in1=tile_of(xs, i, t), op0=ALU.mult, op1=ALU.add).then_inc(S["added"], 1)
                assert step[0] == CH, step[0]

        @block.scalar
        def _(act):
            with act.Fori(0, NG) as i:
                for t in range(TG):
                    act.wait_ge(S["full"], i * TG + t + 1)
                    src = mx[t % 2][:, 0:C].rearrange("p (a b) -> p a b", a=KC)
                    act.activation(xnT[:, :, t * P:(t + 1) * P], src, ACT.Copy)
                    act.activation(M["xh"][:, :, bass.ds(i * GT + t * P, P)], src, ACT.Copy).then_inc(S["emptied"], 1)
                act.wait_ge(S["shifted"], i + 1)
                act.activation(ex[:], sh[:], ACT.Exp).then_inc(S["exped"], 1)
                if l0:
                    act.wait_ge(S["cw_turned"], i + 1)
                    act.activation(cwT[:], pt[:], ACT.Copy).then_inc(S["cwT"], 1)

        @block.tensor
        def _(pe):
            pe.wait_ge(K["s"]["x"], 16 * NG)
            pe.wait_ge(K["s"]["weights"], 16 * K["n_weights"])
            pe.wait_ge(K["s"]["consts"], K["n_consts"])
            with pe.Fori(0, NG) as i:
                for t in range(TG):
                    pe.wait_ge(S["normed"], i * TG + t + 1)
                    if t >= 2:
                        pe.wait_ge(S["emptied"], i * TG + t - 1)
                    for c in range(KC):
                        op = pe.transpose(mx[t % 2][:, c * P:(c + 1) * P], B["xn"][:, t, c * P:(c + 1) * P], K["ident"][:])
                    op.then_inc(S["full"], 1)
                for t in range(TG):
                    pe.wait_ge(S["emptied"], i * TG + t + 1)
                    for kc in range(KC):
                        op = pe.matmul(lg[:, t, :], xnT[:, kc, t * P:(t + 1) * P], R["w"][:, kc, :],
                                       start=(kc == 0), stop=(kc == KC - 1))
                op.then_inc(S["logits"], 1)
                if l0:
                    pe.wait_ge(S["weighed"], i + 1)
                    for t in range(TG):
                        op = pe.transpose(pt[:, t, :], cw[:, t, :], K["ident"][:])
                    op.then_inc(S["cw_turned"], 1)
                    pe.wait_ge(S["cwT"], i + 1)
                    for t in range(TG):
                        if t >= 2:
                            pe.wait_ge(S["added"], i * TG + t - 1)
                        pe.matmul(pbias[t % 2][:, 0:C], cwT[:, t, :], R["b2"][:], start=True, stop=True).then_inc(S["bias"], 1)



def gelu_experts(nc, K, xs, M, w_dram, b1_dram, NE, H):
    HC = H // P
    EB = 2
    NCH = EB * NG * HC
    W1, W2 = KC * H, HC * C
    NHB, NL = 4, 2
    with ExitStack() as ctx:
        def sb(n, s, d=F32):
            return ctx.enter_context(nc.sbuf_tensor("ge_" + n, s, d))

        def pb(n, s, d=F32):
            return ctx.enter_context(nc.psum_tensor("ge_" + n, s, d))

        stage = sb("stage", [P, W1 + W2])
        b1 = sb("b1", [P, EB, HC])
        wh = sb("wh", [P, EB, W1 + W2], BF16)
        wl = sb("wl", [P, EB, W1 + W2], BF16)
        ew = sb("ew", [P, EB, NT])
        hf = sb("hf", [P, 2, GT])
        hh = sb("hh", [P, NHB, GT], BF16)
        hl = sb("hl", [P, NHB, GT], BF16)
        ph = [pb(f"ph{b}", [P, GT]) for b in range(4)]
        py = [[pb(f"py{s}{b}", [P, 2, C]) for b in range(2)] for s in range(2)]
        S = named_semaphores(ctx, nc, "ge", "w_in b_in0 b_in1 w_hi w_lo picked hid hi lo used y_taken")
        b_in = [S["b_in0"], S["b_in1"]]
        block = ctx.enter_context(nc.Block())

        def w1(buf, p, kc, j):
            return buf[:, p, kc * H + j * P:kc * H + (j + 1) * P]

        def w2(buf, p, j):
            return buf[:, p, W1 + j * C:W1 + (j + 1) * C]

        @block.sync
        def _(sp):
            sp.dma_start(stage[:], w_dram[0]).then_inc(S["w_in"], 16)
            sp.dma_start(b1[:, 0, :], b1_dram[0]).then_inc(b_in[0], 16)
            sp.wait_ge(S["w_hi"], 2)
            sp.wait_ge(S["w_lo"], 2)
            sp.dma_start(stage[:], w_dram[1]).then_inc(S["w_in"], 16)
            sp.dma_start(b1[:, 1, :], b1_dram[1]).then_inc(b_in[1], 16)
            with sp.Fori(1, NE // EB) as i:
                for p in range(EB):
                    sp.wait_ge(S["w_hi"], (i * EB + p) * 2)
                    sp.wait_ge(S["w_lo"], (i * EB + p) * 2)
                    sp.dma_start(stage[:], w_dram[bass.ds(i * EB + p, 1)].rearrange("a p n -> p (a n)")).then_inc(S["w_in"], 16)
                    sp.wait_ge(S["hi"], (i * EB + p - 1) * NG * HC)
                    sp.dma_start(b1[:, p, :], b1_dram[bass.ds(i * EB + p, 1)].rearrange("a p n -> p (a n)")).then_inc(b_in[p], 16)

        halves = ((0, W1), (W1, W1 + W2))

        @block.scalar
        def _(act):
            with act.Fori(0, NE // EB) as i:
                def split(p):
                    act.wait_ge(S["w_in"], (i * EB + p) * 16 + 16)
                    for a, b in halves:
                        act.activation(wh[:, p, a:b], stage[:, a:b], ACT.Copy).then_inc(S["w_hi"], 1)

                split(0)
                for q in range(NCH):
                    p, j = q // (NG * HC), q % HC
                    if q == NG * HC - HC:
                        split(1)
                    if q % (NG * HC) == 0:
                        act.wait_ge(b_in[p], i * 16 + 16)
                    act.wait_ge(S["hid"], i * NCH + q + 1)
                    if q >= 2:
                        act.wait_ge(S["lo"], i * NCH + q - 1)
                    act.activation(hf[:, q % 2, :], ph[q % 4][:], ACT.Gelu_apprx_tanh, bias=b1[:, p, j:j + 1])
                    if q >= NHB:
                        act.wait_ge(S["used"], i * NCH + q - NHB + 1)
                    act.activation(hh[:, q % NHB, :], ph[q % 4][:], ACT.Gelu_apprx_tanh, bias=b1[:, p, j:j + 1]).then_inc(S["hi"], 1)

        def taken(dve, i, n):
            p, g = n // NG, n % NG
            dve.wait_ge(S["used"], i * NCH + (n + 1) * HC)
            dve.wait_ge(S["picked"], i * EB + p + 1)
            for t in range(TG):
                T = g * TG + t
                op = dve.scalar_tensor_tensor(out=xs[:, T, :], in0=py[n % 2][t // 2][:, t % 2, :], scalar=ew[:, p, T:T + 1],
                                              in1=xs[:, T, :], op0=ALU.mult, op1=ALU.add)
            op.then_inc(S["y_taken"], 1)

        @block.vector
        def _(dve):
            dve.sem_inc(S["y_taken"], 2)
            with dve.Fori(0, NE // EB) as i:
                def split(p):
                    for n, (a, b) in enumerate(halves):
                        dve.wait_ge(S["w_hi"], (i * EB + p) * 2 + n + 1)
                        dve.tensor_tensor(wl[:, p, a:b], stage[:, a:b], wh[:, p, a:b], ALU.subtract).then_inc(S["w_lo"], 1)
                    dve.tensor_copy(ew[:, p, :], M["rw"][:, :, bass.ds(i * EB + p, 1)].rearrange("p t a -> p (t a)")).then_inc(S["picked"], 1)

                split(0)
                for q in range(NCH + 3):
                    if q == NG * HC - HC:
                        split(1)
                    if q < NCH:
                        dve.wait_ge(S["hi"], i * NCH + q + 1)
                        dve.tensor_tensor(hl[:, q % NHB, :], hf[:, q % 2, :], hh[:, q % NHB, :], ALU.subtract).then_inc(S["lo"], 1)
                    if q >= HC + 2 and (q - 2) % HC == 0:
                        n = (q - 2) // HC - 1
                        taken(dve, i, n)

        @block.tensor
        def _(pe):
            with pe.Fori(0, NE // EB) as i:
                for q in range(NCH + NL):
                    if q < NCH:
                        p, g, j = q // (NG * HC), q // HC % NG, q % HC
                        if q % (NG * HC) == 0:
                            pe.wait_ge(S["w_lo"], (i * EB + p) * 2 + 1)
                        if q >= 4:
                            pe.wait_ge(S["hi"], i * NCH + q - 3)
                        n = 0
                        for kc in range(KC):
                            for w, x in ((wh, "xh"), (wh, "xl"), (wl, "xh")):
                                op = pe.matmul(ph[q % 4][:], w1(w, p, kc, j), M[x][:, kc, g * GT:(g + 1) * GT],
                                               start=(n == 0), stop=(n == 3 * KC - 1))
                                n += 1
                        op.then_inc(S["hid"], 1)
                    if q >= NL:
                        q2 = q - NL
                        p, n, j = q2 // (NG * HC), q2 // HC, q2 % HC
                        if q2 % (NG * HC) == 0:
                            pe.wait_ge(S["w_lo"], (i * EB + p) * 2 + 2)
                        if j == 0:
                            pe.wait_ge(S["y_taken"], i * EB * NG + n + 1)
                        pe.wait_ge(S["lo"], i * NCH + q2 + 1)
                        for t in range(TG):
                            for m, (h, w) in enumerate(((hh, wh), (hh, wl), (hl, wh))):
                                op = pe.matmul(py[n % 2][t // 2][:, t % 2, :], h[:, q2 % NHB, t * P:(t + 1) * P], w2(w, p, j),
                                               start=(j == 0 and m == 0 and t % 2 == 0), stop=(j == HC - 1 and m == 2),
                                               skip_group_check=True)
                        op.then_inc(S["used"], 1)



def silu_experts(nc, K, xs, M, w_dram, NR, I):
    EB = 4
    NU = EB * NG
    WG, WD = KC * 2 * I, C
    NHB, NL = 4, 2
    with ExitStack() as ctx:
        def sb(n, s, d=F32):
            return ctx.enter_context(nc.sbuf_tensor("se_" + n, s, d))

        def pb(n, s, d=F32):
            return ctx.enter_context(nc.psum_tensor("se_" + n, s, d))

        stage = sb("stage", [P, EB, WG + WD])
        wh = sb("wh", [P, EB, WG + WD], BF16)
        wl = sb("wl", [P, EB, WG + WD], BF16)
        ew = sb("ew", [P, EB, NT])
        sg = sb("sg", [P, 2, GT])
        hf = sb("hf", [P, NHB, GT])
        hh = sb("hh", [P, NHB, GT], BF16)
        hl = sb("hl", [P, NHB, GT], BF16)
        pg = [pb(f"pg{b}", [P, GT]) for b in range(2)]
        pu = [pb(f"pu{b}", [P, GT]) for b in range(2)]
        py = [[pb(f"py{s}{b}", [P, 2, C]) for b in range(2)] for s in range(2)]
        S = named_semaphores(ctx, nc, "se", "w_in0 w_in1 w_in2 w_in3 w_hi w_lo picked gu silu prod hi lo used y_taken")
        w_in = [S["w_in0"], S["w_in1"], S["w_in2"], S["w_in3"]]
        block = ctx.enter_context(nc.Block())

        def wgu(buf, p, kc, half):
            return buf[:, p, kc * 2 * I + half * I:kc * 2 * I + (half + 1) * I]

        @block.sync
        def _(sp):
            for p in range(EB):
                sp.dma_start(stage[:, p, :], w_dram[p]).then_inc(w_in[p], 16)
            with sp.Fori(1, NR // EB) as i:
                for p in range(EB):
                    sp.wait_ge(S["w_hi"], (i - 1) * EB + p + 1)
                    sp.wait_ge(S["w_lo"], (i - 1) * EB + p + 1)
                    sp.dma_start(stage[:, p, :], w_dram[bass.ds(i * EB + p, 1)].rearrange("a p n -> p (a n)")).then_inc(w_in[p], 16)

        @block.scalar
        def _(act):
            with act.Fori(0, NR // EB) as i:
                def split(p):
                    act.wait_ge(w_in[p], i * 16 + 16)
                    act.activation(wh[:, p, :], stage[:, p, :], ACT.Copy).then_inc(S["w_hi"], 1)

                split(0)
                for u in range(NU + 1):
                    if u < NU:
                        act.wait_ge(S["gu"], i * NU + u + 1)
                        if u >= 2:
                            act.wait_ge(S["prod"], i * NU + u - 1)
                        act.activation(sg[:, u % 2, :], pg[u % 2][:], ACT.Silu).then_inc(S["silu"], 1)
                    if u >= 1:
                        v = u - 1
                        act.wait_ge(S["prod"], i * NU + v + 1)
                        if v >= NHB:
                            act.wait_ge(S["used"], i * NU + v - NHB + 1)
                        act.activation(hh[:, v % NHB, :], hf[:, v % NHB, :], ACT.Copy).then_inc(S["hi"], 1)
                    if u % NG == 1 and u // NG + 1 < EB:
                        split(u // NG + 1)

        def taken(dve, i, n):
            p, g = n // NG, n % NG
            dve.wait_ge(S["used"], i * NU + n + 1)
            dve.wait_ge(S["picked"], i * EB + p + 1)
            for t in range(TG):
                T = g * TG + t
                op = dve.scalar_tensor_tensor(out=xs[:, T, :], in0=py[n % 2][t // 2][:, t % 2, :], scalar=ew[:, p, T:T + 1],
                                              in1=xs[:, T, :], op0=ALU.mult, op1=ALU.add)
            op.then_inc(S["y_taken"], 1)

        @block.vector
        def _(dve):
            dve.sem_inc(S["y_taken"], 2)
            with dve.Fori(0, NR // EB) as i:
                def split(p):
                    dve.wait_ge(S["w_hi"], i * EB + p + 1)
                    dve.tensor_tensor(wl[:, p, :], stage[:, p, :], wh[:, p, :], ALU.subtract).then_inc(S["w_lo"], 1)
                    dve.tensor_copy(ew[:, p, :], M["rw"][:, :, bass.ds(i * EB + p, 1)].rearrange("p t a -> p (t a)")).then_inc(S["picked"], 1)

                split(0)
                for u in range(NU + 3):
                    if u < NU:
                        dve.wait_ge(S["silu"], i * NU + u + 1)
                        dve.tensor_tensor(hf[:, u % NHB, :], sg[:, u % 2, :], pu[u % 2][:], ALU.mult).then_inc(S["prod"], 1)
                    if 0 <= u - 1 < NU:
                        v = u - 1
                        dve.wait_ge(S["hi"], i * NU + v + 1)
                        dve.tensor_tensor(hl[:, v % NHB, :], hf[:, v % NHB, :], hh[:, v % NHB, :], ALU.subtract).then_inc(S["lo"], 1)
                    if u % NG == 1 and u // NG + 1 < EB:
                        split(u // NG + 1)
                    if u >= 3:
                        taken(dve, i, u - 3)

        @block.tensor
        def _(pe):
            with pe.Fori(0, NR // EB) as i:
                for u in range(NU + NL):
                    if u < NU:
                        p, g = u // NG, u % NG
                        if g == 0:
                            pe.wait_ge(S["w_lo"], i * EB + p + 1)
                        if u >= 2:
                            pe.wait_ge(S["prod"], i * NU + u - 1)
                        for half, bank in ((0, pg), (1, pu)):
                            n = 0
                            for kc in range(KC):
                                for w, x in ((wh, "xh"), (wh, "xl"), (wl, "xh")):
                                    op = pe.matmul(bank[u % 2][:], wgu(w, p, kc, half), M[x][:, kc, g * GT:(g + 1) * GT],
                                                   start=(n == 0), stop=(n == 3 * KC - 1))
                                    n += 1
                        op.then_inc(S["gu"], 1)
                    if u >= NL:
                        v = u - NL
                        p = v // NG
                        pe.wait_ge(S["y_taken"], i * NU + v + 1)
                        pe.wait_ge(S["lo"], i * NU + v + 1)
                        for t in range(TG):
                            for m, (h, w) in enumerate(((hh, wh), (hh, wl), (hl, wh))):
                                op = pe.matmul(py[v % 2][t // 2][:, t % 2, :], h[:, v % NHB, t * P:(t + 1) * P], w[:, p, WG:],
                                               start=(m == 0), stop=(m == 2))
                        op.then_inc(S["used"], 1)



NE0, TOP0, H0 = 8, 2, 1024
NE1, NR1, TOP1, I1 = 40, 32, 6, 128
SCALE1 = 2.5


def mixture_buffers(ctx, nc, pre, NE):
    def sb(n, s, d=F32):
        return ctx.enter_context(nc.sbuf_tensor(f"{pre}_{n}", s, d))

    return dict(xh=sb("xh", [P, KC, NT * P], BF16), xl=sb("xl", [P, KC, NT * P], BF16), rw=sb("rw", [P, NT, NE]))


def decoder(nc, A, out):
    with ExitStack() as ctx:
        def sb(n, s, d=F32):
            return ctx.enter_context(nc.sbuf_tensor(n, s, d))

        xs = sb("xs", [P, NT, C])
        K = {"s": named_semaphores(ctx, nc, "g", "x weights consts zeroed stored")}
        K["ident"] = sb("ident", [P, P])
        K["identb"] = sb("identb", [P, P], BF16)
        K["causal"] = sb("causal", [P, 4, P], BF16)
        K["heads8"] = sb("heads8", [P, P])
        K["evenodd"] = sb("evenodd", [P, 2])
        K["eps4"] = sb("eps4", [P, TG])
        K["half4"] = sb("half4", [P, TG])
        loads = []

        def square(name, cols=C):
            w = sb("w_" + name, [P, KC, cols])
            loads.append((w, A[name].rearrange("(k p) n -> p k n", p=P)))
            return w

        def column(name, n):
            b = sb("b_" + name, [P, n])
            loads.append((b, A[name]))
            return b

        def spread(name):
            b = sb("r_" + name, [P, C])
            loads.append((b, A[name].partition_broadcast(P)))
            return b

        WA = dict(qkv=square("L0_attn_qkv_weight", 3 * C), wp=square("L0_attn_proj_weight"), bp=spread("L0_attn_proj_bias"))
        WX = {k: square("L0_xattn_W" + k[1]) for k in ("wq", "wk", "wv", "wo")}
        WX.update(bq=column("L0_xattn_bq", KC), bk=column("L0_xattn_bk", KC), bv=spread("L0_xattn_bv"), bo=spread("L0_xattn_bo"))
        w_attn = square("L1_attn_w_attn", 3 * C)
        WS = dict(wq=w_attn[:, :, 0:C], wk=w_attn[:, :, C:2 * C], wv=w_attn[:, :, 2 * C:3 * C], wo=square("L1_attn_w_proj"))
        WS.update(bq=column("L1_attn_bq", KC), bk=column("L1_attn_bk", KC), bv=spread("L1_attn_bv"), bo=spread("L1_attn_b_proj"))
        WH = dict(wq=square("L1_xattn_Wq"), wkv=square("L1_xattn_Wkv", 2 * C), wo=square("L1_xattn_Wo"))
        WH.update({b: spread("L1_xattn_" + b) for b in ("bq", "bk", "bv", "bo")})
        R0 = dict(w=square("L0_ffn_router_w", NE0), b2=sb("b2_0", [NE0, C]))
        loads.append((R0["b2"], A["L0_ffn_b2"]))
        R1 = dict(w=square("L1_ffn_classifier_weight", NE1), corr=sb("corr", [P, NE1]), scale=SCALE1)
        loads.append((R1["corr"], A["L1_ffn_corr"].partition_broadcast(P)))
        K["n_weights"] = len(loads)
        K["n_consts"] = 5

        with nc.Block() as block:
            @block.sync
            def _(sp):
                for g in range(NG):
                    sp.dma_start(xs[:, g * TG:(g + 1) * TG, :],
                                 A["x"][g * TG:(g + 1) * TG].rearrange("b t c -> t b c")).then_inc(K["s"]["x"], 16)
                for dst, src in loads:
                    sp.dma_start(dst[:], src).then_inc(K["s"]["weights"], 16)

            @block.gpsimd
            def _(pool):
                s = K["s"]
                pool.memset(K["eps4"][:], LN_EPS).then_inc(s["zeroed"], 1)
                pool.memset(K["half4"][:], -0.5).then_inc(s["zeroed"], 1)
                pool.memset(K["ident"][:], 0.0).then_inc(s["zeroed"], 1)
                pool.memset(K["identb"][:], 0.0).then_inc(s["zeroed"], 1)
                pool.memset(K["causal"][:], 0.0).then_inc(s["zeroed"], 1)
                pool.memset(K["heads8"][:], 1.0).then_inc(s["zeroed"], 1)
                pool.memset(K["evenodd"][:], 0.0).then_inc(s["zeroed"], 1)
                pool.wait_ge(s["zeroed"], 7)
                for name in ("ident", "identb"):
                    pool.affine_select(out=K[name][:], in_=K[name][:], compare_op=ALU.not_equal, fill=1.0, base=0,
                                       pattern=[[-1, P]], channel_multiplier=1).then_inc(s["consts"], 1)
                pool.affine_select(out=K["causal"][:], in_=K["causal"][:], compare_op=ALU.is_ge, fill=-1e30, base=0,
                                   pattern=[[0, 4], [-1, P]], channel_multiplier=1).then_inc(s["consts"], 1)
                h8 = K["heads8"][:].rearrange("p (b e) -> p b e", e=8)
                pool.affine_select(out=h8, in_=h8, compare_op=ALU.is_ge, fill=0.0, base=0,
                                   pattern=[[-8, 16], [0, 8]], channel_multiplier=1).then_inc(s["zeroed"], 1)
                pool.wait_ge(s["zeroed"], 8)
                pool.affine_select(out=h8, in_=h8, compare_op=ALU.is_ge, fill=0.0, base=7,
                                   pattern=[[8, 16], [0, 8]], channel_multiplier=-1).then_inc(s["consts"], 1)
            @block.vector
            def _(dve):
                s = K["s"]
                dve.wait_ge(s["consts"], 4)
                idr = K["ident"][:].rearrange("p (q r n) -> p r q n", q=4, r=2)
                dve.tensor_reduce(K["evenodd"][:], idr, AX.XY, ALU.add).then_inc(s["consts"], 1)

        linear_attention(nc, K, xs, WA)
        softmax_attention(nc, K, xs, WX, "xa", ctx_dram=A["ctx_T"])
        with ExitStack() as m:
            M = mixture_buffers(m, nc, "m0", NE0)
            route(nc, K, xs, R0, "r0", NE0, TOP0, NE0, M)
            gelu_experts(nc, K, xs, M, A["L0_ffn_w"], A["L0_ffn_b1"], NE0, H0)
        softmax_attention(nc, K, xs, WS, "sa", causal=True)
        head_attention(nc, K, xs, WH, A["ctx_T"])
        with ExitStack() as m:
            M = mixture_buffers(m, nc, "m1", NE1)
            route(nc, K, xs, R1, "r1", NE1, TOP1, NR1, M)
            silu_experts(nc, K, xs, M, A["L1_ffn_w"], NR1, I1)

        with nc.Block() as block:
            @block.sync
            def _(sp):
                s = K["s"]
                for g in range(NG):
                    sp.dma_start(out[g * TG:(g + 1) * TG].rearrange("b t c -> t b c"),
                                 xs[:, g * TG:(g + 1) * TG, :]).then_inc(s["stored"], 16)
                sp.wait_ge(s["stored"], 16 * NG)


def kernel(**inputs):
    import numpy as _np
    import concourse.bacc as _bacc
    from concourse import mybir as _mybir
    from concourse.bass_utils import run_bass_kernel_spmd as _run

    a = {k: _np.asarray(v) for k, v in inputs.items()}
    laid = {
        "x": a["x"],
        "ctx_T": a["ctx_1024"].reshape(NT * P, C).T.reshape(KC, P, NT * P),
        "L0_attn_qkv_weight": a["L0_attn_qkv_weight"].T,
        "L0_attn_proj_weight": a["L0_attn_proj_weight"].T,
        "L0_attn_proj_bias": a["L0_attn_proj_bias"],
        "L1_attn_w_attn": a["L1_attn_w_attn"],
        "L1_attn_w_proj": a["L1_attn_w_proj"],
        "L1_attn_bq": a["L1_attn_b_attn"][0:C].reshape(KC, P).T,
        "L1_attn_bk": a["L1_attn_b_attn"][C:2 * C].reshape(KC, P).T,
        "L1_attn_bv": a["L1_attn_b_attn"][2 * C:3 * C],
        "L1_attn_b_proj": a["L1_attn_b_proj"],
        "L0_xattn_bv": a["L0_xattn_bv"], "L0_xattn_bo": a["L0_xattn_bo"],
        "L0_xattn_bq": a["L0_xattn_bq"].reshape(KC, P).T,
        "L0_xattn_bk": a["L0_xattn_bk"].reshape(KC, P).T,
    }
    w1 = a["L0_ffn_w1"].transpose(0, 2, 1).reshape(NE0, KC, P, H0).transpose(0, 2, 1, 3).reshape(NE0, P, KC * H0)
    w2 = a["L0_ffn_w2"].transpose(0, 2, 1).reshape(NE0, H0 // P, P, C).transpose(0, 2, 1, 3).reshape(NE0, P, H0 // P * C)
    gu = a["L1_ffn_gate_up_proj"][:NR1].transpose(0, 2, 1).reshape(NR1, KC, P, 2 * I1).transpose(0, 2, 1, 3).reshape(NR1, P, KC * 2 * I1)
    laid.update({
        "L0_ffn_w": _np.concatenate([w1, w2], axis=2),
        "L0_ffn_b1": a["L0_ffn_b1"].reshape(NE0, H0 // P, P).transpose(0, 2, 1),
        "L0_ffn_b2": a["L0_ffn_b2"],
        "L0_ffn_router_w": a["L0_ffn_router_w"].T,
        "L1_ffn_w": _np.concatenate([gu, a["L1_ffn_down_proj"].transpose(0, 2, 1)], axis=2),
        "L1_ffn_classifier_weight": a["L1_ffn_classifier_weight"].T,
        "L1_ffn_corr": a["L1_ffn_e_score_correction_bias"],
        "L1_xattn_Wq": a["L1_xattn_Wq"],
        "L1_xattn_Wkv": _np.concatenate([a["L1_xattn_Wk"], a["L1_xattn_Wv"]], axis=1),
        "L1_xattn_Wo": a["L1_xattn_Wo"],
        **{"L1_xattn_" + b: a["L1_xattn_" + b] for b in ("bq", "bk", "bv", "bo")},
    })
    for w in ("Wq", "Wk", "Wv", "Wo"):
        laid["L0_xattn_" + w] = a["L0_xattn_" + w].T
    nc = _bacc.Bacc("TRN2", target_bir_lowering=False, num_devices=1)
    arrays, A = {}, {}
    for name, v in laid.items():
        v = _np.ascontiguousarray(v)
        arrays[f"in_{name}"] = v
        A[name] = nc.dram_tensor(f"in_{name}", v.shape, _mybir.dt.from_np(v.dtype), kind="ExternalInput").ap()
    out = nc.dram_tensor("out", (NT, P, C), F32, kind="ExternalOutput").ap()
    decoder(nc, A, out)
    r = _run(nc, [arrays], core_ids=[0])
    return r.results[0]["out"]
```

```python
from contextlib import ExitStack

import concourse.bass as bass
from concourse import mybir

P = 128
NT = 16
TG = 4
NG = NT // TG
GT = TG * P
C = 256
KC = C // P
LN_EPS = 1e-5
LIN_EPS = 1e-15
FAR = 3.0e38

F32 = mybir.dt.float32
BF16 = mybir.dt.bfloat16
ALU = mybir.AluOpType
ACT = mybir.ActivationFunctionType
AX = mybir.AxisListType


def named_semaphores(ctx, nc, prefix, names):
    sems = {n: nc.alloc_semaphore(f"{prefix}_{n}") for n in names.split()}

    def give_back():
        nc.clear_and_free_semaphores(list(sems.values()))
        nc.all_engine_barrier()

    ctx.callback(give_back)
    return sems


def drained(uses, n):
    return sum(u == uses[n] for u in uses[:n + 1])


def total(uses, who):
    return sum(u == who for u in uses)


def tile_of(buf, i, t):
    return buf[:, bass.ds(i * TG + t, 1), :].rearrange("p a c -> p (a c)")



NORM_SEMS = "stats moments eps rstd normed biased"


def norm_buffers(sb, pre):
    return dict(st=sb(f"{pre}_st", [P, TG, 6]), mv=sb(f"{pre}_mv", [P, TG, 2]), ve=sb(f"{pre}_ve", [P, TG]),
                rs=sb(f"{pre}_rs", [P, TG]), xn=sb(f"{pre}_xn", [P, TG, C]), junk=sb(f"{pre}_junk", [P, 1]))


def norm_vector(dve, S, B, xs, i):
    for t in range(TG):
        dve.bn_stats(B["st"][:, t, :], tile_of(xs, i, t)).then_inc(S["stats"], 1)
    dve.wait_ge(S["stats"], i * TG + TG)
    dve.memset(B["junk"][:], 0.0)
    for t in range(TG):
        dve.bn_aggr(B["mv"][:, t, :], B["st"][:, t, :]).then_inc(S["moments"], 1)
    dve.wait_ge(S["rstd"], i + 1)
    for t in range(TG):
        dve.tensor_scalar(B["xn"][:, t, :], tile_of(xs, i, t), B["mv"][:, t, 0:1], B["rs"][:, t:t + 1],
                          ALU.subtract, ALU.mult).then_inc(S["normed"], 1)


def norm_pool(pool, S, B, K, i):
    pool.wait_ge(S["moments"], i * TG + TG)
    pool.tensor_tensor(B["ve"][:], B["mv"][:, :, 1], K["eps4"][:], ALU.add).then_inc(S["eps"], 1)
    pool.wait_ge(S["eps"], i + 1)
    pool.tensor_tensor(B["rs"][:], B["ve"][:], K["half4"][:], ALU.pow).then_inc(S["rstd"], 1)


def bias_pool(pool, S, xs, bias, i):
    for t in range(TG):
        pool.wait_ge(S["normed"], i * TG + t + 1)
        pool.tensor_tensor(tile_of(xs, i, t), tile_of(xs, i, t), bias[:], ALU.add).then_inc(S["biased"], 1)



def linear_attention(nc, K, xs, W):
    with ExitStack() as ctx:
        def sb(n, s, d=F32):
            return ctx.enter_context(nc.sbuf_tensor("la_" + n, s, d))

        def pb(n, s, d=F32):
            return ctx.enter_context(nc.psum_tensor("la_" + n, s, d))

        B = norm_buffers(sb, "n")
        xnT = sb("xnT", [P, KC, GT])
        qT = sb("qT", [P, KC, GT])
        k = sb("k", [P, TG, C])
        v1 = sb("v1", [P, TG, KC, P + 1])
        nd = sb("nd", [P, 2, KC, 2, P])
        den = sb("den", [P, 2, KC, P])
        rden = sb("rden", [P, 2, KC, P])
        y = sb("y", [P, 2, C])
        yT = sb("yT", [P, 2, KC, P])
        mx = [pb(f"mx{b}", [P, 512]) for b in range(2)]
        vk = [pb(f"vk{b}", [P, KC, 256]) for b in range(2)]
        pn = [pb(f"pn{b}", [P, KC, 2, P]) for b in range(2)]
        py = pb("py", [P, 512])
        po = pb("po", [P, 512])
        S = named_semaphores(ctx, nc, "la", NORM_SEMS + " ones full emptied vk masked nd den_eps den_inv y_ready turned yT out added")
        USES = 4 + 2 + 4
        block = ctx.enter_context(nc.Block())

        @block.gpsimd
        def _(pool):
            pool.memset(v1[:, :, :, P:P + 1], 1.0).then_inc(S["ones"], 1)
            pool.wait_ge(K["s"]["x"], 16 * NG)
            pool.wait_ge(K["s"]["weights"], 16 * K["n_weights"])
            with pool.Fori(0, NG) as i:
                norm_pool(pool, S, B, K, i)
                bias_pool(pool, S, xs, W["bp"], i)

        @block.vector
        def _(dve):
            dve.wait_ge(K["s"]["x"], 16 * NG)
            with dve.Fori(0, NG) as i:
                norm_vector(dve, S, B, xs, i)
                for s in range(TG + 3):
                    if s < TG:
                        t = s
                        dve.wait_ge(S["vk"], i * TG + t + 1)
                        dve.tensor_tensor(nd[:, t % 2, :, 0, :], vk[t % 2][:, :, 0:P],
                                          K["heads8"][:].unsqueeze(1).to_broadcast([P, KC, P]), ALU.mult)
                        for c in range(KC):
                            op = dve.tensor_scalar(nd[:, t % 2, c, 1, :], K["heads8"][:], vk[t % 2][:, c, P:P + 1],
                                                   None, ALU.mult)
                        op.then_inc(S["masked"], 1)
                    if 0 <= s - 1 < TG:
                        t = s - 1
                        dve.wait_ge(S["nd"], i * TG + t + 1)
                        dve.tensor_scalar(den[:, t % 2], pn[t % 2][:, :, 1, :], LIN_EPS, None,
                                          ALU.add).then_inc(S["den_eps"], 1)
                        dve.wait_ge(S["den_eps"], i * TG + t + 1)
                        dve.reciprocal(rden[:, t % 2], den[:, t % 2]).then_inc(S["den_inv"], 1)
                        dve.wait_ge(S["den_inv"], i * TG + t + 1)
                        dve.tensor_tensor(y[:, t % 2, :].rearrange("p (a b) -> p a b", a=KC), pn[t % 2][:, :, 0, :],
                                          rden[:, t % 2], ALU.mult).then_inc(S["y_ready"], 1)
                    if 0 <= s - 3 < TG:
                        t = s - 3
                        dve.wait_ge(S["out"], i * TG + t + 1)
                        dve.wait_ge(S["biased"], i * TG + t + 1)
                        dve.tensor_tensor(tile_of(xs, i, t), tile_of(xs, i, t), po[:, 0:C], ALU.add).then_inc(S["added"], 1)

        @block.scalar
        def _(act):
            act.wait_ge(S["ones"], 1)
            with act.Fori(0, NG) as i:
                for t in range(TG):
                    act.wait_ge(S["full"], i * USES + t + 1)
                    act.activation(xnT[:, :, t * P:(t + 1) * P], mx[t % 2][:, 0:C].rearrange("p (a b) -> p a b", a=KC),
                                   ACT.Copy).then_inc(S["emptied"], 1)
                for c in range(KC):
                    act.wait_ge(S["full"], i * USES + 4 + c + 1)
                    act.activation(qT[:, c, :], mx[c % 2][:], ACT.Relu).then_inc(S["emptied"], 1)
                for t in range(TG):
                    act.wait_ge(S["full"], i * USES + 6 + t + 1)
                    act.activation(k[:, t, :], mx[t % 2][:, 0:C], ACT.Relu)
                    act.activation(v1[:, t, :, 0:P], mx[t % 2][:, C:2 * C].rearrange("p (a b) -> p a b", a=KC),
                                   ACT.Relu).then_inc(S["emptied"], 1)
                for t in range(TG):
                    act.wait_ge(S["turned"], i * TG + t + 1)
                    act.activation(yT[:, t % 2], py[:, 0:C].rearrange("p (a b) -> p a b", a=KC),
                                   ACT.Copy).then_inc(S["yT"], 1)

        @block.tensor
        def _(pe):
            pe.wait_ge(K["s"]["weights"], 16 * K["n_weights"])
            pe.wait_ge(K["s"]["consts"], K["n_consts"])
            pe.wait_ge(S["ones"], 1)
            with pe.Fori(0, NG) as i:
                for t in range(TG):
                    pe.wait_ge(S["normed"], i * TG + t + 1)
                    if t >= 2:
                        pe.wait_ge(S["emptied"], i * USES + t - 1)
                    for c in range(KC):
                        op = pe.transpose(mx[t % 2][:, c * P:(c + 1) * P], B["xn"][:, t, c * P:(c + 1) * P], K["ident"][:])
                    op.then_inc(S["full"], 1)
                for c in range(KC):
                    pe.wait_ge(S["emptied"], i * USES + 4)
                    if c:
                        pe.wait_ge(S["emptied"], i * USES + 4)
                    for kc in range(KC):
                        op = pe.matmul(mx[c % 2][:], W["qkv"][:, kc, c * P:(c + 1) * P], xnT[:, kc, :],
                                       start=(kc == 0), stop=(kc == KC - 1))
                    op.then_inc(S["full"], 1)
                for t in range(TG):
                    pe.wait_ge(S["emptied"], i * USES + 5 + t)
                    for kc in range(KC):
                        op = pe.matmul(mx[t % 2][:], xnT[:, kc, t * P:(t + 1) * P], W["qkv"][:, kc, C:3 * C],
                                       start=(kc == 0), stop=(kc == KC - 1))
                    op.then_inc(S["full"], 1)
                for s in range(TG + 3):
                    if s < TG:
                        t = s
                        pe.wait_ge(S["emptied"], i * USES + 7 + t)
                        if t >= 2:
                            pe.wait_ge(S["masked"], i * TG + t - 1)
                        for c in range(KC):
                            op = pe.matmul(vk[t % 2][:, c, 0:P + 1], k[:, t, c * P:(c + 1) * P], v1[:, t, c, :],
                                           start=True, stop=True)
                        op.then_inc(S["vk"], 1)
                    if 0 <= s - 1 < TG:
                        t = s - 1
                        pe.wait_ge(S["masked"], i * TG + t + 1)
                        if t >= 2:
                            pe.wait_ge(S["y_ready"], i * TG + t - 1)
                        for c in range(KC):
                            op = pe.matmul(pn[t % 2][:, c], qT[:, c, t * P:(t + 1) * P],
                                           nd[:, t % 2, c].rearrange("p a b -> p (a b)"), start=True, stop=True)
                        op.then_inc(S["nd"], 1)
                    if 0 <= s - 2 < TG:
                        t = s - 2
                        pe.wait_ge(S["y_ready"], i * TG + t + 1)
                        if t >= 1:
                            pe.wait_ge(S["yT"], i * TG + t)
                        for c in range(KC):
                            op = pe.transpose(py[:, c * P:(c + 1) * P], y[:, t % 2, c * P:(c + 1) * P], K["ident"][:])
                        op.then_inc(S["turned"], 1)
                    if 0 <= s - 3 < TG:
                        t = s - 3
                        pe.wait_ge(S["yT"], i * TG + t + 1)
                        if t >= 1:
                            pe.wait_ge(S["added"], i * TG + t)
                        for kc in range(KC):
                            op = pe.matmul(po[:, 0:C], yT[:, t % 2, kc, :], W["wp"][:, kc, :],
                                           start=(kc == 0), stop=(kc == KC - 1))
                        op.then_inc(S["out"], 1)



def softmax_attention(nc, K, xs, W, pre, ctx_dram=None, causal=False, M=None):
    NH, HD = 16, 16
    NB = 4
    UN = TG * NB
    with ExitStack() as ctx:
        def sb(n, s, d=F32):
            return ctx.enter_context(nc.sbuf_tensor(f"{pre}_{n}", s, d))

        def pb(n, s, d=F32):
            return ctx.enter_context(nc.psum_tensor(f"{pre}_{n}", s, d))

        B = norm_buffers(sb, "n")
        xnT = sb("xnT", [P, KC, GT])
        cT = sb("cT", [P, KC, GT]) if ctx_dram is not None else xnT
        qT = sb("qT", [P, KC, GT])
        kk = sb("kk", [P, KC, TG, 2, P])
        vp = sb("vp", [P, TG, NH, 2 * HD])
        p = sb("p", [P, 2, 4, P])
        pT = sb("pT", [P, 2, 4, P])
        nm = sb("nm", [P, 2, 4])
        z = sb("z", [P, 2, 4])
        rz = sb("rz", [P, 2, 4])
        bq = sb("bq", [P, KC])
        yT = sb("yT", [P, KC, P])
        mx = [pb(f"mx{b}", [P, 512]) for b in range(2)]
        sc = [pb(f"sc{b}", [P, 4, P]) for b in range(2)]
        tp = [pb(f"tp{b}", [P, 4, P]) for b in range(2)]
        py = [pb(f"py{b}", [P, KC, P]) for b in range(2)]
        S = named_semaphores(ctx, nc, pre, NORM_SEMS + " zeros bq ctx_in full by_act by_dve scored maxed exped summed zinv scaled"
                  " pt_full pt pv yT")
        USES = ["act"] * 4 + ["act"] * 2 + ["dve"] * 2 + ["dve"] * 4 + ["dve"] * 4
        NU, NA, ND = len(USES), total(USES, "act"), total(USES, "dve")
        Q0, K0, V0, Y0 = 4, 6, 8, 12
        block = ctx.enter_context(nc.Block())

        def wait_emptied(eng, i, n):
            if USES[n] == "act":
                eng.wait_ge(S["by_act"], i * NA + drained(USES, n))
            else:
                eng.wait_ge(S["by_dve"], i * ND + drained(USES, n))

        def heads(u):
            b = u % NB
            return [2 * b, 2 * b + 1, 8 + 2 * b, 9 + 2 * b]

        if ctx_dram is not None:
            @block.sync
            def _(sp):
                sp.dma_start(cT[:], ctx_dram[:, :, 0:GT].rearrange("k p t -> p k t")).then_inc(S["ctx_in"], 16)
                if M is not None:
                    split_load(sp, M)
                with sp.Fori(1, NG) as i:
                    if M is not None:
                        pieces_load(sp, M, i - 1)
                    sp.wait_ge(S["full"], (i - 1) * NU + Y0)
                    sp.dma_start(cT[:], ctx_dram[:, :, bass.ds(i * GT, GT)].rearrange("k p t -> p k t")).then_inc(S["ctx_in"], 16)
                if M is not None:
                    pieces_load(sp, M, NG - 1)
                    sp.wait_ge(M["s"]["cleared"], 16)

        @block.gpsimd
        def _(pool):
            pool.memset(vp[:], 0.0).then_inc(S["zeros"], 1)
            pool.wait_ge(K["s"]["weights"], 16 * K["n_weights"])
            if M is not None:
                pool.memset(M["zero"][:], 0.0).then_inc(M["s"]["zeroed"], 1)
                pool.wait_ge(M["s"]["zeroed"], 1)
                pool.sem_inc(M["s"]["w_lo"], 2)
            with pool.Fori(0, NG) as i:
                norm_pool(pool, S, B, K, i)
                bias_pool(pool, S, xs, W["bo"], i)
                if M is not None:
                    pieces_split(pool, M, i)

        def resid(dve, i, t):
            n = Y0 + t
            dve.wait_ge(S["full"], i * NU + n + 1)
            dve.wait_ge(S["biased"], i * TG + t + 1)
            dve.tensor_tensor(tile_of(xs, i, t), tile_of(xs, i, t), mx[n % 2][:, 0:C], ALU.add).then_inc(S["by_dve"], 1)

        @block.vector
        def _(dve):
            dve.wait_ge(S["zeros"], 1)
            dve.wait_ge(K["s"]["weights"], 16 * K["n_weights"])
            with dve.Fori(0, NG) as i:
                norm_vector(dve, S, B, xs, i)
                for c in range(KC):
                    dve.wait_ge(S["full"], i * NU + K0 + c + 1)
                    for par in range(2):
                        op = dve.tensor_scalar(kk[:, c, :, par, :], mx[(K0 + c) % 2][:].rearrange("p (t n) -> p t n", t=TG),
                                               W["bk"][:, c:c + 1], K["evenodd"][:, par:par + 1], ALU.add, ALU.mult)
                    op.then_inc(S["by_dve"], 1)
                for t in range(TG):
                    dve.wait_ge(S["full"], i * NU + V0 + t + 1)
                    for par in range(2):
                        op = dve.tensor_tensor(
                            vp[:, t].rearrange("p (j r) d -> p j r d", r=2)[:, :, par, par * HD:(par + 1) * HD],
                            mx[(V0 + t) % 2][:, 0:C].rearrange("p (j r d) -> p j r d", r=2, d=HD)[:, :, par, :],
                            W["bv"][:].rearrange("p (j r d) -> p j r d", r=2, d=HD)[:, :, par, :], ALU.add)
                    op.then_inc(S["by_dve"], 1)
                for s in range(UN + 6):
                    if s < UN:
                        u = s
                        dve.wait_ge(S["scored"], i * UN + u + 1)
                        dve.tensor_reduce(nm[:, u % 2, :], sc[u % 2][:], AX.X, ALU.max, negate=True).then_inc(S["maxed"], 1)
                    if 0 <= s - 1 < UN:
                        u = s - 1
                        dve.wait_ge(S["exped"], i * UN + u + 1)
                        dve.tensor_reduce(z[:, u % 2, :], p[:, u % 2], AX.X, ALU.add).then_inc(S["summed"], 1)
                        dve.wait_ge(S["summed"], i * UN + u + 1)
                        dve.reciprocal(rz[:, u % 2, :], z[:, u % 2, :]).then_inc(S["zinv"], 1)
                        dve.wait_ge(S["zinv"], i * UN + u + 1)
                        dve.tensor_tensor(p[:, u % 2], p[:, u % 2], rz[:, u % 2, :].unsqueeze(2).to_broadcast([P, 4, P]),
                                          ALU.mult).then_inc(S["scaled"], 1)
                    if s >= 9 and (s - 9) % 4 == 0:
                        resid(dve, i, (s - 9) // 4)

        @block.scalar
        def _(act):
            act.wait_ge(K["s"]["weights"], 16 * K["n_weights"])
            act.activation(bq[:], W["bq"][:], ACT.Copy, scale=HD ** -0.5).then_inc(S["bq"], 1)
            act.wait_ge(S["bq"], 1)
            with act.Fori(0, NG) as i:
                for t in range(TG):
                    act.wait_ge(S["full"], i * NU + t + 1)
                    act.activation(xnT[:, :, t * P:(t + 1) * P], mx[t % 2][:, 0:C].rearrange("p (a b) -> p a b", a=KC),
                                   ACT.Copy).then_inc(S["by_act"], 1)
                for c in range(KC):
                    act.wait_ge(S["full"], i * NU + Q0 + c + 1)
                    act.activation(qT[:, c, :], mx[(Q0 + c) % 2][:], ACT.Identity, bias=bq[:, c:c + 1],
                                   scale=HD ** -0.5).then_inc(S["by_act"], 1)

                for s in range(UN + 4):
                    if s < UN:
                        u = s
                        act.wait_ge(S["maxed"], i * UN + u + 1)
                        if u >= 2:
                            act.wait_ge(S["pt_full"], i * UN + u - 1)
                        for j in range(4):
                            op = act.activation(p[:, u % 2, j, :], sc[u % 2][:, j, :], ACT.Exp, bias=nm[:, u % 2, j:j + 1])
                        op.then_inc(S["exped"], 1)
                    if 0 <= s - 2 < UN:
                        u = s - 2
                        act.wait_ge(S["pt_full"], i * UN + u + 1)
                        if u >= 2:
                            act.wait_ge(S["pv"], i * UN + u - 1)
                        act.activation(pT[:, u % 2], tp[u % 2][:], ACT.Copy).then_inc(S["pt"], 1)
                    if s >= 7 and (s - 7) % 4 == 0:
                        t = (s - 7) // 4
                        act.wait_ge(S["pv"], i * UN + 4 * t + 4)
                        act.activation(yT[:], py[t % 2][:], ACT.Copy).then_inc(S["yT"], 1)

        @block.tensor
        def _(pe):
            pe.wait_ge(K["s"]["weights"], 16 * K["n_weights"])
            pe.wait_ge(K["s"]["consts"], K["n_consts"])
            pe.wait_ge(S["zeros"], 1)
            with pe.Fori(0, NG) as i:
                for t in range(TG):
                    pe.wait_ge(S["normed"], i * TG + t + 1)
                    if t >= 2:
                        wait_emptied(pe, i, t - 2)
                    for c in range(KC):
                        op = pe.transpose(mx[t % 2][:, c * P:(c + 1) * P], B["xn"][:, t, c * P:(c + 1) * P], K["ident"][:])
                    op.then_inc(S["full"], 1)
                wait_emptied(pe, i, 3)
                if ctx_dram is not None:
                    pe.wait_ge(S["ctx_in"], i * 16 + 16)
                for what, src, n0 in (("wq", xnT, Q0), ("wk", cT, K0)):
                    for c in range(KC):
                        n = n0 + c
                        wait_emptied(pe, i, n - 2)
                        for kc in range(KC):
                            op = pe.matmul(mx[n % 2][:], W[what][:, kc, c * P:(c + 1) * P], src[:, kc, :],
                                           start=(kc == 0), stop=(kc == KC - 1))
                        op.then_inc(S["full"], 1)
                for t in range(TG):
                    n = V0 + t
                    wait_emptied(pe, i, n - 2)
                    for kc in range(KC):
                        op = pe.matmul(mx[n % 2][:, 0:C], cT[:, kc, t * P:(t + 1) * P], W["wv"][:, kc, :],
                                       start=(kc == 0), stop=(kc == KC - 1))
                    op.then_inc(S["full"], 1)

                def project(t):
                    n = Y0 + t
                    pe.wait_ge(S["yT"], i * TG + t + 1)
                    wait_emptied(pe, i, n - 2)
                    for kc in range(KC):
                        op = pe.matmul(mx[n % 2][:, 0:C], yT[:, kc, :], W["wo"][:, kc, :],
                                       start=(kc == 0), stop=(kc == KC - 1))
                    op.then_inc(S["full"], 1)

                for s in range(UN + 6):
                    if s < UN:
                        u, t, b = s, s // NB, s % NB
                        if u == 0:
                            wait_emptied(pe, i, V0 + 3)
                        if u >= 2:
                            pe.wait_ge(S["exped"], i * UN + u - 1)
                        if causal:
                            pe.matmul(sc[u % 2][:], K["identb"][:], K["causal"][:], start=True, stop=True)
                        for c in range(KC):
                            r = slice(32 * b, 32 * b + 32)
                            op = pe.matmul(sc[u % 2][:, 2 * c:2 * c + 2, :], qT[r, c, t * P:(t + 1) * P],
                                           kk[r, c, t, :, :], start=not causal, stop=True,
                                           tile_position=(32 * b, 0), skip_group_check=causal)
                        op.then_inc(S["scored"], 1)
                    if 0 <= s - 2 < UN:
                        u = s - 2
                        pe.wait_ge(S["scaled"], i * UN + u + 1)
                        if u >= 2:
                            pe.wait_ge(S["pt"], i * UN + u - 1)
                        for j in range(4):
                            op = pe.transpose(tp[u % 2][:, j, :], p[:, u % 2, j, :], K["ident"][:])
                        op.then_inc(S["pt_full"], 1)
                    if 0 <= s - 3 < UN:
                        u = s - 3
                        t, b = u // NB, u % NB
                        pe.wait_ge(S["pt"], i * UN + u + 1)
                        if b == 0 and t >= 2:
                            pe.wait_ge(S["yT"], i * TG + t - 1)
                        for j, h in enumerate(heads(u)):
                            op = pe.matmul(py[t % 2][32 * b:32 * b + 32, j // 2, :], vp[:, t, h, :], pT[:, u % 2, j, :],
                                           start=(j % 2 == 0), stop=(j % 2 == 1), tile_position=(0, 32 * b))
                        op.then_inc(S["pv"], 1)
                    if s >= 8 and (s - 8) % 4 == 0 and (s - 8) // 4 < TG:
                        project((s - 8) // 4)



def head_attention(nc, K, xs, W, ctx_dram):
    NH, HD = 16, 16
    NV = 9
    with ExitStack() as ctx:
        def sb(n, s, d=F32):
            return ctx.enter_context(nc.sbuf_tensor("ha_" + n, s, d))

        def pb(n, s, d=F32):
            return ctx.enter_context(nc.psum_tensor("ha_" + n, s, d))

        B = norm_buffers(sb, "n")
        xnT = sb("xnT", [P, KC, GT])
        cT = sb("cT", [P, KC, GT])
        q = sb("q", [P, 2, NH, HD])
        k = sb("k", [P, 2, NH, HD])
        vT = sb("vT", [P, 2, HD, NH])
        qk = sb("qk", [P, NH, NH, HD])
        wv = sb("wv", [P, NH, HD, NH])
        sc = sb("sc", [P, 2, NH, NH])
        sh = sb("sh", [P, 2, NH, NH])
        w = sb("w", [P, 2, NH, NH])
        nm = sb("nm", [P, 2, NH])
        z = sb("z", [P, 2, NH])
        rz = sb("rz", [P, 2, NH])
        o = sb("o", [P, 2, NH, HD])
        y = sb("y", [P, 2, C])
        yT = sb("yT", [P, 2, KC, P])
        mx = [pb(f"mx{b}", [P, 512]) for b in range(2)]
        pq = [pb(f"pq{b}", [P, 512]) for b in range(2)]
        pk = [pb(f"pk{b}", [P, 512]) for b in range(2)]
        py = pb("py", [P, 512])
        po = pb("po", [P, 512])
        S = named_semaphores(ctx, nc, "ha", NORM_SEMS + " ctx_in full emptied q_full k_full q_taken k_taken qk_dve qk_pool scored maxed"
                  " shifted weighed wv_dve wv_pool summed zed zinv y_ready turned yT out added")
        block = ctx.enter_context(nc.Block())

        def qk_product(eng, b, lo, hi):
            n = hi - lo
            return eng.tensor_tensor(qk[:, lo:hi], q[:, b, lo:hi].unsqueeze(2).to_broadcast([P, n, NH, HD]),
                                     k[:, b].unsqueeze(1).to_broadcast([P, n, NH, HD]), ALU.mult)

        def wv_product(eng, b, lo, hi):
            n = hi - lo
            return eng.tensor_tensor(wv[:, lo:hi], w[:, b, lo:hi].unsqueeze(2).to_broadcast([P, n, HD, NH]),
                                     vT[:, b].unsqueeze(1).to_broadcast([P, n, HD, NH]), ALU.mult)

        @block.sync
        def _(sp):
            sp.dma_start(cT[:], ctx_dram[:, :, 0:GT].rearrange("k p t -> p k t")).then_inc(S["ctx_in"], 16)
            with sp.Fori(1, NG) as i:
                sp.wait_ge(S["k_full"], i * TG)
                sp.dma_start(cT[:], ctx_dram[:, :, bass.ds(i * GT, GT)].rearrange("k p t -> p k t")).then_inc(S["ctx_in"], 16)

        @block.gpsimd
        def _(pool):
            pool.wait_ge(K["s"]["x"], 16 * NG)
            pool.wait_ge(K["s"]["weights"], 16 * K["n_weights"])
            pool.wait_ge(K["s"]["consts"], K["n_consts"])
            with pool.Fori(0, NG) as i:
                norm_pool(pool, S, B, K, i)
                bias_pool(pool, S, xs, W["bo"], i)
                for s in range(TG + 1):
                    if s < TG:
                        t = s
                        pool.wait_ge(S["q_taken"], i * TG + t + 1)
                        pool.wait_ge(S["k_taken"], i * TG + t + 1)
                        if t >= 1:
                            pool.wait_ge(S["scored"], i * TG + t)
                        qk_product(pool, t % 2, NV, NH).then_inc(S["qk_pool"], 1)
                    if s >= 1:
                        t = s - 1
                        pool.wait_ge(S["weighed"], i * TG + t + 1)
                        if t >= 1:
                            pool.wait_ge(S["summed"], i * TG + t)
                        wv_product(pool, t % 2, NV, NH).then_inc(S["wv_pool"], 1)

        def added(dve, i, t):
            dve.wait_ge(S["out"], i * TG + t + 1)
            dve.wait_ge(S["biased"], i * TG + t + 1)
            dve.tensor_tensor(tile_of(xs, i, t), tile_of(xs, i, t), po[:, 0:C], ALU.add).then_inc(S["added"], 1)

        @block.vector
        def _(dve):
            dve.wait_ge(K["s"]["x"], 16 * NG)
            dve.wait_ge(K["s"]["weights"], 16 * K["n_weights"])
            dve.wait_ge(K["s"]["consts"], K["n_consts"])
            with dve.Fori(0, NG) as i:
                norm_vector(dve, S, B, xs, i)
                for s in range(TG + 2):
                    if s < TG:
                        t, b = s, s % 2
                        dve.wait_ge(S["q_full"], i * TG + t + 1)
                        dve.tensor_tensor(q[:, b].rearrange("p h d -> p (h d)"), pq[b][:, 0:C], W["bq"][:],
                                          ALU.add).then_inc(S["q_taken"], 1)
                        dve.wait_ge(S["k_full"], i * TG + t + 1)
                        dve.tensor_tensor(k[:, b].rearrange("p h d -> p (h d)"), pk[b][:, 0:C], W["bk"][:], ALU.add)
                        dve.tensor_tensor(vT[:, b], pk[b][:, C:2 * C].rearrange("p (h d) -> p d h", h=NH),
                                          W["bv"][:].rearrange("p (h d) -> p d h", h=NH), ALU.add).then_inc(S["k_taken"], 1)
                        dve.wait_ge(S["k_taken"], i * TG + t + 1)
                        qk_product(dve, b, 0, NV).then_inc(S["qk_dve"], 1)
                    if 0 <= s - 1 < TG:
                        t, b = s - 1, (s - 1) % 2
                        dve.wait_ge(S["weighed"], i * TG + t + 1)
                        wv_product(dve, b, 0, NV).then_inc(S["wv_dve"], 1)
                        dve.tensor_reduce(z[:, b, :], w[:, b], AX.X, ALU.add).then_inc(S["zed"], 1)
                    if s < TG:
                        t, b = s, s % 2
                        dve.wait_ge(S["qk_dve"], i * TG + t + 1)
                        dve.wait_ge(S["qk_pool"], i * TG + t + 1)
                        dve.tensor_reduce(sc[:, b], qk[:], AX.X, ALU.add).then_inc(S["scored"], 1)
                        dve.wait_ge(S["scored"], i * TG + t + 1)
                        dve.tensor_reduce(nm[:, b, :], sc[:, b], AX.X, ALU.max, negate=True).then_inc(S["maxed"], 1)
                        dve.wait_ge(S["maxed"], i * TG + t + 1)
                        dve.tensor_tensor(sh[:, b], sc[:, b], nm[:, b, :].unsqueeze(2).to_broadcast([P, NH, NH]),
                                          ALU.add).then_inc(S["shifted"], 1)
                    if 0 <= s - 1 < TG:
                        t, b = s - 1, (s - 1) % 2
                        dve.wait_ge(S["zed"], i * TG + t + 1)
                        dve.reciprocal(rz[:, b, :], z[:, b, :]).then_inc(S["zinv"], 1)
                        dve.wait_ge(S["wv_dve"], i * TG + t + 1)
                        dve.wait_ge(S["wv_pool"], i * TG + t + 1)
                        dve.tensor_reduce(o[:, b], wv[:], AX.X, ALU.add).then_inc(S["summed"], 1)
                        dve.wait_ge(S["zinv"], i * TG + t + 1)
                        dve.wait_ge(S["summed"], i * TG + t + 1)
                        dve.tensor_tensor(y[:, b, :].rearrange("p (h d) -> p h d", h=NH), o[:, b],
                                          rz[:, b, :].unsqueeze(2).to_broadcast([P, NH, HD]), ALU.mult).then_inc(S["y_ready"], 1)
                    if 0 <= s - 2 < TG:
                        added(dve, i, s - 2)

        @block.scalar
        def _(act):
            with act.Fori(0, NG) as i:
                for t in range(TG):
                    act.wait_ge(S["full"], i * TG + t + 1)
                    act.activation(xnT[:, :, t * P:(t + 1) * P], mx[t % 2][:, 0:C].rearrange("p (a b) -> p a b", a=KC),
                                   ACT.Copy).then_inc(S["emptied"], 1)
                for s in range(TG + 1):
                    if s < TG:
                        t = s
                        act.wait_ge(S["shifted"], i * TG + t + 1)
                        act.activation(w[:, t % 2], sh[:, t % 2], ACT.Exp, scale=HD ** -0.5).then_inc(S["weighed"], 1)
                    if s >= 1:
                        t = s - 1
                        act.wait_ge(S["turned"], i * TG + t + 1)
                        act.activation(yT[:, t % 2], py[:, 0:C].rearrange("p (a b) -> p a b", a=KC),
                                       ACT.Copy).then_inc(S["yT"], 1)

        @block.tensor
        def _(pe):
            pe.wait_ge(K["s"]["x"], 16 * NG)
            pe.wait_ge(K["s"]["weights"], 16 * K["n_weights"])
            pe.wait_ge(K["s"]["consts"], K["n_consts"])
            with pe.Fori(0, NG) as i:
                for t in range(TG):
                    pe.wait_ge(S["normed"], i * TG + t + 1)
                    if t >= 2:
                        pe.wait_ge(S["emptied"], i * TG + t - 1)
                    for c in range(KC):
                        op = pe.transpose(mx[t % 2][:, c * P:(c + 1) * P], B["xn"][:, t, c * P:(c + 1) * P], K["ident"][:])
                    op.then_inc(S["full"], 1)
                pe.wait_ge(S["ctx_in"], i * 16 + 16)
                for s in range(TG + 1):
                    if s < TG:
                        t, b = s, s % 2
                        pe.wait_ge(S["emptied"], i * TG + t + 1)
                        if t >= 2:
                            pe.wait_ge(S["k_taken"], i * TG + t - 1)
                        for kc in range(KC):
                            op = pe.matmul(pq[b][:, 0:C], xnT[:, kc, t * P:(t + 1) * P], W["wq"][:, kc, :],
                                           start=(kc == 0), stop=(kc == KC - 1))
                        op.then_inc(S["q_full"], 1)
                        for kc in range(KC):
                            op = pe.matmul(pk[b][:], cT[:, kc, t * P:(t + 1) * P], W["wkv"][:, kc, :],
                                           start=(kc == 0), stop=(kc == KC - 1))
                        op.then_inc(S["k_full"], 1)
                    if s >= 1:
                        t, b = s - 1, (s - 1) % 2
                        pe.wait_ge(S["y_ready"], i * TG + t + 1)
                        if t >= 1:
                            pe.wait_ge(S["yT"], i * TG + t)
                        for c in range(KC):
                            op = pe.transpose(py[:, c * P:(c + 1) * P], y[:, b, c * P:(c + 1) * P], K["ident"][:])
                        op.then_inc(S["turned"], 1)
                        pe.wait_ge(S["yT"], i * TG + t + 1)
                        if t >= 1:
                            pe.wait_ge(S["added"], i * TG + t)
                        for kc in range(KC):
                            op = pe.matmul(po[:, 0:C], yT[:, b, kc, :], W["wo"][:, kc, :],
                                           start=(kc == 0), stop=(kc == KC - 1))
                        op.then_inc(S["out"], 1)



def plan_buffers(sb, pb, NE):
    return dict(pre=sb("pre", [P, NT, NE]), cnt=sb("cnt", [P, NE]), more=sb("more", [P, NE, NT]), nb=sb("nb", [P, NE]),
                e0=sb("e0", [P, NE]), e1=sb("e1", [P, NE]), base=sb("base", [P, NE]), k1=sb("k1", [P, NT, NE]),
                k2=sb("k2", [P, NT, NE]), key=sb("key", [P, NT, NE]), p8=sb("p8", [P, NT, 8]), eq=sb("eq", [P, NT, NE]),
                eq2=sb("eq2", [P, NT, NE]),
                past=sb("past", [1, 64, NE]), owner=sb("owner", [1, 64]),
                before=pb("before", [P, NT * NE]), per_tile=pb("per_tile", [P, NT * NE]))


def plan_vector(dve, S, L, K, M, NE):
    n = [0]

    def link(op):
        n[0] += 1
        op.then_inc(S["plan"], 1)
        dve.wait_ge(S["plan"], n[0])

    def over_tiles(ap):
        return ap.unsqueeze(1).to_broadcast([P, NT, NE])

    per_tile = L["per_tile"][:].rearrange("p (t e) -> p t e", e=NE)
    dve.wait_ge(S["counted"], 1)
    link(dve.memset(L["pre"][:, 0, :], 0.0))
    for t in range(1, NT):
        link(dve.tensor_tensor(L["pre"][:, t, :], L["pre"][:, t - 1, :], per_tile[:, t - 1, :], ALU.add))
    link(dve.tensor_tensor(L["cnt"][:], L["pre"][:, NT - 1, :], per_tile[:, NT - 1, :], ALU.add))
    link(dve.tensor_tensor(L["more"][:], L["cnt"][:].unsqueeze(2).to_broadcast([P, NE, NT]),
                           K["steps"][:, 0:NT].unsqueeze(1).to_broadcast([P, NE, NT]), ALU.is_gt))
    link(dve.tensor_reduce(L["nb"][:], L["more"][:], AX.X, ALU.add))
    src, dst = L["nb"], L["e0"]
    d = 1
    while d < NE:
        dve.tensor_copy(dst[:, 0:d], src[:, 0:d])
        link(dve.tensor_tensor(dst[:, d:], src[:, d:], src[:, 0:NE - d], ALU.add))
        src, dst = dst, (L["e1"] if dst is L["e0"] else L["e0"])
        d *= 2
    end = src
    link(dve.tensor_tensor(L["base"][:], end[:], L["nb"][:], ALU.subtract))
    link(dve.tensor_scalar(dst[:], L["base"][:], float(P), None, ALU.mult))
    base = dst
    link(dve.tensor_tensor(L["k1"][:], L["pre"][:], L["before"][:].rearrange("p (t e) -> p t e", e=NE), ALU.add))
    link(dve.tensor_tensor(L["k2"][:], L["k1"][:], over_tiles(base[:]), ALU.add))
    link(dve.scalar_tensor_tensor(out=L["k1"][:], in0=L["k2"][:], scalar=1.0, in1=M["sel"][:], op0=ALU.add, op1=ALU.mult))
    link(dve.tensor_scalar(L["key"][:], L["k1"][:], -1.0, None, ALU.add))
    for t in range(NT):
        op = dve.max(L["p8"][:, t, :], L["key"][:, t, :])
    link(op)
    dve.tensor_copy(M["place"][:], L["p8"][:]).then_inc(S["placed"], 1)
    nb = M["NB"]
    link(dve.tensor_tensor(L["past"][:, 0:nb, :], K["blocks"][0:1, 0:nb].unsqueeze(2).to_broadcast([1, nb, NE]),
                           end[0:1, :].unsqueeze(1).to_broadcast([1, nb, NE]), ALU.is_ge))
    link(dve.tensor_reduce(L["owner"][:, 0:nb], L["past"][:, 0:nb, :], AX.X, ALU.add))
    link(dve.tensor_scalar(M["owner"][:], L["owner"][:, 0:nb], float(NE - 1), None, ALU.min))
    for c in range(M["TOP"]):
        link(dve.tensor_tensor(L["eq"][:], L["key"][:], L["p8"][:, :, c:c + 1].to_broadcast([P, NT, NE]), ALU.is_equal))
        link(dve.tensor_tensor(L["eq2"][:], L["eq"][:], M["rw"][:], ALU.mult))
        link(dve.tensor_reduce(M["pw"][:, :, c:c + 1], L["eq2"][:], AX.X, ALU.add))



def split_load(sp, M):
    s = M["s"]
    sp.wait_ge(s["zeroed"], 1)
    sp.dma_start(M["sent"].rearrange("(b p) c -> p b c", p=P),
                 M["zero"][:].unsqueeze(1).to_broadcast([P, M["NB"], C])).then_inc(s["cleared"], 16)
    sp.dma_start(M["b1"][:], M["b1_dram"].rearrange("e p j -> p e j")).then_inc(s["b1"], 16)


def pieces_load(sp, M, i):
    n = M["PIECES"] // NG
    for q in range(n):
        sp.wait_ge(M["s"]["w_lo"], i * n + q + 1)
        sp.dma_start(M["stage"][:, q % 2, :], M["pieces"][bass.ds(i * n + q, 1)].rearrange("a p n -> p (a n)")).then_inc(M["w_in"][q % 2], 16)


def pieces_split(pool, M, i):
    n = M["PIECES"] // NG
    s = M["s"]

    def held(k):
        pool.tensor_tensor(M["junk"][:, k:k + 1], M["zero"][:, 0:1], M["zero"][:, 1:2], ALU.add)

    for q in range(n):
        at = bass.ds(i * n + q, 1)
        stage = M["stage"][:, q % 2, :]
        wh = M["wh"][:, at, :].rearrange("p a n -> p (a n)")
        wl = M["wl"][:, at, :].rearrange("p a n -> p (a n)")
        pool.wait_ge(M["w_in"][q % 2], i * (n // 2 * 16) + (q // 2 + 1) * 16)
        held(q % 2 * 2)
        pool.tensor_copy(wh, stage).then_inc(s["w_hi"], 1)
        pool.wait_ge(s["w_hi"], i * n + q + 1)
        held(q % 2 * 2 + 1)
        pool.tensor_tensor(wl, stage, wh, ALU.subtract).then_inc(s["w_lo"], 1)


def route(nc, K, xs, R, pre, NE, TOP, NR, M):
    NS = 8 - TOP
    l0 = NE == NR
    with ExitStack() as ctx:
        def sb(n, s, d=F32):
            return ctx.enter_context(nc.sbuf_tensor(f"{pre}_{n}", s, d))

        def pb(n, s, d=F32):
            return ctx.enter_context(nc.psum_tensor(f"{pre}_{n}", s, d))

        B = norm_buffers(sb, "n")
        xnT = sb("xnT", [P, KC, GT])
        nm = sb("nm", [P, TG])
        sh = sb("sh", [P, TG, NE])
        ex = sb("ex", [P, TG, NE])
        z = sb("z", [P, TG])
        rz = sb("rz", [P, TG])
        pr = sb("pr", [P, TG, NE])
        cand = sb("cand", [P, TG, NE + NS])
        top8 = sb("top8", [P, TG, 8])
        pick = sb("pick", [P, TG, 8])
        mark = sb("mark", [P, TG, NE + NS])
        wt = sb("wt", [P, TG, NE])
        zs = sb("zs", [P, TG])
        ze = sb("ze", [P, TG])
        cw = sb("cw", [P, TG, NE])
        cwT = sb("cwT", [NE, TG, P])
        mx = [pb(f"mx{b}", [P, 512]) for b in range(2)]
        lg = pb("lg", [P, TG, NE])
        pt = pb("pt", [NE, TG, P])
        pbias = [pb(f"pbias{b}", [P, 512]) for b in range(2)]
        CH = 13 if l0 else 11
        if l0:
            plan = plan_buffers(sb, pb, NE)
        S = named_semaphores(ctx, nc, pre, NORM_SEMS + " consts full emptied logits shifted exped chain topped marked weighed cw_turned"
                  " cwT bias added counted plan placed scattered")
        block = ctx.enter_context(nc.Block())

        @block.gpsimd
        def _(pool):
            pool.wait_ge(K["s"]["x"], 16 * NG)
            pool.wait_ge(K["s"]["weights"], 16 * K["n_weights"])
            pool.wait_ge(K["s"]["consts"], K["n_consts"])
            with pool.Fori(0, NG) as i:
                norm_pool(pool, S, B, K, i)
            if l0:
                pool.wait_ge(S["placed"], 1)
                pool.wait_ge(S["emptied"], NT)
                for t in range(NT):
                    for c in range(TOP):
                        pool.indirect_dma_start(
                            out=M["sent"], out_offset=bass.IndirectOffsetOnAxis(ap=M["place"][:, t, c:c + 1], axis=0),
                            in_=M["xn"][:, t, :], in_offset=None, bounds_check=M["NB"] * P - 1,
                            oob_is_err=False).then_inc(S["scattered"], 16)
                pool.wait_ge(S["scattered"], 16 * NT * TOP)


        @block.vector
        def _(dve):
            dve.wait_ge(K["s"]["x"], 16 * NG)
            dve.wait_ge(K["s"]["weights"], 16 * K["n_weights"])
            dve.wait_ge(K["s"]["consts"], K["n_consts"])
            dve.memset(cand[:, :, NE:], FAR)
            dve.memset(pick[:, :, TOP:], FAR).then_inc(S["consts"], 1)
            dve.wait_ge(S["consts"], 1)
            with dve.Fori(0, NG) as i:
                step = [0]

                def link(op):
                    step[0] += 1
                    op.then_inc(S["chain"], 1)
                    dve.wait_ge(S["chain"], i * CH + step[0])

                norm_vector(dve, S, B, xs, i)
                for t in range(0 if l0 else TG):
                    dve.wait_ge(S["emptied"], i * TG + t + 1)
                    at = bass.ds(i * GT + t * P, P)
                    dve.tensor_tensor(M["xl"][:, :, at], xnT[:, :, t * P:(t + 1) * P], M["xh"][:, :, at], ALU.subtract)
                dve.wait_ge(S["logits"], i + 1)
                link(dve.tensor_reduce(nm[:], lg[:], AX.X, ALU.max, negate=True))
                dve.tensor_tensor(sh[:], lg[:], nm[:].unsqueeze(2).to_broadcast([P, TG, NE]), ALU.add).then_inc(S["shifted"], 1)
                dve.wait_ge(S["exped"], i + 1)
                link(dve.tensor_reduce(z[:], ex[:], AX.X, ALU.add))
                link(dve.reciprocal(rz[:], z[:]))
                link(dve.tensor_tensor(pr[:], ex[:], rz[:].unsqueeze(2).to_broadcast([P, TG, NE]), ALU.mult))
                if l0:
                    link(dve.tensor_copy(cand[:, :, 0:NE], pr[:]))
                else:
                    link(dve.tensor_tensor(cand[:, :, 0:NE], pr[:], R["corr"][:].unsqueeze(1).to_broadcast([P, TG, NE]), ALU.add))
                dve.memset(B["junk"][:], 0.0)
                for t in range(TG):
                    op = dve.max(top8[:, t, :], cand[:, t, 0:NE])
                link(op)
                link(dve.tensor_copy(pick[:, :, 0:TOP], top8[:, :, 0:TOP]))
                dve.memset(B["junk"][:], 0.0)
                for t in range(TG):
                    op = dve.match_replace(mark[:, t, :], pick[:, t, :], cand[:, t, :], -FAR)
                link(op)
                if l0:
                    link(dve.scalar_tensor_tensor(out=wt[:], in0=mark[:, :, 0:NE], scalar=-FAR, in1=pr[:],
                                                  op0=ALU.is_equal, op1=ALU.mult))
                    link(dve.tensor_reduce(zs[:], wt[:], AX.X, ALU.add))
                    link(dve.tensor_scalar(ze[:], zs[:], 1e-8, None, ALU.add))
                    link(dve.reciprocal(zs[:], ze[:]))
                    link(dve.tensor_tensor(cw[:], wt[:], zs[:].unsqueeze(2).to_broadcast([P, TG, NE]), ALU.mult))
                    dve.tensor_copy(M["rw"][:, bass.ds(i * TG, TG), :], cw[:])
                    dve.tensor_scalar(M["sel"][:, bass.ds(i * TG, TG), :], mark[:, :, 0:NE], -FAR, None,
                                      ALU.is_equal).then_inc(S["weighed"], 1)
                    for t in range(TG):
                        dve.wait_ge(S["bias"], i * TG + t + 1)
                        dve.tensor_tensor(tile_of(xs, i, t), tile_of(xs, i, t), pbias[t % 2][:, 0:C], ALU.add).then_inc(S["added"], 1)
                else:
                    link(dve.scalar_tensor_tensor(out=wt[:], in0=mark[:, :, 0:NE], scalar=-FAR, in1=pr[:],
                                                  op0=ALU.is_equal, op1=ALU.mult))
                    link(dve.tensor_scalar(M["rw"][:, bass.ds(i * TG, TG), :], wt[:], R["scale"], None, ALU.mult))
                    link(dve.tensor_reduce(zs[:], M["rw"][:, bass.ds(i * TG, TG), NR:NE], AX.X, ALU.add))
                    for t in range(TG):
                        dve.scalar_tensor_tensor(out=tile_of(xs, i, t), in0=B["xn"][:, t, :], scalar=zs[:, t:t + 1],
                                                 in1=tile_of(xs, i, t), op0=ALU.mult, op1=ALU.add).then_inc(S["added"], 1)
                assert step[0] == CH, step[0]
            if l0:
                plan_vector(dve, S, plan, K, M, NE)

        @block.scalar
        def _(act):
            with act.Fori(0, NG) as i:
                for t in range(TG):
                    act.wait_ge(S["full"], i * TG + t + 1)
                    src = mx[t % 2][:, 0:C].rearrange("p (a b) -> p a b", a=KC)
                    act.activation(xnT[:, :, t * P:(t + 1) * P], src, ACT.Copy)
                    if l0:
                        op = act.activation(tile_of(M["xn"], i, t), B["xn"][:, t, :], ACT.Copy)
                    else:
                        op = act.activation(M["xh"][:, :, bass.ds(i * GT + t * P, P)], src, ACT.Copy)
                    op.then_inc(S["emptied"], 1)
                act.wait_ge(S["shifted"], i + 1)
                act.activation(ex[:], sh[:], ACT.Exp).then_inc(S["exped"], 1)
                if l0:
                    act.wait_ge(S["cw_turned"], i + 1)
                    act.activation(cwT[:], pt[:], ACT.Copy).then_inc(S["cwT"], 1)

        @block.tensor
        def _(pe):
            pe.wait_ge(K["s"]["x"], 16 * NG)
            pe.wait_ge(K["s"]["weights"], 16 * K["n_weights"])
            pe.wait_ge(K["s"]["consts"], K["n_consts"])
            with pe.Fori(0, NG) as i:
                for t in range(TG):
                    pe.wait_ge(S["normed"], i * TG + t + 1)
                    if t >= 2:
                        pe.wait_ge(S["emptied"], i * TG + t - 1)
                    for c in range(KC):
                        op = pe.transpose(mx[t % 2][:, c * P:(c + 1) * P], B["xn"][:, t, c * P:(c + 1) * P], K["ident"][:])
                    op.then_inc(S["full"], 1)
                for t in range(TG):
                    pe.wait_ge(S["emptied"], i * TG + t + 1)
                    for kc in range(KC):
                        op = pe.matmul(lg[:, t, :], xnT[:, kc, t * P:(t + 1) * P], R["w"][:, kc, :],
                                       start=(kc == 0), stop=(kc == KC - 1))
                op.then_inc(S["logits"], 1)
                if l0:
                    pe.wait_ge(S["weighed"], i + 1)
                    for t in range(TG):
                        op = pe.transpose(pt[:, t, :], cw[:, t, :], K["ident"][:])
                    op.then_inc(S["cw_turned"], 1)
                    pe.wait_ge(S["cwT"], i + 1)
                    for t in range(TG):
                        if t >= 2:
                            pe.wait_ge(S["added"], i * TG + t - 1)
                        pe.matmul(pbias[t % 2][:, 0:C], cwT[:, t, :], R["b2"][:], start=True, stop=True).then_inc(S["bias"], 1)
            if l0:
                sel = M["sel"][:].rearrange("p t e -> p (t e)")
                pe.matmul(plan["before"][:], K["earlier"][:], sel, start=True, stop=True)
                pe.matmul(plan["per_tile"][:], K["all1"][:], sel, start=True, stop=True).then_inc(S["counted"], 1)



def gelu_blocks(nc, K, M, NE, H):
    NB = M["NB"]
    HC, UC = H // P, 4
    BB = 4
    UB = HC // UC
    NU = BB * UB
    LEAD = 2
    with ExitStack() as ctx:
        def sb(n, s, d=F32):
            return ctx.enter_context(nc.sbuf_tensor("gb_" + n, s, d))

        def pb(n, s, d=F32):
            return ctx.enter_context(nc.psum_tensor("gb_" + n, s, d))

        xr = sb("xr", [P, BB, C])
        xh = sb("xh", [P, 4, KC, P], BF16)
        xl = sb("xl", [P, 4, KC, P], BF16)
        hb = sb("hb", [P, 2, UC, P])
        hf = sb("hf", [P, 2, UC, P])
        hh = sb("hh", [P, 4, UC, P], BF16)
        hl = sb("hl", [P, 4, UC, P], BF16)
        yr = sb("yr", [P, BB, C])
        W = {w: M[w][:].rearrange("p (h q) n -> p h (q n)", q=4) for w in ("wh", "wl")}
        px = [pb(f"px{b}", [P, 512]) for b in range(2)]
        ph = [pb(f"ph{b}", [P, UC, P]) for b in range(4)]
        py = [pb(f"py{b}", [P, 512]) for b in range(2)]
        S = named_semaphores(ctx, nc, "gb", "rows0 rows1 rows2 rows3 turned xhi xlo hid biased hi lo used y_out"
                             " stored0 stored1 stored2 stored3")
        rows = [S[f"rows{b}"] for b in range(BB)]
        stored = [S[f"stored{b}"] for b in range(BB)]
        block = ctx.enter_context(nc.Block())

        LAST = NB // BB - 1

        def bodies(eng, body):
            with eng.Fori(0, LAST) as i:
                body(i, False)
            body(LAST, True)

        def owner(eng, b):
            return eng.value_load(M["owner"][0:1, bass.ds(b, 1)], min_val=0, max_val=NE - 1)

        def store(sp, i, m):
            sp.wait_ge(S["y_out"], i * BB + m + 1 + 2)
            sp.dma_start(M["back"][bass.ds((i * BB + m) * P, P), :], yr[:, m, :]).then_inc(stored[m], 16)

        @block.sync
        def _(sp):
            for m in range(BB):
                sp.dma_start(xr[:, m, :], M["sent"][m * P:(m + 1) * P, :]).then_inc(rows[m], 16)
            with sp.Fori(1, NB // BB) as i:
                for m in range(BB):
                    sp.wait_ge(S["turned"], (i - 1) * BB + m + 1)
                    sp.dma_start(xr[:, m, :], M["sent"][bass.ds((i * BB + m) * P, P), :]).then_inc(rows[m], 16)
                    store(sp, i - 1, m)
            for m in range(BB):
                store(sp, LAST, m)
            for m in range(BB):
                sp.wait_ge(stored[m], 16 * (NB // BB + 1))

        @block.gpsimd
        def _(pool):
            pool.sem_inc(S["biased"], 4)
            pool.sem_inc(S["lo"], 2)
            pool.sem_inc(S["used"], 4)
            pool.sem_inc(S["y_out"], 2)
            for m in range(BB):
                pool.sem_inc(stored[m], 16)

        @block.vector
        def _(dve):
            def low_x(i, m):
                dve.wait_ge(S["xhi"], i * BB + m + 1)
                dve.tensor_tensor(xl[:, m % 4], px[m % 2][:, 0:C].rearrange("p (a b) -> p a b", a=KC), xh[:, m % 4],
                                  ALU.subtract).then_inc(S["xlo"], 1)

            def add_bias(i, u, e):
                dve.wait_ge(S["hid"], i * NU + u + 1)
                j = u % UB * UC
                b1 = M["b1"][:, bass.ds(e, 1), j:j + UC].rearrange("p a j -> p (a j)").unsqueeze(2).to_broadcast([P, UC, P])
                dve.tensor_tensor(hb[:, u % 2], ph[u % 4][:], b1, ALU.add).then_inc(S["biased"], 1)

            def low_h(i, u):
                dve.wait_ge(S["hi"], i * NU + u + 1)
                dve.tensor_tensor(hl[:, u % 4], hf[:, u % 2], hh[:, u % 4], ALU.subtract).then_inc(S["lo"], 1)

            def body(i, last):
                es = [owner(dve, i * BB + m) for m in range(BB + (not last))]
                for u in range(NU):
                    m = (u + 1) // UB
                    if u + 1 < NU or not last:
                        add_bias(i, u + 1, es[m])
                    low_h(i, u)
                    if u % UB == 0 and (u // UB + 2 < BB or not last):
                        low_x(i, u // UB + 2)

            low_x(0, 0)
            low_x(0, 1)
            add_bias(0, 0, owner(dve, 0))
            bodies(dve, body)

        @block.scalar
        def _(act):
            def high_x(i, m):
                act.wait_ge(S["turned"], i * BB + m + 1)
                act.activation(xh[:, m % 4], px[m % 2][:, 0:C].rearrange("p (a b) -> p a b", a=KC),
                               ACT.Copy).then_inc(S["xhi"], 1)

            def gelu(i, u):
                act.wait_ge(S["biased"], i * NU + u + 1 + 4)
                act.wait_ge(S["lo"], i * NU + u + 1)
                act.activation(hf[:, u % 2], hb[:, u % 2], ACT.Gelu_apprx_tanh)
                act.wait_ge(S["used"], i * NU + u + 1)
                act.activation(hh[:, u % 4], hb[:, u % 2], ACT.Gelu_apprx_tanh).then_inc(S["hi"], 1)

            def out_rows(i, m):
                act.wait_ge(stored[m], i * 16 + 16)
                act.wait_ge(S["used"], i * NU + (m + 1) * UB + 4)
                act.activation(yr[:, m, :], py[m % 2][:, 0:C], ACT.Copy).then_inc(S["y_out"], 1)

            def body(i, last):
                for m in range(BB):
                    if m + 1 < BB or not last:
                        for k in range(UB):
                            gelu(i, (m + 1) * UB + k)
                            if k == 0 and (m + 3 < BB or not last):
                                high_x(i, m + 3)
                    out_rows(i, m)

            high_x(0, 0)
            high_x(0, 1)
            for k in range(UB):
                gelu(0, k)
                if k == 0:
                    high_x(0, 2)
            bodies(act, body)

        @block.tensor
        def _(pe):
            def turn(i, m):
                pe.wait_ge(rows[m % BB], (i + m // BB) * 16 + 16)
                if m >= 2:
                    pe.wait_ge(S["xlo"], i * BB + m - 1)
                for c in range(KC):
                    op = pe.transpose(px[m % 2][:, c * P:(c + 1) * P], xr[:, m % BB, c * P:(c + 1) * P], K["ident"][:])
                op.then_inc(S["turned"], 1)

            def first(i, u, e):
                m = u // UB
                pe.wait_ge(S["xlo"], i * BB + m + 1)
                pe.wait_ge(S["biased"], i * NU + u + 1)
                for j in range(UC):
                    n = 0
                    for kc in range(KC):
                        at = kc * H + (u % UB * UC + j) * P
                        for w, x in (("wh", xh), ("wh", xl), ("wl", xh)):
                            op = pe.matmul(ph[u % 4][:, j, :], W[w][:, bass.ds(e * 2, 1), at:at + P].rearrange("p a n -> p (a n)"),
                                           x[:, m % 4, kc, :], start=(n == 0), stop=(n == 3 * KC - 1))
                            n += 1
                op.then_inc(S["hid"], 1)

            def second(i, u, e):
                m = u // UB
                if u % UB == 0:
                    pe.wait_ge(S["y_out"], i * BB + m + 1)
                pe.wait_ge(S["lo"], i * NU + u + 1 + 2)
                for j in range(UC):
                    at = (u % UB * UC + j) * C
                    for n, (h, w) in enumerate(((hh, "wh"), (hh, "wl"), (hl, "wh"))):
                        op = pe.matmul(py[m % 2][:, 0:C], h[:, u % 4, j, :],
                                       W[w][:, bass.ds(e * 2 + 1, 1), at:at + C].rearrange("p a n -> p (a n)"),
                                       start=(u % UB == 0 and j == 0 and n == 0),
                                       stop=(u % UB == UB - 1 and j == UC - 1 and n == 2))
                op.then_inc(S["used"], 1)

            def body(i, last):
                es = [owner(pe, i * BB + m) for m in range(BB + (not last))]
                for u in range(NU):
                    if u % UB == 0 and (u // UB + 2 < BB or not last):
                        turn(i, u // UB + 2)
                    if u + LEAD < NU or not last:
                        first(i, u + LEAD, es[(u + LEAD) // UB])
                    second(i, u, es[u // UB])

            e0 = owner(pe, 0)
            turn(0, 0)
            turn(0, 1)
            for u in range(LEAD):
                first(0, u, e0)
            bodies(pe, body)


def combine(nc, K, xs, M, loads, loaded):
    TOP = M["TOP"]
    with ExitStack() as ctx:
        got = ctx.enter_context(nc.sbuf_tensor("cb_got", [P, NT, TOP, C], F32))
        S = named_semaphores(ctx, nc, "cb", "got0 got1 got2 got3 sum")
        arrived = [S[f"got{g}"] for g in range(NG)]
        block = ctx.enter_context(nc.Block())

        @block.sync
        def _(sp):
            for dst, src in loads:
                sp.dma_start(dst[:], src).then_inc(loaded, 16)

        @block.gpsimd
        def _(pool):
            for t in range(NT):
                for c in range(TOP):
                    pool.indirect_dma_start(out=got[:, t, c, :], out_offset=None, in_=M["back"],
                                            in_offset=bass.IndirectOffsetOnAxis(ap=M["place"][:, t, c:c + 1], axis=0),
                                            bounds_check=M["NB"] * P - 1, oob_is_err=False).then_inc(arrived[t // TG], 16)

        @block.vector
        def _(dve):
            for g in range(NG):
                dve.wait_ge(arrived[g], 16 * TG * TOP)
                for c in range(TOP):
                    if c:
                        dve.wait_ge(S["sum"], (g * TOP + c) * TG)
                    for t in range(g * TG, g * TG + TG):
                        dve.scalar_tensor_tensor(out=xs[:, t, :], in0=got[:, t, c, :], scalar=M["pw"][:, t, c:c + 1], in1=xs[:, t, :],
                                                 op0=ALU.mult, op1=ALU.add).then_inc(S["sum"], 1)



def silu_experts(nc, K, xs, M, w_dram, NR, I):
    EB = 4
    NU = EB * NG
    WG, WD = KC * 2 * I, C
    NHB, NL = 4, 2
    with ExitStack() as ctx:
        def sb(n, s, d=F32):
            return ctx.enter_context(nc.sbuf_tensor("se_" + n, s, d))

        def pb(n, s, d=F32):
            return ctx.enter_context(nc.psum_tensor("se_" + n, s, d))

        stage = sb("stage", [P, EB, WG + WD])
        wh = sb("wh", [P, EB, WG + WD], BF16)
        wl = sb("wl", [P, EB, WG + WD], BF16)
        ew = sb("ew", [P, EB, NT])
        sg = sb("sg", [P, 2, GT])
        hf = sb("hf", [P, NHB, GT])
        hh = sb("hh", [P, NHB, GT], BF16)
        hl = sb("hl", [P, NHB, GT], BF16)
        pg = [pb(f"pg{b}", [P, GT]) for b in range(2)]
        pu = [pb(f"pu{b}", [P, GT]) for b in range(2)]
        py = [[pb(f"py{s}{b}", [P, 2, C]) for b in range(2)] for s in range(2)]
        S = named_semaphores(ctx, nc, "se", "w_in0 w_in1 w_in2 w_in3 w_hi w_lo picked gu silu prod hi lo used y_taken")
        w_in = [S["w_in0"], S["w_in1"], S["w_in2"], S["w_in3"]]
        block = ctx.enter_context(nc.Block())

        def wgu(buf, p, kc, half):
            return buf[:, p, kc * 2 * I + half * I:kc * 2 * I + (half + 1) * I]

        @block.sync
        def _(sp):
            for p in range(EB):
                sp.dma_start(stage[:, p, :], w_dram[p]).then_inc(w_in[p], 16)
            with sp.Fori(1, NR // EB) as i:
                for p in range(EB):
                    sp.wait_ge(S["w_hi"], (i - 1) * EB + p + 1)
                    sp.wait_ge(S["w_lo"], (i - 1) * EB + p + 1)
                    sp.dma_start(stage[:, p, :], w_dram[bass.ds(i * EB + p, 1)].rearrange("a p n -> p (a n)")).then_inc(w_in[p], 16)

        @block.scalar
        def _(act):
            with act.Fori(0, NR // EB) as i:
                def split(p):
                    act.wait_ge(w_in[p], i * 16 + 16)
                    act.activation(wh[:, p, :], stage[:, p, :], ACT.Copy).then_inc(S["w_hi"], 1)

                split(0)
                for u in range(NU + 1):
                    if u < NU:
                        act.wait_ge(S["gu"], i * NU + u + 1)
                        if u >= 2:
                            act.wait_ge(S["prod"], i * NU + u - 1)
                        act.activation(sg[:, u % 2, :], pg[u % 2][:], ACT.Silu).then_inc(S["silu"], 1)
                    if u >= 1:
                        v = u - 1
                        act.wait_ge(S["prod"], i * NU + v + 1)
                        if v >= NHB:
                            act.wait_ge(S["used"], i * NU + v - NHB + 1)
                        act.activation(hh[:, v % NHB, :], hf[:, v % NHB, :], ACT.Copy).then_inc(S["hi"], 1)
                    if u % NG == 1 and u // NG + 1 < EB:
                        split(u // NG + 1)

        def taken(dve, i, n):
            p, g = n // NG, n % NG
            dve.wait_ge(S["used"], i * NU + n + 1)
            dve.wait_ge(S["picked"], i * EB + p + 1)
            for t in range(TG):
                T = g * TG + t
                op = dve.scalar_tensor_tensor(out=xs[:, T, :], in0=py[n % 2][t // 2][:, t % 2, :], scalar=ew[:, p, T:T + 1],
                                              in1=xs[:, T, :], op0=ALU.mult, op1=ALU.add)
            op.then_inc(S["y_taken"], 1)

        @block.vector
        def _(dve):
            dve.sem_inc(S["y_taken"], 2)
            with dve.Fori(0, NR // EB) as i:
                def split(p):
                    dve.wait_ge(S["w_hi"], i * EB + p + 1)
                    dve.tensor_tensor(wl[:, p, :], stage[:, p, :], wh[:, p, :], ALU.subtract).then_inc(S["w_lo"], 1)
                    dve.tensor_copy(ew[:, p, :], M["rw"][:, :, bass.ds(i * EB + p, 1)].rearrange("p t a -> p (t a)")).then_inc(S["picked"], 1)

                split(0)
                for u in range(NU + 3):
                    if u < NU:
                        dve.wait_ge(S["silu"], i * NU + u + 1)
                        dve.tensor_tensor(hf[:, u % NHB, :], sg[:, u % 2, :], pu[u % 2][:], ALU.mult).then_inc(S["prod"], 1)
                    if 0 <= u - 1 < NU:
                        v = u - 1
                        dve.wait_ge(S["hi"], i * NU + v + 1)
                        dve.tensor_tensor(hl[:, v % NHB, :], hf[:, v % NHB, :], hh[:, v % NHB, :], ALU.subtract).then_inc(S["lo"], 1)
                    if u % NG == 1 and u // NG + 1 < EB:
                        split(u // NG + 1)
                    if u >= 3:
                        taken(dve, i, u - 3)

        @block.tensor
        def _(pe):
            with pe.Fori(0, NR // EB) as i:
                for u in range(NU + NL):
                    if u < NU:
                        p, g = u // NG, u % NG
                        if g == 0:
                            pe.wait_ge(S["w_lo"], i * EB + p + 1)
                        if u >= 2:
                            pe.wait_ge(S["prod"], i * NU + u - 1)
                        for half, bank in ((0, pg), (1, pu)):
                            n = 0
                            for kc in range(KC):
                                for w, x in ((wh, "xh"), (wh, "xl"), (wl, "xh")):
                                    op = pe.matmul(bank[u % 2][:], wgu(w, p, kc, half), M[x][:, kc, g * GT:(g + 1) * GT],
                                                   start=(n == 0), stop=(n == 3 * KC - 1))
                                    n += 1
                        op.then_inc(S["gu"], 1)
                    if u >= NL:
                        v = u - NL
                        p = v // NG
                        pe.wait_ge(S["y_taken"], i * NU + v + 1)
                        pe.wait_ge(S["lo"], i * NU + v + 1)
                        for t in range(TG):
                            for m, (h, w) in enumerate(((hh, wh), (hh, wl), (hl, wh))):
                                op = pe.matmul(py[v % 2][t // 2][:, t % 2, :], h[:, v % NHB, t * P:(t + 1) * P], w[:, p, WG:],
                                               start=(m == 0), stop=(m == 2))
                        op.then_inc(S["used"], 1)



NE0, TOP0, H0 = 8, 2, 1024
NE1, NR1, TOP1, I1 = 40, 32, 6, 128
SCALE1 = 2.5


def sparse_buffers(ctx, nc, NE, H, TOP, pieces, b1_dram):
    NB = NT * TOP + NE
    ROWS = NB * P

    def sb(n, s, d=F32):
        return ctx.enter_context(nc.sbuf_tensor(f"sp_{n}", s, d))

    s = named_semaphores(ctx, nc, "sp", "zeroed cleared b1 w_in0 w_in1 w_hi w_lo")
    return dict(w_in=[s["w_in0"], s["w_in1"]], NB=NB, TOP=TOP, PIECES=8 * NE, pieces=pieces, b1_dram=b1_dram, s=s, b1=sb("b1", [P, NE, H // P]),
                zero=sb("zero", [P, C]), junk=sb("junk", [P, 4]), stage=sb("stage", [P, 2, KC * H // 4]),
                wh=sb("wh", [P, 8 * NE, KC * H // 4], BF16), wl=sb("wl", [P, 8 * NE, KC * H // 4], BF16),
                owner=sb("owner", [1, NB], mybir.dt.int32),
                sent=nc.dram_tensor("sent_rows", (ROWS, C), F32, kind="Internal").ap(),
                back=nc.dram_tensor("back_rows", (ROWS, C), F32, kind="Internal").ap())


def mixture_buffers(ctx, nc, pre, NE):
    def sb(n, s, d=F32):
        return ctx.enter_context(nc.sbuf_tensor(f"{pre}_{n}", s, d))

    return dict(xh=sb("xh", [P, KC, NT * P], BF16), xl=sb("xl", [P, KC, NT * P], BF16), rw=sb("rw", [P, NT, NE]))


def decoder(nc, A, out):
    with ExitStack() as ctx:
        def sb(n, s, d=F32):
            return ctx.enter_context(nc.sbuf_tensor(n, s, d))

        xs = sb("xs", [P, NT, C])
        K = {"s": named_semaphores(ctx, nc, "g", "x weights consts zeroed stored")}
        K["ident"] = sb("ident", [P, P])
        K["identb"] = sb("identb", [P, P], BF16)
        K["causal"] = sb("causal", [P, 4, P], BF16)
        K["heads8"] = sb("heads8", [P, P])
        K["evenodd"] = sb("evenodd", [P, 2])
        K["eps4"] = sb("eps4", [P, TG])
        K["half4"] = sb("half4", [P, TG])
        K["earlier"] = sb("earlier", [P, P], BF16)
        K["all1"] = sb("all1", [P, P], BF16)
        K["steps"] = sb("steps", [P, NT])
        K["blocks"] = sb("blocks", [1, NT * TOP0 + NE0])
        M0 = dict(place=sb("place", [P, NT, 8], mybir.dt.int32), pw=sb("pw", [P, NT, TOP0]), rw=sb("rw0", [P, NT, NE0]),
                  sel=sb("sel", [P, NT, NE0], BF16))
        loads, later = [], []

        def into(ctx, loads):
            def put(name, shape, src):
                w = ctx.enter_context(nc.sbuf_tensor("w_" + name, shape, F32))
                loads.append((w, src))
                return w

            return (lambda name, cols=C: put(name, [P, KC, cols], A[name].rearrange("(k p) n -> p k n", p=P)),
                    lambda name, n: put(name, [P, n], A[name]),
                    lambda name, n=C: put(name, [P, n], A[name].partition_broadcast(P)))

        square, column, spread = into(ctx, loads)
        WX = {k: square("L0_xattn_W" + k[1]) for k in ("wq", "wk", "wv", "wo")}
        WX.update(bq=column("L0_xattn_bq", KC), bk=column("L0_xattn_bk", KC), bv=spread("L0_xattn_bv"), bo=spread("L0_xattn_bo"))
        R0 = dict(w=square("L0_ffn_router_w", NE0), b2=sb("b2_0", [NE0, C]))
        loads.append((R0["b2"], A["L0_ffn_b2"]))
        first = ctx.enter_context(ExitStack())
        square, column, spread = into(first, loads)
        WA = dict(qkv=square("L0_attn_qkv_weight", 3 * C), wp=square("L0_attn_proj_weight"), bp=spread("L0_attn_proj_bias"))
        K["n_weights"] = len(loads)
        K["n_consts"] = 11

        with nc.sbuf_tensor("steps_i", [P, NT], mybir.dt.int32) as steps, \
                nc.sbuf_tensor("blocks_i", [1, NT * TOP0 + NE0], mybir.dt.int32) as blocks, nc.Block() as block:
            @block.sync
            def _(sp):
                for g in range(NG):
                    sp.dma_start(xs[:, g * TG:(g + 1) * TG, :],
                                 A["x"][g * TG:(g + 1) * TG].rearrange("b t c -> t b c")).then_inc(K["s"]["x"], 16)
                for dst, src in loads:
                    sp.dma_start(dst[:], src).then_inc(K["s"]["weights"], 16)

            @block.gpsimd
            def _(pool):
                s = K["s"]
                pool.memset(K["eps4"][:], LN_EPS).then_inc(s["zeroed"], 1)
                pool.memset(K["half4"][:], -0.5).then_inc(s["zeroed"], 1)
                pool.memset(K["ident"][:], 0.0).then_inc(s["zeroed"], 1)
                pool.memset(K["identb"][:], 0.0).then_inc(s["zeroed"], 1)
                pool.memset(K["causal"][:], 0.0).then_inc(s["zeroed"], 1)
                pool.memset(K["heads8"][:], 1.0).then_inc(s["zeroed"], 1)
                pool.memset(K["evenodd"][:], 0.0).then_inc(s["zeroed"], 1)
                pool.memset(K["earlier"][:], 1.0).then_inc(s["zeroed"], 1)
                pool.memset(K["all1"][:], 1.0).then_inc(s["consts"], 1)
                pool.iota(steps[:], pattern=[[P, NT]], base=0, channel_multiplier=0).then_inc(s["consts"], 1)
                pool.iota(blocks[:], pattern=[[1, NT * TOP0 + NE0]], base=0, channel_multiplier=0).then_inc(s["consts"], 1)
                pool.wait_ge(s["zeroed"], 8)
                pool.affine_select(out=K["earlier"][:], in_=K["earlier"][:], compare_op=ALU.is_ge, fill=0.0, base=-1,
                                   pattern=[[1, P]], channel_multiplier=-1).then_inc(s["consts"], 1)
                for name in ("ident", "identb"):
                    pool.affine_select(out=K[name][:], in_=K[name][:], compare_op=ALU.not_equal, fill=1.0, base=0,
                                       pattern=[[-1, P]], channel_multiplier=1).then_inc(s["consts"], 1)
                pool.affine_select(out=K["causal"][:], in_=K["causal"][:], compare_op=ALU.is_ge, fill=-1e30, base=0,
                                   pattern=[[0, 4], [-1, P]], channel_multiplier=1).then_inc(s["consts"], 1)
                h8 = K["heads8"][:].rearrange("p (b e) -> p b e", e=8)
                pool.affine_select(out=h8, in_=h8, compare_op=ALU.is_ge, fill=0.0, base=0,
                                   pattern=[[-8, 16], [0, 8]], channel_multiplier=1).then_inc(s["zeroed"], 1)
                pool.wait_ge(s["zeroed"], 9)
                pool.affine_select(out=h8, in_=h8, compare_op=ALU.is_ge, fill=0.0, base=7,
                                   pattern=[[8, 16], [0, 8]], channel_multiplier=-1).then_inc(s["consts"], 1)
            @block.vector
            def _(dve):
                s = K["s"]
                dve.wait_ge(s["consts"], 8)
                dve.tensor_copy(K["steps"][:], steps[:]).then_inc(s["consts"], 1)
                dve.tensor_copy(K["blocks"][:], blocks[:]).then_inc(s["consts"], 1)
                idr = K["ident"][:].rearrange("p (q r n) -> p r q n", q=4, r=2)
                dve.tensor_reduce(K["evenodd"][:], idr, AX.XY, ALU.add).then_inc(s["consts"], 1)

        linear_attention(nc, K, xs, WA)
        first.close()
        with ExitStack() as m:
            M0.update(sparse_buffers(m, nc, NE0, H0, TOP0, A["L0_ffn_w"], A["L0_ffn_b1"]))
            softmax_attention(nc, K, xs, WX, "xa", ctx_dram=A["ctx_T"], M=M0)
            with nc.sbuf_tensor("xn_rows", [P, NT, C], F32) as xn:
                M0["xn"] = xn
                route(nc, K, xs, R0, "r0", NE0, TOP0, NE0, M0)
            gelu_blocks(nc, K, M0, NE0, H0)

        square, column, spread = into(ctx, later)
        w_attn = square("L1_attn_w_attn", 3 * C)
        WS = dict(wq=w_attn[:, :, 0:C], wk=w_attn[:, :, C:2 * C], wv=w_attn[:, :, 2 * C:3 * C], wo=square("L1_attn_w_proj"))
        WS.update(bq=column("L1_attn_bq", KC), bk=column("L1_attn_bk", KC), bv=spread("L1_attn_bv"), bo=spread("L1_attn_b_proj"))
        WH = dict(wq=square("L1_xattn_Wq"), wkv=square("L1_xattn_Wkv", 2 * C), wo=square("L1_xattn_Wo"))
        WH.update({b: spread("L1_xattn_" + b) for b in ("bq", "bk", "bv", "bo")})
        R1 = dict(w=square("L1_ffn_classifier_weight", NE1), corr=spread("L1_ffn_corr", NE1), scale=SCALE1)
        K["n_weights"] += len(later)
        combine(nc, K, xs, M0, later, K["s"]["weights"])
        softmax_attention(nc, K, xs, WS, "sa", causal=True)
        head_attention(nc, K, xs, WH, A["ctx_T"])
        with ExitStack() as m:
            M = mixture_buffers(m, nc, "m1", NE1)
            route(nc, K, xs, R1, "r1", NE1, TOP1, NR1, M)
            silu_experts(nc, K, xs, M, A["L1_ffn_w"], NR1, I1)

        with nc.Block() as block:
            @block.sync
            def _(sp):
                s = K["s"]
                for g in range(NG):
                    sp.dma_start(out[g * TG:(g + 1) * TG].rearrange("b t c -> t b c"),
                                 xs[:, g * TG:(g + 1) * TG, :]).then_inc(s["stored"], 16)
                sp.wait_ge(s["stored"], 16 * NG)


def kernel(**inputs):
    import numpy as _np
    import concourse.bacc as _bacc
    from concourse import mybir as _mybir
    from concourse.bass_utils import run_bass_kernel_spmd as _run

    a = {k: _np.asarray(v) for k, v in inputs.items()}
    laid = {
        "x": a["x"],
        "ctx_T": a["ctx_1024"].reshape(NT * P, C).T.reshape(KC, P, NT * P),
        "L0_attn_qkv_weight": a["L0_attn_qkv_weight"].T,
        "L0_attn_proj_weight": a["L0_attn_proj_weight"].T,
        "L0_attn_proj_bias": a["L0_attn_proj_bias"],
        "L1_attn_w_attn": a["L1_attn_w_attn"],
        "L1_attn_w_proj": a["L1_attn_w_proj"],
        "L1_attn_bq": a["L1_attn_b_attn"][0:C].reshape(KC, P).T,
        "L1_attn_bk": a["L1_attn_b_attn"][C:2 * C].reshape(KC, P).T,
        "L1_attn_bv": a["L1_attn_b_attn"][2 * C:3 * C],
        "L1_attn_b_proj": a["L1_attn_b_proj"],
        "L0_xattn_bv": a["L0_xattn_bv"], "L0_xattn_bo": a["L0_xattn_bo"],
        "L0_xattn_bq": a["L0_xattn_bq"].reshape(KC, P).T,
        "L0_xattn_bk": a["L0_xattn_bk"].reshape(KC, P).T,
    }
    w1 = a["L0_ffn_w1"].transpose(0, 2, 1).reshape(NE0, KC, P, H0).transpose(0, 2, 1, 3).reshape(NE0, P, KC * H0)
    w2 = a["L0_ffn_w2"].transpose(0, 2, 1).reshape(NE0, H0 // P, P, C).transpose(0, 2, 1, 3).reshape(NE0, P, H0 // P * C)
    gu = a["L1_ffn_gate_up_proj"][:NR1].transpose(0, 2, 1).reshape(NR1, KC, P, 2 * I1).transpose(0, 2, 1, 3).reshape(NR1, P, KC * 2 * I1)
    laid.update({
        "L0_ffn_w": _np.concatenate([w1, w2], axis=2).reshape(NE0, P, 8, KC * H0 // 4).transpose(0, 2, 1, 3)
                       .reshape(8 * NE0, P, KC * H0 // 4),
        "L0_ffn_b1": a["L0_ffn_b1"].reshape(NE0, H0 // P, P).transpose(0, 2, 1),
        "L0_ffn_b2": a["L0_ffn_b2"],
        "L0_ffn_router_w": a["L0_ffn_router_w"].T,
        "L1_ffn_w": _np.concatenate([gu, a["L1_ffn_down_proj"].transpose(0, 2, 1)], axis=2),
        "L1_ffn_classifier_weight": a["L1_ffn_classifier_weight"].T,
        "L1_ffn_corr": a["L1_ffn_e_score_correction_bias"],
        "L1_xattn_Wq": a["L1_xattn_Wq"],
        "L1_xattn_Wkv": _np.concatenate([a["L1_xattn_Wk"], a["L1_xattn_Wv"]], axis=1),
        "L1_xattn_Wo": a["L1_xattn_Wo"],
        **{"L1_xattn_" + b: a["L1_xattn_" + b] for b in ("bq", "bk", "bv", "bo")},
    })
    for w in ("Wq", "Wk", "Wv", "Wo"):
        laid["L0_xattn_" + w] = a["L0_xattn_" + w].T
    nc = _bacc.Bacc("TRN2", target_bir_lowering=False, num_devices=1)
    arrays, A = {}, {}
    for name, v in laid.items():
        v = _np.ascontiguousarray(v)
        arrays[f"in_{name}"] = v
        A[name] = nc.dram_tensor(f"in_{name}", v.shape, _mybir.dt.from_np(v.dtype), kind="ExternalInput").ap()
    out = nc.dram_tensor("out", (NT, P, C), F32, kind="ExternalOutput").ap()
    decoder(nc, A, out)
    r = _run(nc, [arrays], core_ids=[0])
    return r.results[0]["out"]
```

```python
from contextlib import ExitStack

import concourse.bass as bass
from concourse import mybir

P = 128
NT = 16
TG = 4
NG = NT // TG
GT = TG * P
C = 256
KC = C // P
BR = 2 * P
LN_EPS = 1e-5
LIN_EPS = 1e-15
FAR = 3.0e38

F32 = mybir.dt.float32
BF16 = mybir.dt.bfloat16
ALU = mybir.AluOpType
ACT = mybir.ActivationFunctionType
AX = mybir.AxisListType


def named_semaphores(ctx, nc, prefix, names):
    sems = {n: nc.alloc_semaphore(f"{prefix}_{n}") for n in names.split()}

    def give_back():
        nc.clear_and_free_semaphores(list(sems.values()))
        nc.all_engine_barrier()

    ctx.callback(give_back)
    return sems


def drained(uses, n):
    return sum(u == uses[n] for u in uses[:n + 1])


def total(uses, who):
    return sum(u == who for u in uses)


def tile_of(buf, i, t):
    return buf[:, bass.ds(i * TG + t, 1), :].rearrange("p a c -> p (a c)")



NORM_SEMS = "stats moments eps rstd normed biased"


def norm_buffers(sb, pre):
    return dict(st=sb(f"{pre}_st", [P, TG, 6]), mv=sb(f"{pre}_mv", [P, TG, 2]), ve=sb(f"{pre}_ve", [P, TG]),
                rs=sb(f"{pre}_rs", [P, TG]), xn=sb(f"{pre}_xn", [P, TG, C]), junk=sb(f"{pre}_junk", [P, 2]))


def norm_stats(dve, S, B, xs, i):
    for t in range(TG):
        dve.bn_stats(B["st"][:, t, :], tile_of(xs, i, t)).then_inc(S["stats"], 1)
    dve.wait_ge(S["stats"], i * TG + TG)
    dve.memset(B["junk"][:, 0:1], 0.0)
    for t in range(TG):
        dve.bn_aggr(B["mv"][:, t, :], B["st"][:, t, :]).then_inc(S["moments"], 1)


def norm_apply(dve, S, B, xs, i):
    dve.wait_ge(S["rstd"], i + 1)
    for t in range(TG):
        dve.tensor_scalar(B["xn"][:, t, :], tile_of(xs, i, t), B["mv"][:, t, 0:1], B["rs"][:, t:t + 1],
                          ALU.subtract, ALU.mult).then_inc(S["normed"], 1)


def norm_vector(dve, S, B, xs, i):
    norm_stats(dve, S, B, xs, i)
    norm_apply(dve, S, B, xs, i)


def norm_pool(pool, S, B, K, i):
    pool.wait_ge(S["moments"], i * TG + TG)
    pool.tensor_tensor(B["ve"][:], B["mv"][:, :, 1], K["eps4"][:], ALU.add).then_inc(S["eps"], 1)
    pool.wait_ge(S["eps"], i + 1)
    pool.tensor_tensor(B["rs"][:], B["ve"][:], K["half4"][:], ALU.pow).then_inc(S["rstd"], 1)


def bias_pool(pool, S, xs, bias, i):
    for t in range(TG):
        pool.wait_ge(S["normed"], i * TG + t + 1)
        pool.tensor_tensor(tile_of(xs, i, t), tile_of(xs, i, t), bias[:], ALU.add).then_inc(S["biased"], 1)



def linear_attention(nc, K, xs, W, M, share):
    HD = 8
    EARLY = 2
    CH = P // HD
    NORM_AT, TURN_AT = 1, (2, 3, 4, 5)
    with ExitStack() as ctx:
        def sb(n, s, d=F32):
            return ctx.enter_context(nc.sbuf_tensor("la_" + n, s, d))

        def pb(n, s, d=F32):
            return ctx.enter_context(nc.psum_tensor("la_" + n, s, d))

        B = norm_buffers(sb, "n")
        xnT = sb("xnT", [P, KC, GT])
        qT = sb("qT", [P, KC, GT])
        k = sb("k", [P, TG, C])
        v1 = sb("v1", [P, TG, KC, P + 1])
        nd = sb("nd", [P, 2, KC, P + CH])
        den = sb("den", [P, 2, KC, CH])
        rden = sb("rden", [P, 2, KC, CH])
        y = sb("y", [P, 2, C])
        yT = sb("yT", [P, 2, KC, P])
        mx = [pb(f"mx{b}", [P, 512]) for b in range(2)]
        vk = [pb(f"vk{b}", [P, KC, 256]) for b in range(2)]
        pn = [pb(f"pn{b}", [P, KC, P + CH]) for b in range(2)]
        py = pb("py", [P, 512])
        po = pb("po", [P, 512])
        S = named_semaphores(ctx, nc, "la", NORM_SEMS + " ones full emptied vk masked nd den_eps den_inv y_ready turned yT out added")
        USES, PRE = 2 + 4 + 4, 4
        block = ctx.enter_context(nc.Block())
        head_of = K["heads8"][:].rearrange("p (b e) -> p b e", e=HD)[:, :, 0]

        def bodies(eng, body):
            with eng.Fori(0, NG - 1) as i:
                body(i, False)
            body(NG - 1, True)

        @block.sync
        def _(sp):
            split_load(sp, M)
            with sp.Fori(0, NG) as i:
                pieces_load(sp, M, i, *share)
            sp.wait_ge(M["s"]["cleared"], 16)

        @block.gpsimd
        def _(pool):
            pool.memset(v1[:, :, :, P:P + 1], 1.0).then_inc(S["ones"], 1)
            pool.wait_ge(K["s"]["x"], 16 * NG)
            pool.wait_ge(K["s"]["weights"], 16 * K["n_weights"])
            pool.memset(M["zero"][:], 0.0).then_inc(M["s"]["zeroed"], 1)
            pool.wait_ge(M["s"]["zeroed"], 1)
            pool.sem_inc(M["s"]["w_lo"], 2)
            norm_pool(pool, S, B, K, 0)
            bias_pool(pool, S, xs, W["bp"], 0)

            def body(i, last):
                pieces_split(pool, M, i, share, range(EARLY))
                if not last:
                    norm_pool(pool, S, B, K, i + 1)
                    bias_pool(pool, S, xs, W["bp"], i + 1)
                pieces_split(pool, M, i, share, range(EARLY, share[1]))

            bodies(pool, body)

        @block.vector
        def _(dve):
            dve.wait_ge(K["s"]["x"], 16 * NG)
            norm_vector(dve, S, B, xs, 0)

            def body(i, last):
                for s in range(TG + 3):
                    if s < TG:
                        t = s
                        dve.wait_ge(S["vk"], i * TG + t + 1)
                        dve.tensor_tensor(nd[:, t % 2, :, 0:P], vk[t % 2][:, :, 0:P],
                                          K["heads8"][:].unsqueeze(1).to_broadcast([P, KC, P]), ALU.mult)
                        for c in range(KC):
                            op = dve.tensor_scalar(nd[:, t % 2, c, P:], head_of, vk[t % 2][:, c, P:P + 1],
                                                   None, ALU.mult)
                        op.then_inc(S["masked"], 1)
                    if 0 <= s - 1 < TG:
                        t = s - 1
                        dve.wait_ge(S["nd"], i * TG + t + 1)
                        dve.tensor_scalar(den[:, t % 2], pn[t % 2][:, :, P:], LIN_EPS, None,
                                          ALU.add).then_inc(S["den_eps"], 1)
                        dve.wait_ge(S["den_eps"], i * TG + t + 1)
                        dve.reciprocal(rden[:, t % 2], den[:, t % 2]).then_inc(S["den_inv"], 1)
                        dve.wait_ge(S["den_inv"], i * TG + t + 1)
                        for c in range(KC):
                            op = dve.tensor_tensor(y[:, t % 2, c * P:(c + 1) * P].rearrange("p (h d) -> p h d", d=HD),
                                                   pn[t % 2][:, c, 0:P].rearrange("p (h d) -> p h d", d=HD),
                                                   rden[:, t % 2, c].unsqueeze(2).to_broadcast([P, CH, HD]), ALU.mult)
                        op.then_inc(S["y_ready"], 1)
                    if 0 <= s - 3 < TG:
                        t = s - 3
                        dve.wait_ge(S["out"], i * TG + t + 1)
                        dve.wait_ge(S["biased"], i * TG + t + 1)
                        dve.tensor_tensor(tile_of(xs, i, t), tile_of(xs, i, t), po[:, 0:C], ALU.add).then_inc(S["added"], 1)
                    if s == NORM_AT - 1 and not last:
                        norm_stats(dve, S, B, xs, i + 1)
                    if s == NORM_AT and not last:
                        norm_apply(dve, S, B, xs, i + 1)

            bodies(dve, body)

        @block.scalar
        def _(act):
            act.wait_ge(S["ones"], 1)

            def turned(i, n, t):
                act.wait_ge(S["full"], i * USES + n + 1)
                act.activation(xnT[:, :, t * P:(t + 1) * P], mx[t % 2][:, 0:C].rearrange("p (a b) -> p a b", a=KC),
                               ACT.Copy).then_inc(S["emptied"], 1)

            for t in range(TG):
                turned(0, t, t)

            def body(i, last):
                for c in range(KC):
                    act.wait_ge(S["full"], i * USES + PRE + c + 1)
                    act.activation(qT[:, c, :], mx[c % 2][:], ACT.Relu).then_inc(S["emptied"], 1)
                for t in range(TG):
                    act.wait_ge(S["full"], i * USES + PRE + 2 + t + 1)
                    act.activation(k[:, t, :], mx[t % 2][:, 0:C], ACT.Relu)
                    act.activation(v1[:, t, :, 0:P], mx[t % 2][:, C:2 * C].rearrange("p (a b) -> p a b", a=KC),
                                   ACT.Relu).then_inc(S["emptied"], 1)
                for s in range(TG + 3):
                    if 0 <= s - 2 < TG:
                        t = s - 2
                        act.wait_ge(S["turned"], i * TG + t + 1)
                        act.activation(yT[:, t % 2], py[:, 0:C].rearrange("p (a b) -> p a b", a=KC),
                                       ACT.Copy).then_inc(S["yT"], 1)
                    if s in TURN_AT and not last:
                        t = TURN_AT.index(s)
                        turned(i, PRE + 6 + t, t)

            bodies(act, body)

        @block.tensor
        def _(pe):
            pe.wait_ge(K["s"]["weights"], 16 * K["n_weights"])
            pe.wait_ge(K["s"]["consts"], K["n_consts"])
            pe.wait_ge(S["ones"], 1)

            def turn(i, n, t):
                pe.wait_ge(S["normed"], (i * TG + t + 1) if n < PRE else (i + 1) * TG + t + 1)
                if n >= 2:
                    pe.wait_ge(S["emptied"], i * USES + n - 1)
                for c in range(KC):
                    op = pe.transpose(mx[t % 2][:, c * P:(c + 1) * P], B["xn"][:, t, c * P:(c + 1) * P], K["ident"][:])
                op.then_inc(S["full"], 1)

            for t in range(TG):
                turn(0, t, t)

            def body(i, last):
                pe.wait_ge(S["emptied"], i * USES + PRE)
                for c in range(KC):
                    for kc in range(KC):
                        op = pe.matmul(mx[c % 2][:], W["qkv"][:, kc, c * P:(c + 1) * P], xnT[:, kc, :],
                                       start=(kc == 0), stop=(kc == KC - 1))
                    op.then_inc(S["full"], 1)
                for t in range(TG):
                    pe.wait_ge(S["emptied"], i * USES + PRE + 1 + t)
                    for kc in range(KC):
                        op = pe.matmul(mx[t % 2][:], xnT[:, kc, t * P:(t + 1) * P], W["qkv"][:, kc, C:3 * C],
                                       start=(kc == 0), stop=(kc == KC - 1))
                    op.then_inc(S["full"], 1)
                for s in range(TG + 3):
                    if s < TG:
                        t = s
                        pe.wait_ge(S["emptied"], i * USES + PRE + 3 + t)
                        if t >= 2:
                            pe.wait_ge(S["masked"], i * TG + t - 1)
                        for c in range(KC):
                            op = pe.matmul(vk[t % 2][:, c, 0:P + 1], k[:, t, c * P:(c + 1) * P], v1[:, t, c, :],
                                           start=True, stop=True)
                        op.then_inc(S["vk"], 1)
                    if 0 <= s - 1 < TG:
                        t = s - 1
                        pe.wait_ge(S["masked"], i * TG + t + 1)
                        if t >= 2:
                            pe.wait_ge(S["y_ready"], i * TG + t - 1)
                        for c in range(KC):
                            op = pe.matmul(pn[t % 2][:, c], qT[:, c, t * P:(t + 1) * P],
                                           nd[:, t % 2, c], start=True, stop=True)
                        op.then_inc(S["nd"], 1)
                    if 0 <= s - 2 < TG:
                        t = s - 2
                        pe.wait_ge(S["y_ready"], i * TG + t + 1)
                        if t >= 1:
                            pe.wait_ge(S["yT"], i * TG + t)
                        for c in range(KC):
                            op = pe.transpose(py[:, c * P:(c + 1) * P], y[:, t % 2, c * P:(c + 1) * P], K["ident"][:])
                        op.then_inc(S["turned"], 1)
                    if 0 <= s - 3 < TG:
                        t = s - 3
                        pe.wait_ge(S["yT"], i * TG + t + 1)
                        if t >= 1:
                            pe.wait_ge(S["added"], i * TG + t)
                        for kc in range(KC):
                            op = pe.matmul(po[:, 0:C], yT[:, t % 2, kc, :], W["wp"][:, kc, :],
                                           start=(kc == 0), stop=(kc == KC - 1))
                        op.then_inc(S["out"], 1)
                    if s in TURN_AT and not last:
                        t = TURN_AT.index(s)
                        turn(i, PRE + 6 + t, t)

            bodies(pe, body)



def softmax_attention(nc, K, xs, W, pre, ctx_dram=None, causal=False, M=None, share=None):
    NH, HD = 16, 16
    NB = 4
    UN = TG * NB
    NORM_AT, TURN_AT = 7, (9, 10, 11, 13)
    with ExitStack() as ctx:
        def sb(n, s, d=F32):
            return ctx.enter_context(nc.sbuf_tensor(f"{pre}_{n}", s, d))

        def pb(n, s, d=F32):
            return ctx.enter_context(nc.psum_tensor(f"{pre}_{n}", s, d))

        B = norm_buffers(sb, "n")
        xnT = sb("xnT", [P, KC, GT])
        cT = sb("cT", [P, KC, GT]) if ctx_dram is not None else xnT
        qT = sb("qT", [P, KC, GT])
        kk = sb("kk", [P, KC, TG, 2, P])
        vp = sb("vp", [P, TG, NH, 2 * HD])
        p = sb("p", [P, 2, 4, P])
        pT = sb("pT", [P, 2, 4, P])
        nm = sb("nm", [P, 2, 4])
        z = sb("z", [P, 2, 4])
        rz = sb("rz", [P, 2, 4])
        bq = sb("bq", [P, KC])
        yT = sb("yT", [P, KC, P])
        mx = [pb(f"mx{b}", [P, 512]) for b in range(2)]
        sc = [pb(f"sc{b}", [P, 4, P]) for b in range(2)]
        tp = [pb(f"tp{b}", [P, 4, P]) for b in range(2)]
        py = [pb(f"py{b}", [P, KC, P]) for b in range(2)]
        S = named_semaphores(ctx, nc, pre, NORM_SEMS + " zeros bq ctx_in full by_act by_dve scored maxed exped summed zinv scaled"
                  " pt_full pt pv yT")
        USES = "q0 q1 k0 k1 v0 v1 v2 v3 p0 T0 T1 T2 p1 T3 p2 p3".split()
        LAST = [x for x in USES if x[0] != "T"]
        PRE = TG
        NU, NA = len(USES), sum(x[0] in "qT" for x in USES)
        ND = NU - NA
        block = ctx.enter_context(nc.Block())

        def uses(last):
            return LAST if last else USES

        def bank(x, last):
            return mx[uses(last).index(x) % 2]

        def wait_full(eng, i, x, last):
            eng.wait_ge(S["full"], PRE + i * NU + uses(last).index(x) + 1)

        def wait_emptied(eng, i, x, last):
            order = uses(last)
            before = order[:order.index(x) + 1]
            if x[0] in "qT":
                eng.wait_ge(S["by_act"], PRE + i * NA + sum(y[0] in "qT" for y in before))
            else:
                eng.wait_ge(S["by_dve"], 2 + i * ND + sum(y[0] not in "qT" for y in before))

        def wait_bank(eng, i, x, last):
            n = uses(last).index(x)
            if n >= 2:
                wait_emptied(eng, i, uses(last)[n - 2], last)
            else:
                eng.wait_ge(S["by_dve"], i * ND + n + 1)

        def bodies(eng, body):
            with eng.Fori(0, NG - 1) as i:
                body(i, False)
            body(NG - 1, True)

        def heads(u):
            b = u % NB
            return [2 * b, 2 * b + 1, 8 + 2 * b, 9 + 2 * b]

        if ctx_dram is not None:
            @block.sync
            def _(sp):
                sp.dma_start(cT[:], ctx_dram[:, :, 0:GT].rearrange("k p t -> p k t")).then_inc(S["ctx_in"], 16)
                with sp.Fori(1, NG) as i:
                    if M is not None:
                        pieces_load(sp, M, i - 1, *share)
                    wait_full(sp, i - 1, "v3", False)
                    sp.dma_start(cT[:], ctx_dram[:, :, bass.ds(i * GT, GT)].rearrange("k p t -> p k t")).then_inc(S["ctx_in"], 16)
                if M is not None:
                    pieces_load(sp, M, NG - 1, *share)

        @block.gpsimd
        def _(pool):
            pool.memset(vp[:], 0.0).then_inc(S["zeros"], 1)
            pool.wait_ge(K["s"]["weights"], 16 * K["n_weights"])
            norm_pool(pool, S, B, K, 0)
            bias_pool(pool, S, xs, W["bo"], 0)

            def body(i, last):
                if M is not None:
                    pieces_split(pool, M, i, share, range(share[1] // 4 * 2))
                if not last:
                    norm_pool(pool, S, B, K, i + 1)
                    bias_pool(pool, S, xs, W["bo"], i + 1)
                if M is not None:
                    pieces_split(pool, M, i, share, range(share[1] // 4 * 2, share[1]))

            bodies(pool, body)

        def resid(dve, i, t, last):
            wait_full(dve, i, f"p{t}", last)
            dve.wait_ge(S["biased"], i * TG + t + 1)
            dve.tensor_tensor(tile_of(xs, i, t), tile_of(xs, i, t), bank(f"p{t}", last)[:, 0:C], ALU.add).then_inc(S["by_dve"], 1)

        @block.vector
        def _(dve):
            dve.wait_ge(S["zeros"], 1)
            dve.wait_ge(K["s"]["weights"], 16 * K["n_weights"])
            dve.sem_inc(S["by_dve"], 2)
            norm_vector(dve, S, B, xs, 0)

            def body(i, last):
                for c in range(KC):
                    wait_full(dve, i, f"k{c}", last)
                    for par in range(2):
                        op = dve.tensor_scalar(kk[:, c, :, par, :], bank(f"k{c}", last)[:].rearrange("p (t n) -> p t n", t=TG),
                                               W["bk"][:, c:c + 1], K["evenodd"][:, par:par + 1], ALU.add, ALU.mult)
                    op.then_inc(S["by_dve"], 1)
                for t in range(TG):
                    wait_full(dve, i, f"v{t}", last)
                    for par in range(2):
                        op = dve.tensor_tensor(
                            vp[:, t].rearrange("p (j r) d -> p j r d", r=2)[:, :, par, par * HD:(par + 1) * HD],
                            bank(f"v{t}", last)[:, 0:C].rearrange("p (j r d) -> p j r d", r=2, d=HD)[:, :, par, :],
                            W["bv"][:].rearrange("p (j r d) -> p j r d", r=2, d=HD)[:, :, par, :], ALU.add)
                    op.then_inc(S["by_dve"], 1)
                for s in range(UN + 6):
                    if s < UN:
                        u = s
                        dve.wait_ge(S["scored"], i * UN + u + 1)
                        dve.tensor_reduce(nm[:, u % 2, :], sc[u % 2][:], AX.X, ALU.max, negate=True).then_inc(S["maxed"], 1)
                    if 0 <= s - 1 < UN:
                        u = s - 1
                        dve.wait_ge(S["exped"], i * UN + u + 1)
                        dve.tensor_reduce(z[:, u % 2, :], p[:, u % 2], AX.X, ALU.add).then_inc(S["summed"], 1)
                        dve.wait_ge(S["summed"], i * UN + u + 1)
                        dve.reciprocal(rz[:, u % 2, :], z[:, u % 2, :]).then_inc(S["zinv"], 1)
                        dve.wait_ge(S["zinv"], i * UN + u + 1)
                        dve.tensor_tensor(p[:, u % 2], p[:, u % 2], rz[:, u % 2, :].unsqueeze(2).to_broadcast([P, 4, P]),
                                          ALU.mult).then_inc(S["scaled"], 1)
                    if s >= 9 and (s - 9) % 4 == 0:
                        resid(dve, i, (s - 9) // 4, last)
                    if s == NORM_AT - 1 and not last:
                        norm_stats(dve, S, B, xs, i + 1)
                    if s == NORM_AT and not last:
                        norm_apply(dve, S, B, xs, i + 1)

            bodies(dve, body)

        @block.scalar
        def _(act):
            act.wait_ge(K["s"]["weights"], 16 * K["n_weights"])
            act.activation(bq[:], W["bq"][:], ACT.Copy, scale=HD ** -0.5).then_inc(S["bq"], 1)
            act.wait_ge(S["bq"], 1)

            def turned(t, mxb):
                act.activation(xnT[:, :, t * P:(t + 1) * P], mxb[:, 0:C].rearrange("p (a b) -> p a b", a=KC),
                               ACT.Copy).then_inc(S["by_act"], 1)

            for t in range(TG):
                act.wait_ge(S["full"], t + 1)
                turned(t, mx[t % 2])

            def body(i, last):
                for c in range(KC):
                    wait_full(act, i, f"q{c}", last)
                    act.activation(qT[:, c, :], bank(f"q{c}", last)[:], ACT.Identity, bias=bq[:, c:c + 1],
                                   scale=HD ** -0.5).then_inc(S["by_act"], 1)

                for s in range(UN + 4):
                    if s < UN:
                        u = s
                        act.wait_ge(S["maxed"], i * UN + u + 1)
                        if u >= 2:
                            act.wait_ge(S["pt_full"], i * UN + u - 1)
                        for j in range(4):
                            op = act.activation(p[:, u % 2, j, :], sc[u % 2][:, j, :], ACT.Exp, bias=nm[:, u % 2, j:j + 1])
                        op.then_inc(S["exped"], 1)
                    if 0 <= s - 2 < UN:
                        u = s - 2
                        act.wait_ge(S["pt_full"], i * UN + u + 1)
                        if u >= 2:
                            act.wait_ge(S["pv"], i * UN + u - 1)
                        act.activation(pT[:, u % 2], tp[u % 2][:], ACT.Copy).then_inc(S["pt"], 1)
                    if s >= 7 and (s - 7) % 4 == 0:
                        t = (s - 7) // 4
                        act.wait_ge(S["pv"], i * UN + 4 * t + 4)
                        act.activation(yT[:], py[t % 2][:], ACT.Copy).then_inc(S["yT"], 1)
                    if s in TURN_AT and not last:
                        t = TURN_AT.index(s)
                        wait_full(act, i, f"T{t}", last)
                        turned(t, bank(f"T{t}", last))

            bodies(act, body)

        @block.tensor
        def _(pe):
            pe.wait_ge(K["s"]["weights"], 16 * K["n_weights"])
            pe.wait_ge(K["s"]["consts"], K["n_consts"])
            pe.wait_ge(S["zeros"], 1)

            def turn(i, t, mxb):
                pe.wait_ge(S["normed"], i * TG + t + 1)
                for c in range(KC):
                    op = pe.transpose(mxb[:, c * P:(c + 1) * P], B["xn"][:, t, c * P:(c + 1) * P], K["ident"][:])
                op.then_inc(S["full"], 1)

            for t in range(TG):
                if t >= 2:
                    pe.wait_ge(S["by_act"], t - 1)
                turn(0, t, mx[t % 2])

            def body(i, last):
                pe.wait_ge(S["by_act"], i * NA + TG)
                for what, src in (("wq", xnT), ("wk", cT)):
                    if what == "wk" and ctx_dram is not None:
                        pe.wait_ge(S["ctx_in"], i * 16 + 16)
                    for c in range(KC):
                        x = f"{what[1]}{c}"
                        wait_bank(pe, i, x, last)
                        for kc in range(KC):
                            op = pe.matmul(bank(x, last)[:], W[what][:, kc, c * P:(c + 1) * P], src[:, kc, :],
                                           start=(kc == 0), stop=(kc == KC - 1))
                        op.then_inc(S["full"], 1)
                for t in range(TG):
                    wait_bank(pe, i, f"v{t}", last)
                    for kc in range(KC):
                        op = pe.matmul(bank(f"v{t}", last)[:, 0:C], cT[:, kc, t * P:(t + 1) * P], W["wv"][:, kc, :],
                                       start=(kc == 0), stop=(kc == KC - 1))
                    op.then_inc(S["full"], 1)

                def project(t):
                    pe.wait_ge(S["yT"], i * TG + t + 1)
                    wait_bank(pe, i, f"p{t}", last)
                    for kc in range(KC):
                        op = pe.matmul(bank(f"p{t}", last)[:, 0:C], yT[:, kc, :], W["wo"][:, kc, :],
                                       start=(kc == 0), stop=(kc == KC - 1))
                    op.then_inc(S["full"], 1)

                for s in range(UN + 6):
                    if s < UN:
                        u, t, b = s, s // NB, s % NB
                        if u == 0:
                            wait_emptied(pe, i, "q1", last)
                            wait_emptied(pe, i, "v3", last)
                        if u >= 2:
                            pe.wait_ge(S["exped"], i * UN + u - 1)
                        if causal:
                            pe.matmul(sc[u % 2][:], K["identb"][:], K["causal"][:], start=True, stop=True)
                        for c in range(KC):
                            r = slice(32 * b, 32 * b + 32)
                            op = pe.matmul(sc[u % 2][:, 2 * c:2 * c + 2, :], qT[r, c, t * P:(t + 1) * P],
                                           kk[r, c, t, :, :], start=not causal, stop=True,
                                           tile_position=(32 * b, 0), skip_group_check=causal)
                        op.then_inc(S["scored"], 1)
                    if 0 <= s - 2 < UN:
                        u = s - 2
                        pe.wait_ge(S["scaled"], i * UN + u + 1)
                        if u >= 2:
                            pe.wait_ge(S["pt"], i * UN + u - 1)
                        for j in range(4):
                            op = pe.transpose(tp[u % 2][:, j, :], p[:, u % 2, j, :], K["ident"][:])
                        op.then_inc(S["pt_full"], 1)
                    if 0 <= s - 3 < UN:
                        u = s - 3
                        t, b = u // NB, u % NB
                        pe.wait_ge(S["pt"], i * UN + u + 1)
                        if b == 0 and t >= 2:
                            pe.wait_ge(S["yT"], i * TG + t - 1)
                        for j, h in enumerate(heads(u)):
                            op = pe.matmul(py[t % 2][32 * b:32 * b + 32, j // 2, :], vp[:, t, h, :], pT[:, u % 2, j, :],
                                           start=(j % 2 == 0), stop=(j % 2 == 1), tile_position=(0, 32 * b))
                        op.then_inc(S["pv"], 1)
                    if s >= 8 and (s - 8) % 4 == 0 and (s - 8) // 4 < TG:
                        project((s - 8) // 4)
                    if s in TURN_AT and not last:
                        t = TURN_AT.index(s)
                        wait_bank(pe, i, f"T{t}", last)
                        turn(i + 1, t, bank(f"T{t}", last))

            bodies(pe, body)



def head_attention(nc, K, xs, W, ctx_dram):
    NH, HD = 16, 16
    NV = 7
    with ExitStack() as ctx:
        def sb(n, s, d=F32):
            return ctx.enter_context(nc.sbuf_tensor("ha_" + n, s, d))

        def pb(n, s, d=F32):
            return ctx.enter_context(nc.psum_tensor("ha_" + n, s, d))

        B = norm_buffers(sb, "n")
        xnT = sb("xnT", [P, KC, GT])
        cT = sb("cT", [P, KC, GT])
        q = sb("q", [P, 2, NH, HD])
        k = sb("k", [P, 2, NH, HD])
        vT = sb("vT", [P, 2, HD, NH])
        qk = sb("qk", [P, NH, NH, HD])
        wv = sb("wv", [P, NH, HD, NH])
        sc = sb("sc", [P, 2, NH, NH])
        sh = sb("sh", [P, 2, NH, NH])
        w = sb("w", [P, 2, NH, NH])
        nm = sb("nm", [P, 2, NH])
        z = sb("z", [P, 2, NH])
        rz = sb("rz", [P, 2, NH])
        o = sb("o", [P, 2, NH, HD])
        y = sb("y", [P, 2, C])
        yT = sb("yT", [P, 2, KC, P])
        mx = [pb(f"mx{b}", [P, 512]) for b in range(2)]
        pq = [pb(f"pq{b}", [P, 512]) for b in range(2)]
        pk = [pb(f"pk{b}", [P, 512]) for b in range(2)]
        py = pb("py", [P, 512])
        po = pb("po", [P, 512])
        S = named_semaphores(ctx, nc, "ha", NORM_SEMS + " ctx_in0 ctx_in1 ctx_in2 ctx_in3 full emptied q_full k_full q_taken k_taken qk_dve qk_pool scored maxed"
                  " shifted weighed wv_dve wv_pool summed zed zinv y_ready turned yT out added")
        ctx_in = [S[f"ctx_in{t}"] for t in range(TG)]
        block = ctx.enter_context(nc.Block())

        def bodies(eng, body):
            with eng.Fori(0, NG - 1) as i:
                body(i, False)
            body(NG - 1, True)

        def qk_product(eng, b, lo, hi):
            n = hi - lo
            return eng.tensor_tensor(qk[:, lo:hi], q[:, b, lo:hi].unsqueeze(2).to_broadcast([P, n, NH, HD]),
                                     k[:, b].unsqueeze(1).to_broadcast([P, n, NH, HD]), ALU.mult)

        def wv_product(eng, b, lo, hi):
            n = hi - lo
            return eng.tensor_tensor(wv[:, lo:hi], w[:, b, lo:hi].unsqueeze(2).to_broadcast([P, n, HD, NH]),
                                     vT[:, b].unsqueeze(1).to_broadcast([P, n, HD, NH]), ALU.mult)

        def slot(buf, t):
            return buf[:, :, t % TG * P:(t % TG + 1) * P]

        @block.sync
        def _(sp):
            for t in range(TG):
                sp.dma_start(slot(cT, t), ctx_dram[:, :, t * P:(t + 1) * P].rearrange("k p t -> p k t")).then_inc(ctx_in[t], 16)
            with sp.Fori(1, NG) as i:
                for t in range(TG):
                    sp.wait_ge(S["k_full"], (i - 1) * TG + t + 1)
                    sp.dma_start(slot(cT, t), ctx_dram[:, :, bass.ds(i * GT + t * P, P)].rearrange("k p t -> p k t")).then_inc(ctx_in[t], 16)

        @block.gpsimd
        def _(pool):
            pool.wait_ge(K["s"]["x"], 16 * NG)
            pool.wait_ge(K["s"]["weights"], 16 * K["n_weights"])
            pool.wait_ge(K["s"]["consts"], K["n_consts"])

            def qk_pool(i, t):
                pool.wait_ge(S["q_taken"], i * TG + t + 1)
                pool.wait_ge(S["k_taken"], i * TG + t + 1)
                if t >= 1:
                    pool.wait_ge(S["scored"], i * TG + t)
                qk_product(pool, t % 2, NV, NH).then_inc(S["qk_pool"], 1)

            def wv_pool(i, t):
                pool.wait_ge(S["weighed"], i * TG + t + 1)
                if t >= 1:
                    pool.wait_ge(S["summed"], i * TG + t)
                wv_product(pool, t % 2, NV, NH).then_inc(S["wv_pool"], 1)

            def body(i, last):
                if not last:
                    norm_pool(pool, S, B, K, i + 1)
                    bias_pool(pool, S, xs, W["bo"], i + 1)
                for s in range(TG):
                    if s + 2 < TG or not last:
                        qk_pool(i, s + 2)
                    if s + 1 < TG or not last:
                        wv_pool(i, s + 1)

            norm_pool(pool, S, B, K, 0)
            bias_pool(pool, S, xs, W["bo"], 0)
            qk_pool(0, 0)
            qk_pool(0, 1)
            wv_pool(0, 0)
            bodies(pool, body)

        @block.vector
        def _(dve):
            dve.wait_ge(K["s"]["x"], 16 * NG)
            dve.wait_ge(K["s"]["weights"], 16 * K["n_weights"])
            dve.wait_ge(K["s"]["consts"], K["n_consts"])

            def take(i, t):
                b = t % 2
                dve.wait_ge(S["q_full"], i * TG + t + 1)
                dve.tensor_tensor(q[:, b].rearrange("p h d -> p (h d)"), pq[b][:, 0:C], W["bq"][:],
                                  ALU.add).then_inc(S["q_taken"], 1)
                dve.wait_ge(S["k_full"], i * TG + t + 1)
                dve.tensor_tensor(k[:, b].rearrange("p h d -> p (h d)"), pk[b][:, 0:C], W["bk"][:], ALU.add)
                dve.tensor_tensor(vT[:, b], pk[b][:, C:2 * C].rearrange("p (h d) -> p d h", h=NH),
                                  W["bv"][:].rearrange("p (h d) -> p d h", h=NH), ALU.add).then_inc(S["k_taken"], 1)
                dve.wait_ge(S["k_taken"], i * TG + t + 1)
                qk_product(dve, b, 0, NV).then_inc(S["qk_dve"], 1)

            def weigh(i, t):
                b = t % 2
                dve.wait_ge(S["weighed"], i * TG + t + 1)
                wv_product(dve, b, 0, NV).then_inc(S["wv_dve"], 1)
                dve.tensor_reduce(z[:, b, :], w[:, b], AX.X, ALU.add).then_inc(S["zed"], 1)

            def score(i, t):
                b = t % 2
                dve.wait_ge(S["qk_dve"], i * TG + t + 1)
                dve.tensor_reduce(sc[:, b, 0:NV], qk[:, 0:NV], AX.X, ALU.add)
                dve.wait_ge(S["qk_pool"], i * TG + t + 1)
                dve.tensor_reduce(sc[:, b, NV:], qk[:, NV:], AX.X, ALU.add).then_inc(S["scored"], 1)
                dve.wait_ge(S["scored"], i * TG + t + 1)
                dve.tensor_reduce(nm[:, b, :], sc[:, b], AX.X, ALU.max, negate=True).then_inc(S["maxed"], 1)
                dve.wait_ge(S["maxed"], i * TG + t + 1)
                dve.tensor_tensor(sh[:, b], sc[:, b], nm[:, b, :].unsqueeze(2).to_broadcast([P, NH, NH]),
                                  ALU.add).then_inc(S["shifted"], 1)

            def attend(i, t):
                b = t % 2
                dve.wait_ge(S["zed"], i * TG + t + 1)
                dve.reciprocal(rz[:, b, :], z[:, b, :]).then_inc(S["zinv"], 1)
                dve.wait_ge(S["wv_dve"], i * TG + t + 1)
                dve.tensor_reduce(o[:, b, 0:NV], wv[:, 0:NV], AX.X, ALU.add)
                dve.wait_ge(S["wv_pool"], i * TG + t + 1)
                dve.tensor_reduce(o[:, b, NV:], wv[:, NV:], AX.X, ALU.add).then_inc(S["summed"], 1)
                dve.wait_ge(S["zinv"], i * TG + t + 1)
                dve.wait_ge(S["summed"], i * TG + t + 1)
                dve.tensor_tensor(y[:, b, :].rearrange("p (h d) -> p h d", h=NH), o[:, b],
                                  rz[:, b, :].unsqueeze(2).to_broadcast([P, NH, HD]), ALU.mult).then_inc(S["y_ready"], 1)

            def added(i, t):
                dve.wait_ge(S["out"], i * TG + t + 1)
                dve.wait_ge(S["biased"], i * TG + t + 1)
                dve.tensor_tensor(tile_of(xs, i, t), tile_of(xs, i, t), po[:, 0:C], ALU.add).then_inc(S["added"], 1)

            def body(i, last):
                if not last:
                    norm_stats(dve, S, B, xs, i + 1)
                for s in range(TG):
                    new, mid = s + 2 < TG or not last, s + 1 < TG or not last
                    if new:
                        take(i, s + 2)
                    if s == 0 and not last:
                        dve.wait_ge(S["full"], (i + 1) * TG)
                        dve.memset(B["junk"][:, 1:2], 0.0)
                        norm_apply(dve, S, B, xs, i + 1)
                    if mid:
                        weigh(i, s + 1)
                    if new:
                        score(i, s + 2)
                    added(i, s)
                    if mid:
                        attend(i, s + 1)

            norm_vector(dve, S, B, xs, 0)
            take(0, 0)
            score(0, 0)
            take(0, 1)
            weigh(0, 0)
            score(0, 1)
            attend(0, 0)
            bodies(dve, body)

        @block.scalar
        def _(act):
            def turned(i, t):
                act.wait_ge(S["full"], i * TG + t + 1)
                act.activation(slot(xnT, t), mx[t % 2][:, 0:C].rearrange("p (a b) -> p a b", a=KC), ACT.Copy).then_inc(S["emptied"], 1)

            def exponentials(i, t):
                act.wait_ge(S["shifted"], i * TG + t + 1)
                act.activation(w[:, t % 2], sh[:, t % 2], ACT.Exp, scale=HD ** -0.5).then_inc(S["weighed"], 1)

            def y_turned(i, t):
                act.wait_ge(S["turned"], i * TG + t + 1)
                act.activation(yT[:, t % 2], py[:, 0:C].rearrange("p (a b) -> p a b", a=KC), ACT.Copy).then_inc(S["yT"], 1)

            def body(i, last):
                for s in range(TG):
                    if not last:
                        turned(i + 1, s)
                    if s + 2 < TG or not last:
                        exponentials(i, s + 2)
                    if s + 1 < TG or not last:
                        y_turned(i, s + 1)

            for t in range(TG):
                turned(0, t)
            exponentials(0, 0)
            exponentials(0, 1)
            y_turned(0, 0)
            bodies(act, body)

        @block.tensor
        def _(pe):
            pe.wait_ge(K["s"]["x"], 16 * NG)
            pe.wait_ge(K["s"]["weights"], 16 * K["n_weights"])
            pe.wait_ge(K["s"]["consts"], K["n_consts"])

            def turn(i, t, used):
                pe.wait_ge(S["normed"], i * TG + t + 1)
                if used:
                    pe.wait_ge(S["emptied"], i * TG + t - 1)
                for c in range(KC):
                    op = pe.transpose(mx[t % 2][:, c * P:(c + 1) * P], B["xn"][:, t, c * P:(c + 1) * P], K["ident"][:])
                op.then_inc(S["full"], 1)

            def project(i, t):
                b = t % 2
                pe.wait_ge(ctx_in[t % TG], (i + t // TG) * 16 + 16)
                pe.wait_ge(S["emptied"], i * TG + t + 1)
                if t >= 2:
                    pe.wait_ge(S["k_taken"], i * TG + t - 1)
                for kc in range(KC):
                    op = pe.matmul(pq[b][:, 0:C], slot(xnT, t)[:, kc], W["wq"][:, kc, :], start=(kc == 0), stop=(kc == KC - 1))
                op.then_inc(S["q_full"], 1)
                for kc in range(KC):
                    op = pe.matmul(pk[b][:], slot(cT, t)[:, kc], W["wkv"][:, kc, :], start=(kc == 0), stop=(kc == KC - 1))
                op.then_inc(S["k_full"], 1)

            def output(i, t):
                b = t % 2
                pe.wait_ge(S["y_ready"], i * TG + t + 1)
                if t >= 1:
                    pe.wait_ge(S["yT"], i * TG + t)
                for c in range(KC):
                    op = pe.transpose(py[:, c * P:(c + 1) * P], y[:, b, c * P:(c + 1) * P], K["ident"][:])
                op.then_inc(S["turned"], 1)
                pe.wait_ge(S["yT"], i * TG + t + 1)
                if t >= 1:
                    pe.wait_ge(S["added"], i * TG + t)
                for kc in range(KC):
                    op = pe.matmul(po[:, 0:C], yT[:, b, kc, :], W["wo"][:, kc, :], start=(kc == 0), stop=(kc == KC - 1))
                op.then_inc(S["out"], 1)

            def body(i, last):
                for s in range(TG):
                    if s + 3 < TG or not last:
                        project(i, s + 3)
                    if not last:
                        turn(i + 1, s, True)
                    if s + 1 < TG or not last:
                        output(i, s + 1)

            for t in range(TG):
                turn(0, t, t >= 2)
            for t in range(3):
                project(0, t)
            output(0, 0)
            bodies(pe, body)



def plan_buffers(sb, pb, NE):
    return dict(pre=sb("pre", [P, NT, NE]), cnt=sb("cnt", [P, NE]), more=sb("more", [P, NE, NT]), nb=sb("nb", [P, NE]),
                e0=sb("e0", [P, NE]), e1=sb("e1", [P, NE]), base=sb("base", [P, NE]), k1=sb("k1", [P, NT, NE]),
                k2=sb("k2", [P, NT, NE]), key=sb("key", [P, NT, NE]), p8=sb("p8", [P, NT, 8]), eq=sb("eq", [P, NT, NE]),
                eq2=sb("eq2", [P, NT, NE]),
                past=sb("past", [1, 64, NE]), owner=sb("owner", [1, 64]),
                before=pb("before", [P, NT * NE]), per_tile=pb("per_tile", [P, NT * NE]))


def plan_vector(dve, S, L, K, M, NE):
    n = [0]

    def link(op):
        n[0] += 1
        op.then_inc(S["plan"], 1)
        dve.wait_ge(S["plan"], n[0])

    def over_tiles(ap):
        return ap.unsqueeze(1).to_broadcast([P, NT, NE])

    per_tile = L["per_tile"][:].rearrange("p (t e) -> p t e", e=NE)
    dve.wait_ge(S["counted"], 1)
    link(dve.memset(L["pre"][:, 0, :], 0.0))
    for t in range(1, NT):
        link(dve.tensor_tensor(L["pre"][:, t, :], L["pre"][:, t - 1, :], per_tile[:, t - 1, :], ALU.add))
    link(dve.tensor_tensor(L["cnt"][:], L["pre"][:, NT - 1, :], per_tile[:, NT - 1, :], ALU.add))
    link(dve.tensor_tensor(L["more"][:], L["cnt"][:].unsqueeze(2).to_broadcast([P, NE, NT]),
                           K["steps"][:, 0:NT].unsqueeze(1).to_broadcast([P, NE, NT]), ALU.is_gt))
    link(dve.tensor_reduce(L["nb"][:], L["more"][:], AX.X, ALU.add))
    src, dst = L["nb"], L["e0"]
    d = 1
    while d < NE:
        dve.tensor_copy(dst[:, 0:d], src[:, 0:d])
        link(dve.tensor_tensor(dst[:, d:], src[:, d:], src[:, 0:NE - d], ALU.add))
        src, dst = dst, (L["e1"] if dst is L["e0"] else L["e0"])
        d *= 2
    end = src
    link(dve.tensor_tensor(L["base"][:], end[:], L["nb"][:], ALU.subtract))
    link(dve.tensor_scalar(dst[:], L["base"][:], float(BR), None, ALU.mult))
    base = dst
    link(dve.tensor_tensor(L["k1"][:], L["pre"][:], L["before"][:].rearrange("p (t e) -> p t e", e=NE), ALU.add))
    link(dve.tensor_tensor(L["k2"][:], L["k1"][:], over_tiles(base[:]), ALU.add))
    link(dve.scalar_tensor_tensor(out=L["k1"][:], in0=L["k2"][:], scalar=1.0, in1=M["sel"][:], op0=ALU.add, op1=ALU.mult))
    link(dve.tensor_scalar(L["key"][:], L["k1"][:], -1.0, None, ALU.add))
    for t in range(NT):
        op = dve.max(L["p8"][:, t, :], L["key"][:, t, :])
    link(op)
    dve.tensor_copy(M["place"][:], L["p8"][:]).then_inc(S["placed"], 1)
    nb = M["NB"]
    link(dve.tensor_tensor(L["past"][:, 0:nb, :], K["blocks"][0:1, 0:nb].unsqueeze(2).to_broadcast([1, nb, NE]),
                           end[0:1, :].unsqueeze(1).to_broadcast([1, nb, NE]), ALU.is_ge))
    link(dve.tensor_reduce(L["owner"][:, 0:nb], L["past"][:, 0:nb, :], AX.X, ALU.add))
    link(dve.tensor_scalar(M["owner"][:], L["owner"][:, 0:nb], float(NE - 1), None, ALU.min))
    for c in range(M["TOP"]):
        link(dve.tensor_tensor(L["eq"][:], L["key"][:], L["p8"][:, :, c:c + 1].to_broadcast([P, NT, NE]), ALU.is_equal))
        link(dve.tensor_tensor(L["eq2"][:], L["eq"][:], M["rw"][:], ALU.mult))
        link(dve.tensor_reduce(M["pw"][:, :, c:c + 1], L["eq2"][:], AX.X, ALU.add))



def split_load(sp, M):
    s = M["s"]
    sp.wait_ge(s["zeroed"], 1)
    sp.dma_start(M["sent"].rearrange("(b p) c -> p b c", p=P),
                 M["zero"][:].unsqueeze(1).to_broadcast([P, M["NB"] * BR // P, C])).then_inc(s["cleared"], 16)
    sp.dma_start(M["b1"][:], M["b1_dram"].rearrange("e p j -> p e j")).then_inc(s["b1"], 16)


def pieces_load(sp, M, i, first, n):
    for q in range(n):
        at = i * n + (first + q)
        sp.wait_ge(M["s"]["w_lo"], at + 1)
        sp.dma_start(M["stage"][:, q % 2, :], M["pieces"][bass.ds(at, 1)].rearrange("a p n -> p (a n)")).then_inc(M["w_in"][q % 2], 16)


def pieces_split(pool, M, i, share, some):
    first, n = share
    s = M["s"]

    def held(k):
        pool.tensor_tensor(M["junk"][:, k:k + 1], M["zero"][:, 0:1], M["zero"][:, 1:2], ALU.add)

    for q in some:
        at = bass.ds(i * n + (first + q), 1)
        stage = M["stage"][:, q % 2, :]
        wh = M["wh"][:, at, :].rearrange("p a n -> p (a n)")
        wl = M["wl"][:, at, :].rearrange("p a n -> p (a n)")
        pool.wait_ge(M["w_in"][q % 2], i * (n // 2 * 16) + ((first + q) // 2 + 1) * 16)
        held(q % 2 * 2)
        pool.tensor_copy(wh, stage).then_inc(s["w_hi"], 1)
        pool.wait_ge(s["w_hi"], i * n + (first + q + 1))
        held(q % 2 * 2 + 1)
        pool.tensor_tensor(wl, stage, wh, ALU.subtract).then_inc(s["w_lo"], 1)


def route(nc, K, xs, R, pre, NE, TOP, NR, M):
    NS = 8 - TOP
    l0 = NE == NR
    with ExitStack() as ctx:
        def sb(n, s, d=F32):
            return ctx.enter_context(nc.sbuf_tensor(f"{pre}_{n}", s, d))

        def pb(n, s, d=F32):
            return ctx.enter_context(nc.psum_tensor(f"{pre}_{n}", s, d))

        def over_experts(ap):
            return ap.unsqueeze(2).to_broadcast([P, NT, NE])

        B = norm_buffers(sb, "n")
        rows = M["xn"] if l0 else sb("rows", [P, NT, C])
        xnT = sb("xnT", [P, KC, GT])
        nm = sb("nm", [P, TG])
        sh = sb("sh", [P, NT, NE])
        ex = sb("ex", [P, NT, NE])
        z = sb("z", [P, NT])
        rz = sb("rz", [P, NT])
        pr = sb("pr", [P, NT, NE])
        cand = sb("cand", [P, NT, NE + NS])
        top8 = sb("top8", [P, NT, 8])
        pick = sb("pick", [P, NT, 8])
        mark = sb("mark", [P, NT, NE + NS])
        wt = sb("wt", [P, NT, NE])
        zs = sb("zs", [P, NT])
        ze = sb("ze", [P, NT])
        mx = [pb(f"mx{b}", [P, 512]) for b in range(2)]
        lg = pb("lg", [P, TG, NE])
        if l0:
            plan = plan_buffers(sb, pb, NE)
            cwT = sb("cwT", [NE, TG, P])
            pt = pb("pt", [NE, TG, P])
            pbias = [pb(f"pbias{b}", [P, 512]) for b in range(2)]
        S = named_semaphores(ctx, nc, pre, NORM_SEMS + " consts full emptied logits maxed shifted exped chain weighed cw_turned"
                  " cwT bias added counted plan placed scattered")
        block = ctx.enter_context(nc.Block())

        def bodies(eng, body):
            with eng.Fori(0, NG - 1) as i:
                body(i, False)
            body(NG - 1, True)

        @block.gpsimd
        def _(pool):
            pool.wait_ge(K["s"]["x"], 16 * NG)
            pool.wait_ge(K["s"]["weights"], 16 * K["n_weights"])
            pool.wait_ge(K["s"]["consts"], K["n_consts"])
            with pool.Fori(0, NG) as i:
                norm_pool(pool, S, B, K, i)
            if l0:
                pool.wait_ge(S["placed"], 1)
                pool.wait_ge(S["emptied"], NT)
                for t in range(NT):
                    for c in range(TOP):
                        pool.indirect_dma_start(
                            out=M["sent"], out_offset=bass.IndirectOffsetOnAxis(ap=M["place"][:, t, c:c + 1], axis=0),
                            in_=M["xn"][:, t, :], in_offset=None, bounds_check=M["NB"] * BR - 1,
                            oob_is_err=False).then_inc(S["scattered"], 16)
                pool.wait_ge(S["scattered"], 16 * NT * TOP)

        @block.vector
        def _(dve):
            dve.wait_ge(K["s"]["x"], 16 * NG)
            dve.wait_ge(K["s"]["weights"], 16 * K["n_weights"])
            dve.wait_ge(K["s"]["consts"], K["n_consts"])
            dve.memset(cand[:, :, NE:], FAR)
            dve.memset(pick[:, :, TOP:], FAR).then_inc(S["consts"], 1)
            dve.wait_ge(S["consts"], 1)
            dve.sem_inc(S["shifted"], 1)
            norm_vector(dve, S, B, xs, 0)

            def body(i, last):
                if not last:
                    norm_stats(dve, S, B, xs, i + 1)
                if l0:
                    dve.wait_ge(S["emptied"], i * TG + TG)
                    dve.memset(B["junk"][:, 1:2], 0.0)
                else:
                    for t in range(TG):
                        dve.wait_ge(S["emptied"], i * TG + t + 1)
                        at = bass.ds(i * GT + t * P, P)
                        dve.tensor_tensor(M["xl"][:, :, at], xnT[:, :, t * P:(t + 1) * P], M["xh"][:, :, at],
                                          ALU.subtract).then_inc(S["weighed"], 1)
                if not last:
                    norm_apply(dve, S, B, xs, i + 1)
                dve.wait_ge(S["logits"], i + 1)
                dve.tensor_reduce(nm[:], lg[:], AX.X, ALU.max, negate=True).then_inc(S["maxed"], 1)
                dve.wait_ge(S["maxed"], i + 1)
                dve.tensor_tensor(sh[:, bass.ds(i * TG, TG), :], lg[:], nm[:].unsqueeze(2).to_broadcast([P, TG, NE]),
                                  ALU.add).then_inc(S["shifted"], 1)

            bodies(dve, body)
            step = [0]

            def link(op):
                step[0] += 1
                op.then_inc(S["chain"], 1)
                dve.wait_ge(S["chain"], step[0])

            dve.wait_ge(S["exped"], 1)
            link(dve.tensor_reduce(z[:], ex[:], AX.X, ALU.add))
            link(dve.reciprocal(rz[:], z[:]))
            link(dve.tensor_tensor(pr[:], ex[:], over_experts(rz[:]), ALU.mult))
            if l0:
                link(dve.tensor_copy(cand[:, :, 0:NE], pr[:]))
            else:
                link(dve.tensor_tensor(cand[:, :, 0:NE], pr[:], R["corr"][:].unsqueeze(1).to_broadcast([P, NT, NE]), ALU.add))
            for t in range(NT):
                op = dve.max(top8[:, t, :], cand[:, t, 0:NE])
            link(op)
            link(dve.tensor_copy(pick[:, :, 0:TOP], top8[:, :, 0:TOP]))
            for t in range(NT):
                op = dve.match_replace(mark[:, t, :], pick[:, t, :], cand[:, t, :], -FAR)
            link(op)
            link(dve.scalar_tensor_tensor(out=wt[:], in0=mark[:, :, 0:NE], scalar=-FAR, in1=pr[:],
                                          op0=ALU.is_equal, op1=ALU.mult))
            if l0:
                link(dve.tensor_reduce(zs[:], wt[:], AX.X, ALU.add))
                link(dve.tensor_scalar(ze[:], zs[:], 1e-8, None, ALU.add))
                link(dve.reciprocal(zs[:], ze[:]))
                dve.tensor_tensor(M["rw"][:], wt[:], over_experts(zs[:]), ALU.mult)
                dve.tensor_scalar(M["sel"][:], mark[:, :, 0:NE], -FAR, None, ALU.is_equal).then_inc(S["weighed"], 1)
                plan_vector(dve, S, plan, K, M, NE)
                for t in range(NT):
                    dve.wait_ge(S["bias"], t + 1)
                    dve.tensor_tensor(xs[:, t, :], xs[:, t, :], pbias[t % 2][:, 0:C], ALU.add).then_inc(S["added"], 1)
            else:
                link(dve.tensor_scalar(M["rw"][:], wt[:], R["scale"], None, ALU.mult))
                link(dve.tensor_reduce(zs[:], M["rw"][:, :, NR:NE], AX.X, ALU.add))
                dve.wait_ge(S["emptied"], NT)
                for t in range(NT):
                    dve.scalar_tensor_tensor(out=xs[:, t, :], in0=rows[:, t, :], scalar=zs[:, t:t + 1], in1=xs[:, t, :],
                                             op0=ALU.mult, op1=ALU.add).then_inc(S["added"], 1)

        @block.scalar
        def _(act):
            if not l0:
                act.sem_inc(S["weighed"], TG)
            with act.Fori(0, NG) as i:
                for t in range(TG):
                    act.wait_ge(S["full"], i * TG + t + 1)
                    if not l0:
                        act.wait_ge(S["weighed"], i * TG + t + 1)
                    src = mx[t % 2][:, 0:C].rearrange("p (a b) -> p a b", a=KC)
                    act.activation(xnT[:, :, t * P:(t + 1) * P], src, ACT.Copy)
                    if not l0:
                        act.activation(M["xh"][:, :, bass.ds(i * GT + t * P, P)], src, ACT.Copy)
                    act.activation(tile_of(rows, i, t), B["xn"][:, t, :], ACT.Copy).then_inc(S["emptied"], 1)
            act.wait_ge(S["shifted"], NG + 1)
            act.activation(ex[:], sh[:], ACT.Exp).then_inc(S["exped"], 1)
            if l0:
                for g in range(NG):
                    act.wait_ge(S["cw_turned"], g + 1)
                    if g:
                        act.wait_ge(S["bias"], g * TG)
                    act.activation(cwT[:], pt[:], ACT.Copy).then_inc(S["cwT"], 1)

        @block.tensor
        def _(pe):
            pe.wait_ge(K["s"]["x"], 16 * NG)
            pe.wait_ge(K["s"]["weights"], 16 * K["n_weights"])
            pe.wait_ge(K["s"]["consts"], K["n_consts"])
            with pe.Fori(0, NG) as i:
                for t in range(TG):
                    pe.wait_ge(S["normed"], i * TG + t + 1)
                    if t >= 2:
                        pe.wait_ge(S["emptied"], i * TG + t - 1)
                    for c in range(KC):
                        op = pe.transpose(mx[t % 2][:, c * P:(c + 1) * P], B["xn"][:, t, c * P:(c + 1) * P], K["ident"][:])
                    op.then_inc(S["full"], 1)
                pe.wait_ge(S["shifted"], i + 1)
                for t in range(TG):
                    pe.wait_ge(S["emptied"], i * TG + t + 1)
                    for kc in range(KC):
                        op = pe.matmul(lg[:, t, :], xnT[:, kc, t * P:(t + 1) * P], R["w"][:, kc, :],
                                       start=(kc == 0), stop=(kc == KC - 1))
                op.then_inc(S["logits"], 1)
            if l0:
                pe.wait_ge(S["weighed"], 1)
                sel = M["sel"][:].rearrange("p t e -> p (t e)")
                pe.matmul(plan["before"][:], K["earlier"][:], sel, start=True, stop=True)
                pe.matmul(plan["per_tile"][:], K["all1"][:], sel, start=True, stop=True).then_inc(S["counted"], 1)
                for g in range(NG):
                    if g:
                        pe.wait_ge(S["cwT"], g)
                    for t in range(TG):
                        op = pe.transpose(pt[:, t, :], M["rw"][:, g * TG + t, :], K["ident"][:])
                    op.then_inc(S["cw_turned"], 1)
                    pe.wait_ge(S["cwT"], g + 1)
                    for t in range(g * TG, g * TG + TG):
                        if t >= 2:
                            pe.wait_ge(S["added"], t - 1)
                        pe.matmul(pbias[t % 2][:, 0:C], cwT[:, t % TG, :], R["b2"][:], start=True, stop=True).then_inc(S["bias"], 1)



def gelu_blocks(nc, K, M, NE, H):
    NB = M["NB"]
    HC, UC = H // P, 2
    BB = 4
    UB = HC // UC
    NU = BB * UB
    LEAD = 2
    with ExitStack() as ctx:
        def sb(n, s, d=F32):
            return ctx.enter_context(nc.sbuf_tensor("gb_" + n, s, d))

        def pb(n, s, d=F32):
            return ctx.enter_context(nc.psum_tensor("gb_" + n, s, d))

        TT = BR // P
        xr = sb("xr", [P, BB, TT, C])
        xh = sb("xh", [P, 4, KC, BR], BF16)
        xl = sb("xl", [P, 4, KC, BR], BF16)
        hb = sb("hb", [P, 2, UC, BR])
        hf = sb("hf", [P, 2, UC, BR])
        hh = sb("hh", [P, 4, UC, BR], BF16)
        hl = sb("hl", [P, 4, UC, BR], BF16)
        yr = sb("yr", [P, BB, TT, C])
        W = {w: M[w][:].rearrange("p (h q) n -> p h (q n)", q=4) for w in ("wh", "wl")}
        px = [pb(f"px{b}", [P, 512]) for b in range(2)]
        ph = [pb(f"ph{b}", [P, UC, BR]) for b in range(4)]
        py = [pb(f"py{b}", [P, 512]) for b in range(2)]
        S = named_semaphores(ctx, nc, "gb", "rows0 rows1 rows2 rows3 turned xhi xlo hid biased hi lo used y_out"
                             " stored0 stored1 stored2 stored3")
        rows = [S[f"rows{b}"] for b in range(BB)]
        stored = [S[f"stored{b}"] for b in range(BB)]
        block = ctx.enter_context(nc.Block())

        LAST = NB // BB - 1

        def bodies(eng, body):
            with eng.Fori(0, LAST) as i:
                body(i, False)
            body(LAST, True)

        def owner(eng, b):
            return eng.value_load(M["owner"][0:1, bass.ds(b, 1)], min_val=0, max_val=NE - 1)

        def tiles(rows_of_block):
            return rows_of_block.rearrange("(a p) c -> p a c", p=P)

        def store(sp, i, m):
            sp.wait_ge(S["y_out"], i * BB + m + 1 + 2)
            sp.dma_start(tiles(M["back"][bass.ds((i * BB + m) * BR, BR), :]), yr[:, m]).then_inc(stored[m], 16)

        @block.sync
        def _(sp):
            for m in range(BB):
                sp.dma_start(xr[:, m], tiles(M["sent"][m * BR:(m + 1) * BR, :])).then_inc(rows[m], 16)
            with sp.Fori(1, NB // BB) as i:
                for m in range(BB):
                    sp.wait_ge(S["turned"], (i - 1) * BB + m + 1)
                    sp.dma_start(xr[:, m], tiles(M["sent"][bass.ds((i * BB + m) * BR, BR), :])).then_inc(rows[m], 16)
                    store(sp, i - 1, m)
            for m in range(BB):
                store(sp, LAST, m)
            for m in range(BB):
                sp.wait_ge(stored[m], 16 * (NB // BB + 1))

        @block.gpsimd
        def _(pool):
            pool.sem_inc(S["biased"], 4)
            pool.sem_inc(S["lo"], 2)
            pool.sem_inc(S["used"], 4)
            pool.sem_inc(S["y_out"], 2)
            for m in range(BB):
                pool.sem_inc(stored[m], 16)

        @block.vector
        def _(dve):
            def low_x(i, m):
                dve.wait_ge(S["xhi"], i * BB + m + 1)
                dve.tensor_tensor(xl[:, m % 4], px[m % 2][:].rearrange("p (a b) -> p a b", a=KC), xh[:, m % 4],
                                  ALU.subtract).then_inc(S["xlo"], 1)

            def add_bias(i, u, e):
                dve.wait_ge(S["hid"], i * NU + u + 1)
                j = u % UB * UC
                b1 = M["b1"][:, bass.ds(e, 1), j:j + UC].rearrange("p a j -> p (a j)").unsqueeze(2).to_broadcast([P, UC, BR])
                dve.tensor_tensor(hb[:, u % 2], ph[u % 4][:], b1, ALU.add).then_inc(S["biased"], 1)

            def low_h(i, u):
                dve.wait_ge(S["hi"], i * NU + u + 1)
                dve.tensor_tensor(hl[:, u % 4], hf[:, u % 2], hh[:, u % 4], ALU.subtract).then_inc(S["lo"], 1)

            def body(i, last):
                es = {}
                for u in range(NU):
                    m = (u + 1) // UB
                    if m not in es and (m < BB or not last):
                        es[m] = owner(dve, i * BB + m)
                    if u + 1 < NU or not last:
                        add_bias(i, u + 1, es[m])
                    low_h(i, u)
                    if u % UB == 0 and (u // UB + 2 < BB or not last):
                        low_x(i, u // UB + 2)

            low_x(0, 0)
            low_x(0, 1)
            add_bias(0, 0, owner(dve, 0))
            bodies(dve, body)

        @block.scalar
        def _(act):
            def high_x(i, m):
                act.wait_ge(S["turned"], i * BB + m + 1)
                act.activation(xh[:, m % 4], px[m % 2][:].rearrange("p (a b) -> p a b", a=KC),
                               ACT.Copy).then_inc(S["xhi"], 1)

            def gelu(i, u):
                act.wait_ge(S["biased"], i * NU + u + 1 + 4)
                act.wait_ge(S["lo"], i * NU + u + 1)
                act.activation(hf[:, u % 2], hb[:, u % 2], ACT.Gelu_apprx_tanh)
                act.wait_ge(S["used"], i * NU + u + 1)
                act.activation(hh[:, u % 4], hb[:, u % 2], ACT.Gelu_apprx_tanh).then_inc(S["hi"], 1)

            def out_rows(i, m):
                act.wait_ge(stored[m], i * 16 + 16)
                act.wait_ge(S["used"], i * NU + (m + 1) * UB + 4)
                act.activation(yr[:, m].rearrange("p a c -> p (a c)"), py[m % 2][:], ACT.Copy).then_inc(S["y_out"], 1)

            def body(i, last):
                for m in range(BB):
                    if m + 1 < BB or not last:
                        for k in range(UB):
                            gelu(i, (m + 1) * UB + k)
                            if k == 0 and (m + 3 < BB or not last):
                                high_x(i, m + 3)
                    out_rows(i, m)

            high_x(0, 0)
            high_x(0, 1)
            for k in range(UB):
                gelu(0, k)
                if k == 0:
                    high_x(0, 2)
            bodies(act, body)

        @block.tensor
        def _(pe):
            def turn(i, m):
                pe.wait_ge(rows[m % BB], (i + m // BB) * 16 + 16)
                if m >= 2:
                    pe.wait_ge(S["xlo"], i * BB + m - 1)
                for c in range(KC):
                    for a in range(TT):
                        op = pe.transpose(px[m % 2][:, c * BR + a * P:c * BR + (a + 1) * P],
                                          xr[:, m % BB, a, c * P:(c + 1) * P], K["ident"][:])
                op.then_inc(S["turned"], 1)

            def first(i, u, e):
                m = u // UB
                pe.wait_ge(S["xlo"], i * BB + m + 1)
                pe.wait_ge(S["biased"], i * NU + u + 1)
                for j in range(UC):
                    n = 0
                    for kc in range(KC):
                        at = kc * H + (u % UB * UC + j) * P
                        for w, x in (("wh", xh), ("wh", xl), ("wl", xh)):
                            op = pe.matmul(ph[u % 4][:, j, :], W[w][:, bass.ds(e * 2, 1), at:at + P].rearrange("p a n -> p (a n)"),
                                           x[:, m % 4, kc, :], start=(n == 0), stop=(n == 3 * KC - 1))
                            n += 1
                op.then_inc(S["hid"], 1)

            def second(i, u, e):
                m = u // UB
                if u % UB == 0:
                    pe.wait_ge(S["y_out"], i * BB + m + 1)
                pe.wait_ge(S["lo"], i * NU + u + 1 + 2)
                for j in range(UC):
                    at = (u % UB * UC + j) * C
                    for n, (h, w) in enumerate(((hh, "wh"), (hl, "wh"), (hh, "wl"))):
                        for a in range(TT):
                            op = pe.matmul(py[m % 2][:, a * C:(a + 1) * C], h[:, u % 4, j, a * P:(a + 1) * P],
                                           W[w][:, bass.ds(e * 2 + 1, 1), at:at + C].rearrange("p a n -> p (a n)"),
                                           start=(u % UB == 0 and j == 0 and n == 0 and a == 0),
                                           stop=(u % UB == UB - 1 and j == UC - 1 and n == 2), skip_group_check=True)
                op.then_inc(S["used"], 1)

            def body(i, last):
                es = [owner(pe, i * BB + m) for m in range(2)]
                for u in range(NU):
                    if u % UB == 0 and (u // UB + 2 < BB or not last):
                        turn(i, u // UB + 2)
                    if u + LEAD < NU or not last:
                        first(i, u + LEAD, es[(u + LEAD) // UB])
                    m = (u + 1 + LEAD) // UB
                    if m == len(es) and (m < BB or not last):
                        es.append(owner(pe, i * BB + m))
                    second(i, u, es[u // UB])

            e0 = owner(pe, 0)
            turn(0, 0)
            turn(0, 1)
            for u in range(LEAD):
                first(0, u, e0)
            bodies(pe, body)


def combine(nc, K, xs, M, loads, loaded):
    TOP = M["TOP"]
    with ExitStack() as ctx:
        got = ctx.enter_context(nc.sbuf_tensor("cb_got", [P, NT, TOP, C], F32))
        S = named_semaphores(ctx, nc, "cb", "got0 got1 got2 got3 sum")
        arrived = [S[f"got{g}"] for g in range(NG)]
        block = ctx.enter_context(nc.Block())

        @block.sync
        def _(sp):
            for dst, src in loads:
                sp.dma_start(dst[:], src).then_inc(loaded, 16)

        @block.gpsimd
        def _(pool):
            for t in range(NT):
                for c in range(TOP):
                    pool.indirect_dma_start(out=got[:, t, c, :], out_offset=None, in_=M["back"],
                                            in_offset=bass.IndirectOffsetOnAxis(ap=M["place"][:, t, c:c + 1], axis=0),
                                            bounds_check=M["NB"] * BR - 1, oob_is_err=False).then_inc(arrived[t // TG], 16)

        @block.vector
        def _(dve):
            for g in range(NG):
                dve.wait_ge(arrived[g], 16 * TG * TOP)
                for c in range(TOP):
                    if c:
                        dve.wait_ge(S["sum"], (g * TOP + c) * TG)
                    for t in range(g * TG, g * TG + TG):
                        dve.scalar_tensor_tensor(out=xs[:, t, :], in0=got[:, t, c, :], scalar=M["pw"][:, t, c:c + 1], in1=xs[:, t, :],
                                                 op0=ALU.mult, op1=ALU.add).then_inc(S["sum"], 1)



def silu_experts(nc, K, xs, M, w_dram, NR, I):
    EB = 4
    NU = EB * NG
    WG, WD = KC * 2 * I, C
    NHB, NL = 4, 2
    with ExitStack() as ctx:
        def sb(n, s, d=F32):
            return ctx.enter_context(nc.sbuf_tensor("se_" + n, s, d))

        def pb(n, s, d=F32):
            return ctx.enter_context(nc.psum_tensor("se_" + n, s, d))

        stage = sb("stage", [P, EB, WG + WD])
        wh = sb("wh", [P, EB, WG + WD], BF16)
        wl = sb("wl", [P, EB, WG + WD], BF16)
        ew = sb("ew", [P, EB, NT])
        sg = sb("sg", [P, 2, GT])
        hf = sb("hf", [P, NHB, GT])
        hh = sb("hh", [P, NHB, GT], BF16)
        hl = sb("hl", [P, NHB, GT], BF16)
        pg = [pb(f"pg{b}", [P, GT]) for b in range(2)]
        pu = [pb(f"pu{b}", [P, GT]) for b in range(2)]
        py = [[pb(f"py{s}{b}", [P, 2, C]) for b in range(2)] for s in range(2)]
        S = named_semaphores(ctx, nc, "se", "w_in0 w_in1 w_in2 w_in3 w_hi w_lo picked gu silu prod hi lo used y_taken")
        w_in = [S["w_in0"], S["w_in1"], S["w_in2"], S["w_in3"]]
        SPLIT_AT = 0
        block = ctx.enter_context(nc.Block())

        def wgu(buf, p, kc, half):
            return buf[:, p, kc * 2 * I + half * I:kc * 2 * I + (half + 1) * I]

        @block.sync
        def _(sp):
            for p in range(EB):
                sp.dma_start(stage[:, p, :], w_dram[p]).then_inc(w_in[p], 16)
            with sp.Fori(1, NR // EB) as i:
                for p in range(EB):
                    sp.wait_ge(S["w_hi"], (i - 1) * EB + p + 1)
                    sp.wait_ge(S["w_lo"], (i - 1) * EB + p + 1)
                    sp.dma_start(stage[:, p, :], w_dram[bass.ds(i * EB + p, 1)].rearrange("a p n -> p (a n)")).then_inc(w_in[p], 16)

        NBODY = NR // EB

        def bodies(eng, body):
            with eng.Fori(0, NBODY - 1) as i:
                body(i, False)
            body(NBODY - 1, True)

        @block.scalar
        def _(act):
            def split(i, p):
                act.wait_ge(w_in[p % EB], (i + p // EB) * 16 + 16)
                act.activation(wh[:, p % EB, :], stage[:, p % EB, :], ACT.Copy).then_inc(S["w_hi"], 1)

            def silu(i, u):
                act.wait_ge(S["gu"], i * NU + u + 1)
                act.wait_ge(S["prod"], i * NU + u + 1)
                act.activation(sg[:, u % 2, :], pg[u % 2][:], ACT.Silu).then_inc(S["silu"], 1)

            def high_h(i, u):
                act.wait_ge(S["prod"], i * NU + u + 1 + 2)
                act.wait_ge(S["used"], i * NU + u + 1)
                act.activation(hh[:, u % NHB, :], hf[:, u % NHB, :], ACT.Copy).then_inc(S["hi"], 1)

            def body(i, last):
                for u in range(NU):
                    if u + 1 < NU or not last:
                        silu(i, u + 1)
                    high_h(i, u)
                    p = u // NG + 1
                    if u % NG == SPLIT_AT and (p < EB or not last):
                        split(i, p)

            act.wait_ge(w_in[0], 16)
            act.activation(wh[:, 0, :], stage[:, 0, :], ACT.Copy).then_inc(S["w_hi"], 1)
            silu(0, 0)
            bodies(act, body)

        @block.vector
        def _(dve):
            dve.sem_inc(S["y_taken"], 2)
            dve.sem_inc(S["prod"], 2)
            dve.sem_inc(S["used"], NHB)

            def split(i, p):
                dve.wait_ge(S["w_hi"], i * EB + p + 1)
                dve.tensor_tensor(wl[:, p % EB, :], stage[:, p % EB, :], wh[:, p % EB, :], ALU.subtract).then_inc(S["w_lo"], 1)
                dve.tensor_copy(ew[:, p % EB, :], M["rw"][:, :, bass.ds(i * EB + p, 1)].rearrange("p t a -> p (t a)")).then_inc(S["picked"], 1)

            def product(i, u):
                dve.wait_ge(S["silu"], i * NU + u + 1)
                dve.tensor_tensor(hf[:, u % NHB, :], sg[:, u % 2, :], pu[u % 2][:], ALU.mult).then_inc(S["prod"], 1)

            def low_h(i, u):
                dve.wait_ge(S["hi"], i * NU + u + 1)
                dve.tensor_tensor(hl[:, u % NHB, :], hf[:, u % NHB, :], hh[:, u % NHB, :], ALU.subtract).then_inc(S["lo"], 1)

            def taken(i, u):
                p, g = u // NG, u % NG
                dve.wait_ge(S["used"], i * NU + u + 1 + NHB)
                dve.wait_ge(S["picked"], i * EB + p + 1)
                for t in range(TG):
                    T = g * TG + t
                    op = dve.scalar_tensor_tensor(out=xs[:, T, :], in0=py[u % 2][t // 2][:, t % 2, :], scalar=ew[:, p % EB, T:T + 1],
                                                  in1=xs[:, T, :], op0=ALU.mult, op1=ALU.add)
                op.then_inc(S["y_taken"], 1)

            def body(i, last):
                for u in range(NU):
                    if u + 1 < NU or not last:
                        product(i, u + 1)
                    low_h(i, u)
                    p = u // NG + 1
                    if u % NG == SPLIT_AT and (p < EB or not last):
                        split(i, p)
                    if u >= 1:
                        taken(i, u - 1)
                taken(i, NU - 1)

            split(0, 0)
            product(0, 0)
            bodies(dve, body)

        @block.tensor
        def _(pe):
            def first(i, u):
                p, g = u // NG, u % NG
                if g == 0:
                    pe.wait_ge(S["w_lo"], i * EB + p + 1)
                pe.wait_ge(S["prod"], i * NU + u + 1)
                for half, bank in ((0, pg), (1, pu)):
                    n = 0
                    for kc in range(KC):
                        for w, x in ((wh, "xh"), (wh, "xl"), (wl, "xh")):
                            op = pe.matmul(bank[u % 2][:], wgu(w, p % EB, kc, half), M[x][:, kc, g * GT:(g + 1) * GT],
                                           start=(n == 0), stop=(n == 3 * KC - 1))
                            n += 1
                op.then_inc(S["gu"], 1)

            def second(i, u):
                p = u // NG
                pe.wait_ge(S["y_taken"], i * NU + u + 1)
                pe.wait_ge(S["lo"], i * NU + u + 1)
                for t in range(TG):
                    for m, (h, w) in enumerate(((hh, wh), (hh, wl), (hl, wh))):
                        op = pe.matmul(py[u % 2][t // 2][:, t % 2, :], h[:, u % NHB, t * P:(t + 1) * P], w[:, p % EB, WG:],
                                       start=(m == 0), stop=(m == 2))
                op.then_inc(S["used"], 1)

            def body(i, last):
                for u in range(NU):
                    if u + NL < NU or not last:
                        first(i, u + NL)
                    second(i, u)

            for u in range(NL):
                first(0, u)
            bodies(pe, body)



NE0, TOP0, H0 = 8, 2, 1024
NE1, NR1, TOP1, I1 = 40, 32, 6, 128
SCALE1 = 2.5
IN_LINEAR = 4


def sparse_buffers(ctx, nc, NE, H, TOP, pieces, b1_dram):
    NB = NT * TOP * P // BR + NE
    ROWS = NB * BR

    def sb(n, s, d=F32):
        return ctx.enter_context(nc.sbuf_tensor(f"sp_{n}", s, d))

    s = named_semaphores(ctx, nc, "sp", "zeroed cleared b1 w_in0 w_in1 w_hi w_lo")
    return dict(w_in=[s["w_in0"], s["w_in1"]], NB=NB, TOP=TOP, PIECES=8 * NE, pieces=pieces, b1_dram=b1_dram, s=s, b1=sb("b1", [P, NE, H // P]),
                zero=sb("zero", [P, C]), junk=sb("junk", [P, 4]), stage=sb("stage", [P, 2, KC * H // 4]),
                wh=sb("wh", [P, 8 * NE, KC * H // 4], BF16), wl=sb("wl", [P, 8 * NE, KC * H // 4], BF16),
                owner=sb("owner", [1, NB], mybir.dt.int32),
                sent=nc.dram_tensor("sent_rows", (ROWS, C), F32, kind="Internal").ap(),
                back=nc.dram_tensor("back_rows", (ROWS, C), F32, kind="Internal").ap())


def mixture_buffers(ctx, nc, pre, NE):
    def sb(n, s, d=F32):
        return ctx.enter_context(nc.sbuf_tensor(f"{pre}_{n}", s, d))

    return dict(xh=sb("xh", [P, KC, NT * P], BF16), xl=sb("xl", [P, KC, NT * P], BF16), rw=sb("rw", [P, NT, NE]))


def decoder(nc, A, out):
    with ExitStack() as ctx:
        def sb(n, s, d=F32):
            return ctx.enter_context(nc.sbuf_tensor(n, s, d))

        xs = sb("xs", [P, NT, C])
        K = {"s": named_semaphores(ctx, nc, "g", "x weights consts zeroed stored")}
        K["ident"] = sb("ident", [P, P])
        K["identb"] = sb("identb", [P, P], BF16)
        K["causal"] = sb("causal", [P, 4, P], BF16)
        K["heads8"] = sb("heads8", [P, P])
        K["evenodd"] = sb("evenodd", [P, 2])
        K["eps4"] = sb("eps4", [P, TG])
        K["half4"] = sb("half4", [P, TG])
        K["earlier"] = sb("earlier", [P, P], BF16)
        K["all1"] = sb("all1", [P, P], BF16)
        K["steps"] = sb("steps", [P, NT])
        K["blocks"] = sb("blocks", [1, NT * TOP0 + NE0])
        M0 = dict(place=sb("place", [P, NT, 8], mybir.dt.int32), pw=sb("pw", [P, NT, TOP0]), rw=sb("rw0", [P, NT, NE0]),
                  sel=sb("sel", [P, NT, NE0], BF16))
        loads, later = [], []

        def into(ctx, loads):
            def put(name, shape, src):
                w = ctx.enter_context(nc.sbuf_tensor("w_" + name, shape, F32))
                loads.append((w, src))
                return w

            return (lambda name, cols=C: put(name, [P, KC, cols], A[name].rearrange("(k p) n -> p k n", p=P)),
                    lambda name, n: put(name, [P, n], A[name]),
                    lambda name, n=C: put(name, [P, n], A[name].partition_broadcast(P)))

        square, column, spread = into(ctx, loads)
        WX = {k: square("L0_xattn_W" + k[1]) for k in ("wq", "wk", "wv", "wo")}
        WX.update(bq=column("L0_xattn_bq", KC), bk=column("L0_xattn_bk", KC), bv=spread("L0_xattn_bv"), bo=spread("L0_xattn_bo"))
        R0 = dict(w=square("L0_ffn_router_w", NE0), b2=sb("b2_0", [NE0, C]))
        loads.append((R0["b2"], A["L0_ffn_b2"]))
        sparse = ExitStack()
        M0.update(sparse_buffers(sparse, nc, NE0, H0, TOP0, A["L0_ffn_w"], A["L0_ffn_b1"]))
        first = sparse.enter_context(ExitStack())
        square, column, spread = into(first, loads)
        WA = dict(qkv=square("L0_attn_qkv_weight", 3 * C), wp=square("L0_attn_proj_weight"), bp=spread("L0_attn_proj_bias"))
        K["n_weights"] = len(loads)
        K["n_consts"] = 11

        with nc.sbuf_tensor("steps_i", [P, NT], mybir.dt.int32) as steps, \
                nc.sbuf_tensor("blocks_i", [1, NT * TOP0 + NE0], mybir.dt.int32) as blocks, nc.Block() as block:
            @block.sync
            def _(sp):
                for g in range(NG):
                    sp.dma_start(xs[:, g * TG:(g + 1) * TG, :],
                                 A["x"][g * TG:(g + 1) * TG].rearrange("b t c -> t b c")).then_inc(K["s"]["x"], 16)
                for dst, src in loads:
                    sp.dma_start(dst[:], src).then_inc(K["s"]["weights"], 16)

            @block.gpsimd
            def _(pool):
                s = K["s"]
                pool.memset(K["eps4"][:], LN_EPS).then_inc(s["zeroed"], 1)
                pool.memset(K["half4"][:], -0.5).then_inc(s["zeroed"], 1)
                pool.memset(K["ident"][:], 0.0).then_inc(s["zeroed"], 1)
                pool.memset(K["identb"][:], 0.0).then_inc(s["zeroed"], 1)
                pool.memset(K["causal"][:], 0.0).then_inc(s["zeroed"], 1)
                pool.memset(K["heads8"][:], 1.0).then_inc(s["zeroed"], 1)
                pool.memset(K["evenodd"][:], 0.0).then_inc(s["zeroed"], 1)
                pool.memset(K["earlier"][:], 1.0).then_inc(s["zeroed"], 1)
                pool.memset(K["all1"][:], 1.0).then_inc(s["consts"], 1)
                pool.iota(steps[:], pattern=[[BR, NT]], base=0, channel_multiplier=0).then_inc(s["consts"], 1)
                pool.iota(blocks[:], pattern=[[1, NT * TOP0 + NE0]], base=0, channel_multiplier=0).then_inc(s["consts"], 1)
                pool.wait_ge(s["zeroed"], 8)
                pool.affine_select(out=K["earlier"][:], in_=K["earlier"][:], compare_op=ALU.is_ge, fill=0.0, base=-1,
                                   pattern=[[1, P]], channel_multiplier=-1).then_inc(s["consts"], 1)
                for name in ("ident", "identb"):
                    pool.affine_select(out=K[name][:], in_=K[name][:], compare_op=ALU.not_equal, fill=1.0, base=0,
                                       pattern=[[-1, P]], channel_multiplier=1).then_inc(s["consts"], 1)
                pool.affine_select(out=K["causal"][:], in_=K["causal"][:], compare_op=ALU.is_ge, fill=-1e30, base=0,
                                   pattern=[[0, 4], [-1, P]], channel_multiplier=1).then_inc(s["consts"], 1)
                h8 = K["heads8"][:].rearrange("p (b e) -> p b e", e=8)
                pool.affine_select(out=h8, in_=h8, compare_op=ALU.is_ge, fill=0.0, base=0,
                                   pattern=[[-8, 16], [0, 8]], channel_multiplier=1).then_inc(s["zeroed"], 1)
                pool.wait_ge(s["zeroed"], 9)
                pool.affine_select(out=h8, in_=h8, compare_op=ALU.is_ge, fill=0.0, base=7,
                                   pattern=[[8, 16], [0, 8]], channel_multiplier=-1).then_inc(s["consts"], 1)
            @block.vector
            def _(dve):
                s = K["s"]
                dve.wait_ge(s["consts"], 8)
                dve.tensor_copy(K["steps"][:], steps[:]).then_inc(s["consts"], 1)
                dve.tensor_copy(K["blocks"][:], blocks[:]).then_inc(s["consts"], 1)
                idr = K["ident"][:].rearrange("p (q r n) -> p r q n", q=4, r=2)
                dve.tensor_reduce(K["evenodd"][:], idr, AX.XY, ALU.add).then_inc(s["consts"], 1)

        with sparse:
            per_group = M0["PIECES"] // NG
            share = (0, IN_LINEAR), (NG * IN_LINEAR, per_group - IN_LINEAR)
            linear_attention(nc, K, xs, WA, M0, share[0])
            first.close()
            softmax_attention(nc, K, xs, WX, "xa", ctx_dram=A["ctx_T"], M=M0, share=share[1])
            with nc.sbuf_tensor("xn_rows", [P, NT, C], F32) as xn:
                M0["xn"] = xn
                route(nc, K, xs, R0, "r0", NE0, TOP0, NE0, M0)
            gelu_blocks(nc, K, M0, NE0, H0)

        square, column, spread = into(ctx, later)
        w_attn = square("L1_attn_w_attn", 3 * C)
        WS = dict(wq=w_attn[:, :, 0:C], wk=w_attn[:, :, C:2 * C], wv=w_attn[:, :, 2 * C:3 * C], wo=square("L1_attn_w_proj"))
        WS.update(bq=column("L1_attn_bq", KC), bk=column("L1_attn_bk", KC), bv=spread("L1_attn_bv"), bo=spread("L1_attn_b_proj"))
        WH = dict(wq=square("L1_xattn_Wq"), wkv=square("L1_xattn_Wkv", 2 * C), wo=square("L1_xattn_Wo"))
        WH.update({b: spread("L1_xattn_" + b) for b in ("bq", "bk", "bv", "bo")})
        R1 = dict(w=square("L1_ffn_classifier_weight", NE1), corr=spread("L1_ffn_corr", NE1), scale=SCALE1)
        K["n_weights"] += len(later)
        combine(nc, K, xs, M0, later, K["s"]["weights"])
        softmax_attention(nc, K, xs, WS, "sa", causal=True)
        head_attention(nc, K, xs, WH, A["ctx_T"])
        with ExitStack() as m:
            M = mixture_buffers(m, nc, "m1", NE1)
            route(nc, K, xs, R1, "r1", NE1, TOP1, NR1, M)
            silu_experts(nc, K, xs, M, A["L1_ffn_w"], NR1, I1)

        with nc.Block() as block:
            @block.sync
            def _(sp):
                s = K["s"]
                for g in range(NG):
                    sp.dma_start(out[g * TG:(g + 1) * TG].rearrange("b t c -> t b c"),
                                 xs[:, g * TG:(g + 1) * TG, :]).then_inc(s["stored"], 16)
                sp.wait_ge(s["stored"], 16 * NG)


def kernel(**inputs):
    import numpy as _np
    import concourse.bacc as _bacc
    from concourse import mybir as _mybir
    from concourse.bass_utils import run_bass_kernel_spmd as _run

    a = {k: _np.asarray(v) for k, v in inputs.items()}
    laid = {
        "x": a["x"],
        "ctx_T": a["ctx_1024"].reshape(NT * P, C).T.reshape(KC, P, NT * P),
        "L0_attn_qkv_weight": a["L0_attn_qkv_weight"].T,
        "L0_attn_proj_weight": a["L0_attn_proj_weight"].T,
        "L0_attn_proj_bias": a["L0_attn_proj_bias"],
        "L1_attn_w_attn": a["L1_attn_w_attn"],
        "L1_attn_w_proj": a["L1_attn_w_proj"],
        "L1_attn_bq": a["L1_attn_b_attn"][0:C].reshape(KC, P).T,
        "L1_attn_bk": a["L1_attn_b_attn"][C:2 * C].reshape(KC, P).T,
        "L1_attn_bv": a["L1_attn_b_attn"][2 * C:3 * C],
        "L1_attn_b_proj": a["L1_attn_b_proj"],
        "L0_xattn_bv": a["L0_xattn_bv"], "L0_xattn_bo": a["L0_xattn_bo"],
        "L0_xattn_bq": a["L0_xattn_bq"].reshape(KC, P).T,
        "L0_xattn_bk": a["L0_xattn_bk"].reshape(KC, P).T,
    }
    w1 = a["L0_ffn_w1"].transpose(0, 2, 1).reshape(NE0, KC, P, H0).transpose(0, 2, 1, 3).reshape(NE0, P, KC * H0)
    w2 = a["L0_ffn_w2"].transpose(0, 2, 1).reshape(NE0, H0 // P, P, C).transpose(0, 2, 1, 3).reshape(NE0, P, H0 // P * C)
    gu = a["L1_ffn_gate_up_proj"][:NR1].transpose(0, 2, 1).reshape(NR1, KC, P, 2 * I1).transpose(0, 2, 1, 3).reshape(NR1, P, KC * 2 * I1)
    laid.update({
        "L0_ffn_w": _np.concatenate([w1, w2], axis=2).reshape(NE0, P, 8, KC * H0 // 4).transpose(0, 2, 1, 3)
                       .reshape(8 * NE0, P, KC * H0 // 4),
        "L0_ffn_b1": a["L0_ffn_b1"].reshape(NE0, H0 // P, P).transpose(0, 2, 1),
        "L0_ffn_b2": a["L0_ffn_b2"],
        "L0_ffn_router_w": a["L0_ffn_router_w"].T,
        "L1_ffn_w": _np.concatenate([gu, a["L1_ffn_down_proj"].transpose(0, 2, 1)], axis=2),
        "L1_ffn_classifier_weight": a["L1_ffn_classifier_weight"].T,
        "L1_ffn_corr": a["L1_ffn_e_score_correction_bias"],
        "L1_xattn_Wq": a["L1_xattn_Wq"],
        "L1_xattn_Wkv": _np.concatenate([a["L1_xattn_Wk"], a["L1_xattn_Wv"]], axis=1),
        "L1_xattn_Wo": a["L1_xattn_Wo"],
        **{"L1_xattn_" + b: a["L1_xattn_" + b] for b in ("bq", "bk", "bv", "bo")},
    })
    for w in ("Wq", "Wk", "Wv", "Wo"):
        laid["L0_xattn_" + w] = a["L0_xattn_" + w].T
    nc = _bacc.Bacc("TRN2", target_bir_lowering=False, num_devices=1)
    arrays, A = {}, {}
    for name, v in laid.items():
        v = _np.ascontiguousarray(v)
        arrays[f"in_{name}"] = v
        A[name] = nc.dram_tensor(f"in_{name}", v.shape, _mybir.dt.from_np(v.dtype), kind="ExternalInput").ap()
    out = nc.dram_tensor("out", (NT, P, C), F32, kind="ExternalOutput").ap()
    decoder(nc, A, out)
    r = _run(nc, [arrays], core_ids=[0])
    return r.results[0]["out"]
```
